# Optimizing a Trainium2 kernel written in Bass

```python
import numpy as np
import jax
import jax.numpy as jnp

def _softmax(x, axis=-1):
    return jax.nn.softmax(x, axis=axis)

def _gelu(x):
    return jax.nn.gelu(x, approximate=True)

def _silu(x):
    return jax.nn.silu(x)

def _sigmoid(x):
    return jax.nn.sigmoid(x)

def _layernorm(x, axis=-1, eps=1e-05):
    m = jnp.mean(x, axis=axis, keepdims=True)
    v = jnp.var(x, axis=axis, keepdims=True)
    return (x - m) / jnp.sqrt(v + eps)

def _scatter_add(tgt, idx, src, axis=0):
    return tgt.at[idx].add(src)

def _segment_sum(src, seg, n):
    return jax.ops.segment_sum(src, seg, n)
kernel_name = 'mk_xattn_ffn_d4_seqx_r4_f1c8be'

def setup_inputs(seed: int=0):
    np.random.seed(seed)
    _w = jnp.asarray

    def _rec_inputs():
        import jax
        import jax.numpy as jnp
        _rk = jax.random.key(seed)
        x = -0.0003929 + 0.9999 * jax.random.normal(jax.random.fold_in(_rk, 1), (4, 512, 256), jnp.float32)
        _lenS = 512 - jax.random.randint(jax.random.fold_in(_rk, 7), (4,), 0, max(1, 512 // 4) + 1, jnp.int32)
        _lenS2 = 1024 - jax.random.randint(jax.random.fold_in(_rk, 8), (4,), 0, max(1, 1024 // 4) + 1, jnp.int32)
        _ctx_1024P = jax.random.normal(jax.random.fold_in(_rk, 11), (4, 16, 256), jnp.float32)
        _ctx_1024c = jax.random.dirichlet(jax.random.fold_in(_rk, 511), 0.3 * jnp.ones((16,), jnp.float32), (4, 1024))
        _ctx_1024t = jnp.einsum('bsk,bkd->bsd', _ctx_1024c, _ctx_1024P)
        _ctx_1024t = _ctx_1024t * jax.lax.rsqrt(jnp.mean(jnp.square(_ctx_1024t)) + 1e-12) * 0.953939
        ctx_1024 = 2.81802e-05 + 1.00001 * (_ctx_1024t + 0.3 * jax.random.normal(jax.random.fold_in(_rk, 611), (4, 1024, 256), jnp.float32))
        _validS = jnp.arange(512)[None, :] < _lenS[:, None]
        _validS2 = jnp.arange(1024)[None, :] < _lenS2[:, None]
        _causal = jnp.tril(jnp.ones((512, 512), dtype=bool))
        mask_SxS2_bk0 = jnp.logical_not(jnp.broadcast_to(_validS2[0:1, :], (512, 1024)))
        mask_BxS2_if1 = jnp.where(jnp.ones((4, 1024), dtype=bool), 1, 0).astype(jnp.int32)
        return (x, ctx_1024, mask_SxS2_bk0, mask_BxS2_if1)
    x, ctx_1024, mask_SxS2_bk0, mask_BxS2_if1 = _rec_inputs()

    def _L0_xattn_setup():
        import jax, jax.numpy as jnp
        import numpy as np
        B, S, H = (8, 512, 256)
        key = jax.random.key(seed)
        ks = jax.random.split(key, 12)
        s = 1.0 / np.sqrt(H)
        return {'_q': jax.random.normal(ks[0], (B, S, H), jnp.float32), '_kv': jax.random.normal(ks[1], (B, S, H), jnp.float32), 'W_kv': jax.random.normal(ks[2], (H, 2 * H), jnp.float32) * s, 'b_kv': jnp.zeros((2 * H,), jnp.float32), 'W_q': jax.random.normal(ks[3], (H, H), jnp.float32) * s, 'b_q': jnp.zeros((H,), jnp.float32), 'W1': jax.random.normal(ks[4], (H, 4 * H), jnp.float32) * s, 'b1': jnp.zeros((4 * H,), jnp.float32), 'W2': jax.random.normal(ks[5], (4 * H, H), jnp.float32) * (1.0 / np.sqrt(4 * H)), 'b2': jnp.zeros((H,), jnp.float32)}
    _L0_xattn_all = _L0_xattn_setup()
    _L0_xattn_in = {k: v for k, v in _L0_xattn_all.items() if k in ('W_kv', 'b_kv', 'W_q', 'b_q', 'W1', 'b1', 'W2', 'b2')}
    del _L0_xattn_all

    def _L0_ffn_setup():
        import jax, jax.numpy as jnp
        import numpy as np
        B, S, DIM = (4, 1024, 256)
        BASE_COUPLING = 0.1
        NUM_CYCLES = 3

        def _gelu(x):
            return jax.nn.gelu(x, approximate=False)

        def _coupling_net(h, w1, b1, w2, b2, w3, b3, w4, b4):
            h = _gelu(h @ w1 + b1)
            h = _gelu(h @ w2 + b2)
            h = _gelu(h @ w3 + b3)
            return jax.nn.sigmoid(h @ w4 + b4)

        def _global_net(h, w1, b1, w2, b2, w3, b3):
            h = _gelu(h @ w1 + b1)
            h = _gelu(h @ w2 + b2)
            return jax.nn.sigmoid(h @ w3 + b3)

        def _twist(x):
            o_r, o_i, p_r, p_i = jnp.split(x, 4, axis=-1)
            return jnp.concatenate([p_r, -p_i, -o_r, o_i], axis=-1)
        key = jax.random.key(seed)
        ks = jax.random.split(key, 9)
        d = DIM

        def w(k, fan_in, fan_out):
            return jax.random.normal(k, (fan_in, fan_out), dtype=jnp.float32) / np.sqrt(fan_in).astype(np.float32)
        inp = {'x': jax.random.normal(ks[0], (B, S, d), dtype=jnp.float32)}
        cn_dims = [(d, d), (d, d // 2), (d // 2, d // 4), (d // 4, 1)]
        for i, (a, b) in enumerate(cn_dims):
            inp[f'cn_w{i + 1}'] = w(ks[1 + i], a, b)
            inp[f'cn_b{i + 1}'] = jnp.zeros((b,), dtype=jnp.float32)
        gc_dims = [(d, d // 2), (d // 2, d // 4), (d // 4, 1)]
        for i, (a, b) in enumerate(gc_dims):
            inp[f'gc_w{i + 1}'] = w(ks[5 + i], a, b)
            inp[f'gc_b{i + 1}'] = jnp.zeros((b,), dtype=jnp.float32)
        inp['adaptive_range'] = jnp.full((1,), 0.2, dtype=jnp.float32)
        return inp
    _L0_ffn_all = _L0_ffn_setup()
    _L0_ffn_in = {k: v for k, v in _L0_ffn_all.items() if k in ('cn_w1', 'cn_b1', 'cn_w2', 'cn_b2', 'cn_w3', 'cn_b3', 'cn_w4', 'cn_b4', 'gc_w1', 'gc_b1', 'gc_w2', 'gc_b2', 'gc_w3', 'gc_b3', 'adaptive_range')}
    del _L0_ffn_all

    def _L1_xattn_setup():
        import jax, jax.numpy as jnp
        import numpy as np
        D_MODEL = 256
        NUM_HEADS = 16
        HEAD_DIM = D_MODEL // NUM_HEADS
        key = jax.random.key(seed)
        ks = jax.random.split(key, 11)
        B, S = (2, 512)
        scale = 1.0 / np.sqrt(D_MODEL)
        inp = {'q': jax.random.normal(ks[0], (B, S, D_MODEL), jnp.float32), 'k': jax.random.normal(ks[1], (B, S, D_MODEL), jnp.float32), 'v': jax.random.normal(ks[2], (B, S, D_MODEL), jnp.float32), 'Wq': jax.random.normal(ks[3], (D_MODEL, D_MODEL), jnp.float32) * scale, 'bq': jnp.zeros((D_MODEL,), jnp.float32), 'Wk': jax.random.normal(ks[4], (D_MODEL, D_MODEL), jnp.float32) * scale, 'bk': jnp.zeros((D_MODEL,), jnp.float32), 'Wv': jax.random.normal(ks[5], (D_MODEL, D_MODEL), jnp.float32) * scale, 'bv': jnp.zeros((D_MODEL,), jnp.float32), 'Wo': jax.random.normal(ks[6], (D_MODEL, D_MODEL), jnp.float32) * scale, 'bo': jnp.zeros((D_MODEL,), jnp.float32)}
        return inp
    _L1_xattn_all = _L1_xattn_setup()
    _L1_xattn_in = {k: v for k, v in _L1_xattn_all.items() if k in ('Wq', 'bq', 'Wk', 'bk', 'Wv', 'bv', 'Wo', 'bo')}
    del _L1_xattn_all

    def _L1_ffn_setup():
        import jax, jax.numpy as jnp
        import numpy as np
        B, N, C, F, E, K = (2, 512, 256, 1024, 8, 2)
        key = jax.random.key(seed)
        k = jax.random.split(key, 6)
        xavier1 = float(np.sqrt(6.0 / (C + F)))
        xavier2 = float(np.sqrt(6.0 / (F + C)))
        return {'x': jax.random.normal(k[0], (B, N, C), dtype=jnp.float32), 'router_w': jax.random.normal(k[1], (E, C), dtype=jnp.float32) * 0.01, 'w1': jax.random.uniform(k[2], (E, F, C), dtype=jnp.float32, minval=-xavier1, maxval=xavier1), 'b1': jnp.zeros((E, F), dtype=jnp.float32), 'w2': jax.random.uniform(k[3], (E, C, F), dtype=jnp.float32, minval=-xavier2, maxval=xavier2), 'b2': jnp.zeros((E, C), dtype=jnp.float32)}
    _L1_ffn_all = _L1_ffn_setup()
    _L1_ffn_in = {k: v for k, v in _L1_ffn_all.items() if k in ('router_w', 'w1', 'b1', 'w2', 'b2')}
    del _L1_ffn_all

    def _L2_xattn_setup():
        import jax, jax.numpy as jnp
        import numpy as np
        B, S, DIM, H = (4, 512, 256, 16)
        HD = DIM // H
        SCALE = HD ** (-0.5)

        def _heads(x):
            b, s, _ = x.shape
            return x.reshape(b, s, H, HD).transpose(0, 2, 1, 3)
        key = jax.random.key(seed)
        ks = jax.random.split(key, 7)
        init = 0.02
        return {'query': jax.random.normal(ks[0], (B, S, DIM), dtype=jnp.float32), 'key': jax.random.normal(ks[1], (B, S, DIM), dtype=jnp.float32), 'value': jax.random.normal(ks[2], (B, S, DIM), dtype=jnp.float32), 'attn_mask': jnp.tril(jnp.ones((S, S), dtype=bool)), 'Wq': jax.random.normal(ks[3], (DIM, DIM), dtype=jnp.float32) * init, 'Wk': jax.random.normal(ks[4], (DIM, DIM), dtype=jnp.float32) * init, 'Wv': jax.random.normal(ks[5], (DIM, DIM), dtype=jnp.float32) * init, 'Wo': jax.random.normal(ks[6], (DIM, DIM), dtype=jnp.float32) * init}
    _L2_xattn_all = _L2_xattn_setup()
    _L2_xattn_in = {k: v for k, v in _L2_xattn_all.items() if k in ('Wq', 'Wk', 'Wv', 'Wo')}
    del _L2_xattn_all

    def _L2_ffn_setup():
        import jax, jax.numpy as jnp
        import numpy as np
        B, S, D = (4, 1024, 256)
        DD = 4 * D
        N_EXPERTS = 8
        CAPACITY = 1.0
        LN_EPS = 1e-05
        key = jax.random.key(seed)
        ks = jax.random.split(key, 8)
        s1 = 1.0 / np.sqrt(D)
        s2 = 1.0 / np.sqrt(DD)
        return {'x': jax.random.normal(ks[0], (B, S, D), jnp.float32), 'gate_w': jax.random.normal(ks[1], (N_EXPERTS, D), jnp.float32) * 0.02, 'ln_w': jnp.ones((D,), jnp.float32), 'ln_b': jnp.zeros((D,), jnp.float32), 'fc1s': jax.random.normal(ks[2], (N_EXPERTS, DD, D), jnp.float32) * s1, 'b1s': jax.random.normal(ks[3], (N_EXPERTS, DD), jnp.float32) * s1, 'fc2s': jax.random.normal(ks[4], (N_EXPERTS, D, DD), jnp.float32) * s2, 'b2s': jax.random.normal(ks[5], (N_EXPERTS, D), jnp.float32) * s2}
    _L2_ffn_all = _L2_ffn_setup()
    _L2_ffn_in = {k: v for k, v in _L2_ffn_all.items() if k in ('gate_w', 'ln_w', 'ln_b', 'fc1s', 'b1s', 'fc2s', 'b2s')}
    del _L2_ffn_all

    def _L3_xattn_setup():
        import jax, jax.numpy as jnp
        import numpy as np
        N_HEADS, EMB_DIM, K_DIM, V_DIM = (16, 256, 64, 64)
        B, L = (4, 512)
        key = jax.random.key(seed)
        ks = jax.random.split(key, 7)
        scale = 1.0 / np.sqrt(EMB_DIM)
        return {'query': jax.random.normal(ks[0], (B, L, EMB_DIM), dtype=jnp.float32), 'key': jax.random.normal(ks[1], (B, L, EMB_DIM), dtype=jnp.float32), 'value': jax.random.normal(ks[2], (B, L, EMB_DIM), dtype=jnp.float32), 'pad_mask': jnp.ones((B, L), dtype=jnp.int32), 'Wq': jax.random.normal(ks[3], (EMB_DIM, N_HEADS * K_DIM), dtype=jnp.float32) * scale, 'Wk': jax.random.normal(ks[4], (EMB_DIM, N_HEADS * K_DIM), dtype=jnp.float32) * scale, 'Wv': jax.random.normal(ks[5], (EMB_DIM, N_HEADS * V_DIM), dtype=jnp.float32) * scale, 'Wo': jax.random.normal(ks[6], (N_HEADS * V_DIM, EMB_DIM), dtype=jnp.float32) * scale}
    _L3_xattn_all = _L3_xattn_setup()
    _L3_xattn_in = {k: v for k, v in _L3_xattn_all.items() if k in ('Wq', 'Wk', 'Wv', 'Wo')}
    del _L3_xattn_all

    def _L3_ffn_setup():
        import jax, jax.numpy as jnp
        import numpy as np
        TOP_K = 2
        key = jax.random.key(seed)
        ks = jax.random.split(key, 5)
        B, N, C, FF, E = (2, 512, 256, 1024, 8)
        x = jax.random.normal(ks[0], (B, N, C), dtype=jnp.float32)
        router_w = jax.random.normal(ks[1], (E, C), dtype=jnp.float32) * 0.02
        lim1 = np.sqrt(6.0 / (FF + C))
        expert_w1 = jax.random.uniform(ks[2], (E, FF, C), dtype=jnp.float32, minval=-lim1, maxval=lim1)
        expert_b1 = jnp.zeros((E, FF), dtype=jnp.float32)
        expert_w2 = jax.random.uniform(ks[3], (E, C, FF), dtype=jnp.float32, minval=-lim1, maxval=lim1)
        expert_b2 = jnp.zeros((E, C), dtype=jnp.float32)
        return {'x': x, 'router_w': router_w, 'expert_w1': expert_w1, 'expert_b1': expert_b1, 'expert_w2': expert_w2, 'expert_b2': expert_b2}
    _L3_ffn_all = _L3_ffn_setup()
    _L3_ffn_in = {k: v for k, v in _L3_ffn_all.items() if k in ('router_w', 'expert_w1', 'expert_b1', 'expert_w2', 'expert_b2')}
    del _L3_ffn_all
    return {'x': x, 'ctx_1024': ctx_1024, 'mask_SxS2_bk0': mask_SxS2_bk0, 'mask_BxS2_if1': mask_BxS2_if1, 'L0_xattn_W_kv': _L0_xattn_in['W_kv'], 'L0_xattn_b_kv': _L0_xattn_in['b_kv'], 'L0_xattn_W_q': _L0_xattn_in['W_q'], 'L0_xattn_b_q': _L0_xattn_in['b_q'], 'L0_xattn_W1': _L0_xattn_in['W1'], 'L0_xattn_b1': _L0_xattn_in['b1'], 'L0_xattn_W2': _L0_xattn_in['W2'], 'L0_xattn_b2': _L0_xattn_in['b2'], 'L0_ffn_cn_w1': _L0_ffn_in['cn_w1'], 'L0_ffn_cn_b1': _L0_ffn_in['cn_b1'], 'L0_ffn_cn_w2': _L0_ffn_in['cn_w2'], 'L0_ffn_cn_b2': _L0_ffn_in['cn_b2'], 'L0_ffn_cn_w3': _L0_ffn_in['cn_w3'], 'L0_ffn_cn_b3': _L0_ffn_in['cn_b3'], 'L0_ffn_cn_w4': _L0_ffn_in['cn_w4'], 'L0_ffn_cn_b4': _L0_ffn_in['cn_b4'], 'L0_ffn_gc_w1': _L0_ffn_in['gc_w1'], 'L0_ffn_gc_b1': _L0_ffn_in['gc_b1'], 'L0_ffn_gc_w2': _L0_ffn_in['gc_w2'], 'L0_ffn_gc_b2': _L0_ffn_in['gc_b2'], 'L0_ffn_gc_w3': _L0_ffn_in['gc_w3'], 'L0_ffn_gc_b3': _L0_ffn_in['gc_b3'], 'L0_ffn_adaptive_range': _L0_ffn_in['adaptive_range'], 'L1_xattn_Wq': _L1_xattn_in['Wq'], 'L1_xattn_bq': _L1_xattn_in['bq'], 'L1_xattn_Wk': _L1_xattn_in['Wk'], 'L1_xattn_bk': _L1_xattn_in['bk'], 'L1_xattn_Wv': _L1_xattn_in['Wv'], 'L1_xattn_bv': _L1_xattn_in['bv'], 'L1_xattn_Wo': _L1_xattn_in['Wo'], 'L1_xattn_bo': _L1_xattn_in['bo'], 'L1_ffn_router_w': _L1_ffn_in['router_w'], 'L1_ffn_w1': _L1_ffn_in['w1'], 'L1_ffn_b1': _L1_ffn_in['b1'], 'L1_ffn_w2': _L1_ffn_in['w2'], 'L1_ffn_b2': _L1_ffn_in['b2'], 'L2_xattn_Wq': _L2_xattn_in['Wq'], 'L2_xattn_Wk': _L2_xattn_in['Wk'], 'L2_xattn_Wv': _L2_xattn_in['Wv'], 'L2_xattn_Wo': _L2_xattn_in['Wo'], 'L2_ffn_gate_w': _L2_ffn_in['gate_w'], 'L2_ffn_ln_w': _L2_ffn_in['ln_w'], 'L2_ffn_ln_b': _L2_ffn_in['ln_b'], 'L2_ffn_fc1s': _L2_ffn_in['fc1s'], 'L2_ffn_b1s': _L2_ffn_in['b1s'], 'L2_ffn_fc2s': _L2_ffn_in['fc2s'], 'L2_ffn_b2s': _L2_ffn_in['b2s'], 'L3_xattn_Wq': _L3_xattn_in['Wq'], 'L3_xattn_Wk': _L3_xattn_in['Wk'], 'L3_xattn_Wv': _L3_xattn_in['Wv'], 'L3_xattn_Wo': _L3_xattn_in['Wo'], 'L3_ffn_router_w': _L3_ffn_in['router_w'], 'L3_ffn_expert_w1': _L3_ffn_in['expert_w1'], 'L3_ffn_expert_b1': _L3_ffn_in['expert_b1'], 'L3_ffn_expert_w2': _L3_ffn_in['expert_w2'], 'L3_ffn_expert_b2': _L3_ffn_in['expert_b2']}

def reference(x, ctx_1024, mask_SxS2_bk0, mask_BxS2_if1, L0_xattn_W_kv, L0_xattn_b_kv, L0_xattn_W_q, L0_xattn_b_q, L0_xattn_W1, L0_xattn_b1, L0_xattn_W2, L0_xattn_b2, L0_ffn_cn_w1, L0_ffn_cn_b1, L0_ffn_cn_w2, L0_ffn_cn_b2, L0_ffn_cn_w3, L0_ffn_cn_b3, L0_ffn_cn_w4, L0_ffn_cn_b4, L0_ffn_gc_w1, L0_ffn_gc_b1, L0_ffn_gc_w2, L0_ffn_gc_b2, L0_ffn_gc_w3, L0_ffn_gc_b3, L0_ffn_adaptive_range, L1_xattn_Wq, L1_xattn_bq, L1_xattn_Wk, L1_xattn_bk, L1_xattn_Wv, L1_xattn_bv, L1_xattn_Wo, L1_xattn_bo, L1_ffn_router_w, L1_ffn_w1, L1_ffn_b1, L1_ffn_w2, L1_ffn_b2, L2_xattn_Wq, L2_xattn_Wk, L2_xattn_Wv, L2_xattn_Wo, L2_ffn_gate_w, L2_ffn_ln_w, L2_ffn_ln_b, L2_ffn_fc1s, L2_ffn_b1s, L2_ffn_fc2s, L2_ffn_b2s, L3_xattn_Wq, L3_xattn_Wk, L3_xattn_Wv, L3_xattn_Wo, L3_ffn_router_w, L3_ffn_expert_w1, L3_ffn_expert_b1, L3_ffn_expert_w2, L3_ffn_expert_b2):
    import jax
    import jax.numpy as jnp

    def _L0_xattn_ref(_q, _kv, W_kv, b_kv, W_q, b_q, W1, b1, W2, b2):
        import jax, jax.numpy as jnp
        import numpy as np
        B, S, H = (8, 512, 256)
        kv = _kv @ W_kv + b_kv
        k, v = jnp.split(kv, 2, axis=-1)
        q = _q @ W_q + b_q
        scores = jnp.einsum('bqh,bkh->bqk', q, k)
        attn = jax.nn.softmax(scores, axis=-1)
        out = jnp.einsum('bqk,bkh->bqh', attn, v)
        hidden = jax.nn.gelu(out @ W1 + b1, approximate=False)
        return hidden @ W2 + b2

    def _L0_ffn_ref(x, cn_w1, cn_b1, cn_w2, cn_b2, cn_w3, cn_b3, cn_w4, cn_b4, gc_w1, gc_b1, gc_w2, gc_b2, gc_w3, gc_b3, adaptive_range):
        import jax, jax.numpy as jnp
        import numpy as np
        B, S, DIM = (4, 1024, 256)
        BASE_COUPLING = 0.1
        NUM_CYCLES = 3

        def _gelu(x):
            return jax.nn.gelu(x, approximate=False)

        def _coupling_net(h, w1, b1, w2, b2, w3, b3, w4, b4):
            h = _gelu(h @ w1 + b1)
            h = _gelu(h @ w2 + b2)
            h = _gelu(h @ w3 + b3)
            return jax.nn.sigmoid(h @ w4 + b4)

        def _global_net(h, w1, b1, w2, b2, w3, b3):
            h = _gelu(h @ w1 + b1)
            h = _gelu(h @ w2 + b2)
            return jax.nn.sigmoid(h @ w3 + b3)

        def _twist(x):
            o_r, o_i, p_r, p_i = jnp.split(x, 4, axis=-1)
            return jnp.concatenate([p_r, -p_i, -o_r, o_i], axis=-1)
        global_context = x.mean(axis=1, keepdims=True)
        gf = _global_net(global_context, gc_w1, gc_b1, gc_w2, gc_b2, gc_w3, gc_b3)
        out = x
        for _ in range(NUM_CYCLES):
            tf = _coupling_net(out, cn_w1, cn_b1, cn_w2, cn_b2, cn_w3, cn_b3, cn_w4, cn_b4)
            combined = 0.7 * gf + 0.3 * tf
            coupling = BASE_COUPLING + adaptive_range * (combined - 0.5) * 2.0
            out = out + coupling * _twist(out)
        return out

    def _L1_xattn_ref(q, k, v, Wq, bq, Wk, bk, Wv, bv, Wo, bo):
        import jax, jax.numpy as jnp
        import numpy as np
        D_MODEL = 256
        NUM_HEADS = 16
        HEAD_DIM = D_MODEL // NUM_HEADS
        B, S, _ = q.shape

        def proj(x, W, b):
            y = jnp.einsum('bsm,nm->bsn', x, W) + b
            return y.reshape(B, -1, NUM_HEADS, HEAD_DIM).transpose(0, 2, 1, 3)
        qh = proj(q, Wq, bq)
        kh = proj(k, Wk, bk)
        vh = proj(v, Wv, bv)
        factor = jnp.sqrt(jnp.float32(D_MODEL))
        scores = jnp.einsum('bhqd,bhkd->bhqk', qh, kh) / factor
        attn = jax.nn.softmax(scores, axis=-1)
        out = jnp.einsum('bhqk,bhkd->bhqd', attn, vh)
        out = out.transpose(0, 2, 1, 3).reshape(B, S, D_MODEL)
        return jnp.einsum('bsm,nm->bsn', out, Wo) + bo

    def _L1_ffn_ref(x, router_w, w1, b1, w2, b2):
        import jax, jax.numpy as jnp
        import numpy as np
        B, N, C, F, E, K = (2, 512, 256, 1024, 8, 2)
        Bb, Nn, Cc = x.shape
        x_flat = x.reshape(-1, Cc)
        logits = jnp.einsum('tc,ec->te', x_flat, router_w)
        probs = jax.nn.softmax(logits, axis=-1)
        top_w, top_idx = jax.lax.top_k(probs, K)
        top_w = top_w / (jnp.sum(top_w, axis=-1, keepdims=True) + 1e-09)
        h = jnp.einsum('tc,efc->tef', x_flat, w1) + b1[None]
        h = jax.nn.relu(h)
        y = jnp.einsum('tef,ecf->tec', h, w2) + b2[None]
        sel = jnp.take_along_axis(y, top_idx[:, :, None], axis=1)
        out = jnp.einsum('tkc,tk->tc', sel, top_w)
        return out.reshape(Bb, Nn, Cc)

    def _L2_xattn_ref(query, key, value, attn_mask, Wq, Wk, Wv, Wo):
        import jax, jax.numpy as jnp
        import numpy as np
        B, S, DIM, H = (4, 512, 256, 16)
        HD = DIM // H
        SCALE = HD ** (-0.5)

        def _heads(x):
            b, s, _ = x.shape
            return x.reshape(b, s, H, HD).transpose(0, 2, 1, 3)
        q = _heads(query @ Wq.T)
        k = _heads(key @ Wk.T)
        v = _heads(value @ Wv.T)
        logits = jnp.einsum('bhqd,bhkd->bhqk', q, k) * SCALE
        mask = attn_mask[None, None, :, :]
        masked = jnp.where(mask, logits, -1000000000.0)
        weights = jax.nn.softmax(masked, axis=-1)
        weights = weights * mask.astype(weights.dtype)
        denom = jnp.maximum(weights.sum(axis=-1, keepdims=True), 1e-09)
        weights = weights / denom
        out = jnp.einsum('bhqk,bhkd->bhqd', weights, v)
        out = out.transpose(0, 2, 1, 3).reshape(query.shape[0], query.shape[1], -1)
        return out @ Wo.T

    def _L2_ffn_ref(x, gate_w, ln_w, ln_b, fc1s, b1s, fc2s, b2s):
        import jax, jax.numpy as jnp
        import numpy as np
        B, S, D = (4, 1024, 256)
        DD = 4 * D
        N_EXPERTS = 8
        CAPACITY = 1.0
        LN_EPS = 1e-05
        og_shape = x.shape
        d = og_shape[-1]
        xf = x.reshape(-1, d)
        bs = xf.shape[0]
        n = gate_w.shape[0]
        k = int(bs * CAPACITY) // n
        scores = jax.nn.softmax(xf @ gate_w.T, axis=-1)
        vals, idx = jax.lax.top_k(scores.T, k)
        kept_w = vals.T
        kept_idx = idx.T
        flat_idx = kept_idx.reshape(-1)
        y = xf[flat_idx].reshape(k, n, d)
        mu = y.mean(-1, keepdims=True)
        var = ((y - mu) ** 2).mean(-1, keepdims=True)
        y = (y - mu) * jax.lax.rsqrt(var + LN_EPS) * ln_w + ln_b
        h = jnp.einsum('knd,nfd->knf', y, fc1s) + b1s
        h = jax.nn.gelu(h, approximate=True)
        out = jnp.einsum('knf,ndf->knd', h, fc2s) + b2s
        out = out * kept_w[..., None]
        xf = xf.at[flat_idx].add(out.reshape(k * n, d))
        return xf.reshape(og_shape)

    def _L3_xattn_ref(query, key, value, pad_mask, Wq, Wk, Wv, Wo):
        import jax, jax.numpy as jnp
        import numpy as np
        N_HEADS, EMB_DIM, K_DIM, V_DIM = (16, 256, 64, 64)
        B, L = (4, 512)
        batch, Lq, _ = query.shape
        Lk = key.shape[1]
        q = (query @ Wq).reshape(batch, Lq, N_HEADS, K_DIM)
        k = (key @ Wk).reshape(batch, Lk, N_HEADS, K_DIM)
        v = (value @ Wv).reshape(batch, Lk, N_HEADS, V_DIM)
        logits = jnp.einsum('bqhd,bkhd->bhqk', q, k) / np.sqrt(K_DIM).astype(np.float32)
        causal = jnp.tril(jnp.ones((Lq, Lk), dtype=bool))
        logits = jnp.where(causal[None, None], logits, -jnp.inf)
        keep = (pad_mask != 0)[:, None, None, :]
        logits = jnp.where(keep, logits, -jnp.inf)
        probs = jax.nn.softmax(logits, axis=-1)
        attn = jnp.einsum('bhqk,bkhd->bqhd', probs, v).reshape(batch, Lq, N_HEADS * V_DIM)
        return attn @ Wo

    def _L3_ffn_ref(x, router_w, expert_w1, expert_b1, expert_w2, expert_b2):
        import jax, jax.numpy as jnp
        import numpy as np
        TOP_K = 2
        router_logits = jnp.einsum('bnc,ec->bne', x, router_w)
        router_probs = jax.nn.softmax(router_logits, axis=-1)
        expert_weights, expert_idx = jax.lax.top_k(router_probs, TOP_K)
        expert_weights = expert_weights / (expert_weights.sum(axis=-1, keepdims=True) + 1e-09)
        h = jnp.einsum('bnc,efc->bnef', x, expert_w1) + expert_b1
        h = jax.nn.gelu(h, approximate=False)
        out_all = jnp.einsum('bnef,ecf->bnec', h, expert_w2) + expert_b2
        out_k = jnp.take_along_axis(out_all, expert_idx[..., None], axis=2)
        return (out_k * expert_weights[..., None]).sum(axis=2)
    x = x + _L0_xattn_ref(_layernorm(x, axis=-1), ctx_1024, L0_xattn_W_kv, L0_xattn_b_kv, L0_xattn_W_q, L0_xattn_b_q, L0_xattn_W1, L0_xattn_b1, L0_xattn_W2, L0_xattn_b2)
    x = x + _L0_ffn_ref(_layernorm(x, axis=-1), L0_ffn_cn_w1, L0_ffn_cn_b1, L0_ffn_cn_w2, L0_ffn_cn_b2, L0_ffn_cn_w3, L0_ffn_cn_b3, L0_ffn_cn_w4, L0_ffn_cn_b4, L0_ffn_gc_w1, L0_ffn_gc_b1, L0_ffn_gc_w2, L0_ffn_gc_b2, L0_ffn_gc_w3, L0_ffn_gc_b3, L0_ffn_adaptive_range)
    x = x + _L1_xattn_ref(_layernorm(x, axis=-1), ctx_1024, ctx_1024, L1_xattn_Wq, L1_xattn_bq, L1_xattn_Wk, L1_xattn_bk, L1_xattn_Wv, L1_xattn_bv, L1_xattn_Wo, L1_xattn_bo)
    x = x + _L1_ffn_ref(_layernorm(x, axis=-1), L1_ffn_router_w, L1_ffn_w1, L1_ffn_b1, L1_ffn_w2, L1_ffn_b2)
    x = x + _L2_xattn_ref(_layernorm(x, axis=-1), ctx_1024, ctx_1024, mask_SxS2_bk0, L2_xattn_Wq, L2_xattn_Wk, L2_xattn_Wv, L2_xattn_Wo)
    x = x + _L2_ffn_ref(_layernorm(x, axis=-1), L2_ffn_gate_w, L2_ffn_ln_w, L2_ffn_ln_b, L2_ffn_fc1s, L2_ffn_b1s, L2_ffn_fc2s, L2_ffn_b2s)
    x = x + _L3_xattn_ref(_layernorm(x, axis=-1), ctx_1024, ctx_1024, mask_BxS2_if1, L3_xattn_Wq, L3_xattn_Wk, L3_xattn_Wv, L3_xattn_Wo)
    x = x + _L3_ffn_ref(_layernorm(x, axis=-1), L3_ffn_router_w, L3_ffn_expert_w1, L3_ffn_expert_b1, L3_ffn_expert_w2, L3_ffn_expert_b2)
    return x

_drawn_inputs = setup_inputs


def setup_inputs(seed=0):
    import zlib

    import numpy as np

    out = dict(_drawn_inputs(seed))
    spreads = {'L0_xattn_b_kv': (0.0, 0.1),
     'L0_xattn_b_q': (0.0, 0.1),
     'L0_xattn_b1': (0.0, 0.1),
     'L0_xattn_b2': (0.0, 0.1),
     'L0_ffn_cn_b1': (0.0, 0.8),
     'L0_ffn_cn_b2': (0.0, 2.0),
     'L0_ffn_cn_b3': (0.0, 2.0),
     'L0_ffn_gc_b1': (0.0, 0.798),
     'L0_ffn_gc_b2': (0.0, 0.698),
     'L1_xattn_bq': (0.0, 0.8),
     'L1_xattn_bk': (0.0, 2.0),
     'L1_xattn_bv': (0.0, 0.1),
     'L1_xattn_bo': (0.0, 0.1),
     'L1_ffn_b1': (0.0, 0.27),
     'L1_ffn_b2': (0.0, 0.1),
     'L2_ffn_ln_w': (1.0, 0.6),
     'L2_ffn_ln_b': (0.0, 0.8),
     'L3_ffn_expert_b1': (0.0, 0.513),
     'L3_ffn_expert_b2': (0.0, 0.412)}
    factors = {'L0_ffn_cn_w1': 4.326,
     'L0_ffn_cn_w2': 4.764,
     'L0_ffn_cn_w3': 4.225,
     'L0_ffn_cn_w4': 4.532,
     'L0_ffn_gc_w1': 4.39,
     'L0_ffn_gc_w3': 3.187,
     'L2_xattn_Wq': 8.0,
     'L2_xattn_Wk': 8.0,
     'L2_ffn_b1s': 8.0,
     'L2_ffn_b2s': 22.903}
    for name, (base, spread) in spreads.items():
        noise = np.random.default_rng([zlib.crc32(name.encode()), seed]).standard_normal(out[name].shape)
        drawn = base * np.exp(spread * noise) if base else spread * noise
        out[name] = jnp.asarray(drawn.astype(out[name].dtype))
    for name, factor in factors.items():
        out[name] = (out[name] * factor).astype(out[name].dtype)
    return out
```

```python
from contextlib import ExitStack

import concourse.bass as bass
from concourse import mybir

F32 = mybir.dt.float32
BF16 = mybir.dt.bfloat16
I32 = mybir.dt.int32
U8 = mybir.dt.uint8
ACT = mybir.ActivationFunctionType
ALU = mybir.AluOpType
AX = mybir.AxisListType
ds = bass.ds

P = 128
B = 4
S = 512
SK = 1024
D = 256
DT = D // P
QT = S // P
KT = SK // P
NT = B * QT
F = 1024
FT = F // P
E = 8
H = 16
LN_EPS = 1e-5
BIG = 2.0 ** 30


class Chain:

    def __init__(self, eng, sem, base=0):
        self.eng, self.sem, self.base, self.n = eng, sem, base, 0

    def mark(self, ins):
        ins.then_inc(self.sem, 1)
        self.n += 1
        return self.n

    def wait(self, k=None):
        self.eng.wait_ge(self.sem, self.base + (self.n if k is None else k))


class Ring:

    def __init__(self, banks, full, free, per):
        self.banks, self.full, self.free, self.per = banks, full, free, per

    def start(self, eng):
        eng.sem_inc(self.free, 1)

    def bank(self, n):
        return self.banks[n % len(self.banks)]

    def wait_turns(self, eng, b):
        eng.wait_ge(self.free, b * self.per + 1)

    def wait_free(self, pe, b, n):
        if n >= len(self.banks):
            pe.wait_ge(self.free, b * self.per + n - len(self.banks) + 2)

    def wait_full(self, eng, b, n):
        eng.wait_ge(self.full, b * self.per + n + 1)

    def wait_done(self, eng, b, n):
        eng.wait_ge(self.free, b * self.per + n + 2)


def split_wait(eng, sem):
    eng.sem_inc(sem, 1)


def program(nc, t, out, stages):
    ctx = ExitStack()
    with ctx:
        def sb(c, name, shape, dt=F32):
            return c.enter_context(nc.sbuf_tensor(name, shape, dt))

        taken = []

        def sem(name):
            taken.append(nc.alloc_semaphore(name))
            return taken[-1]

        def end_layer():
            nc.clear_and_free_semaphores(taken)
            taken.clear()
            nc.all_engine_barrier()

        K = {"nc": nc, "t": t, "sb": sb, "sem": sem}
        K["PS"] = ctx.enter_context(nc.psum_tensor("PS", [P, 8, 512], F32))
        K["X"] = sb(ctx, "X", [P, NT, D])
        K["ctxT"] = sb(ctx, "ctxT", [P, DT, B * SK])
        K["ident"] = sb(ctx, "ident", [P, P])
        K["identb"] = sb(ctx, "identb", [P, P], BF16)
        K["ones"] = sb(ctx, "ones", [P, P])
        K["onesb"] = sb(ctx, "onesb", [1, SK], BF16)
        K["eps"] = sb(ctx, "eps", [P, 1])
        K["passed"] = nc.alloc_semaphore("waits_passed")
        load_stage(K)
        layers = (lambda: single_head_attention(K),
                  lambda: coupled_ffn(K),
                  lambda: head_attention(K, "L1", 1.0 / 16.0, True, False),
                  lambda: experts(K, "L1", ACT.Relu, False),
                  lambda: head_attention(K, "L2", 0.25, False, True),
                  lambda: experts(K, "L2", ACT.Gelu_apprx_tanh, True),
                  lambda: causal_attention(K),
                  lambda: experts(K, "L3", ACT.Gelu, False))
        for i in stages:
            layers[i]()
            end_layer()
        store_stage(K, out)


def load_stage(K):
    nc, t, sb, sem, PS = K["nc"], K["t"], K["sb"], K["sem"], K["PS"]
    X, ctxT, ident, identb, ones, onesb, eps = (K[n] for n in ("X", "ctxT", "ident", "identb", "ones", "onesb", "eps"))
    with ExitStack() as c:
        raw = sb(c, "ctx_raw", [P, B * KT, D])
        x_in, ctx_in, made, idm, turned, moved, movedv = (sem(n) for n in (
            "x_in", "ctx_in", "ident_zero", "ident_made", "ctx_turned", "ctx_moved_act", "ctx_moved_dve"))
        with nc.Block() as block:
            @block.sync
            def _(sp):
                for b in range(B):
                    sp.dma_start(raw[:, KT * b:KT * (b + 1), :],
                                 t["ctx_1024"][b].rearrange("(k p) d -> p k d", p=P)).then_inc(ctx_in, 16)
                sp.dma_start(X[:], t["x"].rearrange("b (k p) d -> p (b k) d", p=P)).then_inc(x_in, 16)
                sp.wait_ge(x_in, 16)

            @block.gpsimd
            def _(pool):
                pool.memset(ones[:], 1.0).then_inc(made, 1)
                pool.memset(eps[:], LN_EPS).then_inc(made, 1)
                pool.memset(onesb[:], 1.0).then_inc(made, 1)
                pool.wait_ge(made, 3)
                pool.affine_select(out=ident[:], in_=ones[:], compare_op=ALU.is_equal, fill=0.0, base=0,
                                   pattern=[[1, P]], channel_multiplier=-1).then_inc(idm, 1)
                pool.wait_ge(idm, 1)
                pool.tensor_copy(identb[:], ident[:]).then_inc(idm, 1)
                pool.wait_ge(idm, 2)

            def half(n):
                return n // DT, n % DT

            @block.tensor
            def _(pe):
                pe.wait_ge(idm, 1)
                for n in range(B * KT // 4 * DT):
                    g, f = half(n)
                    pe.wait_ge(ctx_in, 16 * B)
                    if n >= 8:
                        pe.wait_ge((moved, movedv)[n % 2], (n - 8) // 2 + 1)
                    for k in range(4):
                        mm = pe.transpose(PS[:, n % 8, k * P:(k + 1) * P], raw[:, 4 * g + k, f * P:(f + 1) * P], ident[:])
                    mm.then_inc(turned, 1)

            def move(eng, mine, done, op):
                for n in range(mine, B * KT // 4 * DT, 2):
                    g, f = half(n)
                    eng.wait_ge(turned, n + 1)
                    op(ctxT[:, f, 512 * g:512 * (g + 1)], PS[:, n % 8, :]).then_inc(done, 1)
                eng.wait_ge(done, B * KT // 4 * DT // 2)

            @block.scalar
            def _(act):
                move(act, 0, moved, act.copy)

            @block.vector
            def _(dve):
                move(dve, 1, movedv, dve.tensor_copy)


def store_stage(K, out):
    nc, X = K["nc"], K["X"]
    stored = K["sem"]("stored")
    with nc.Block() as block:
        @block.sync
        def _(sp):
            sp.dma_start(out.rearrange("b (k p) d -> p (b k) d", p=P), X[:]).then_inc(stored, 16)
            sp.wait_ge(stored, 16)


def ln_statistics(dve, ch, src, st, mv):
    for k in range(QT):
        ch.mark(dve.bn_stats(st[:, k, :], src(k)))
    ch.wait()
    for k in range(QT):
        ch.mark(dve.bn_aggr(mv[:, k, :], st[:, k, :]))
    ch.wait()


def ln_apply(dve, ch, src, mv, std, rstd, xn, done):
    ch.mark(dve.reciprocal(rstd[:], std[:]))
    ch.wait()
    for k in range(QT):
        dve.tensor_scalar(xn[:, k, :], src(k), mv[:, k, 0:1], rstd[:, k:k + 1], ALU.subtract, ALU.mult).then_inc(done, 1)


def single_head_attention(K):
    nc, t, sb, sem, PS, X, ctxT = (K[n] for n in ("nc", "t", "sb", "sem", "PS", "X", "ctxT"))
    ident, ones, eps = K["ident"], K["ones"], K["eps"]
    N_ACT = 4 + 1 + 2 + FT
    N_DVE = 4 + 1 + 2 * QT + DT + QT
    XT_A, Q_A, H_A = 4, 5, 7
    XT_D, T_D, O_D, Y_D = 4, 5, 5 + 2 * QT, 5 + 2 * QT + DT
    N_CH = 2 * QT - 1 + 1 + QT
    with ExitStack() as c:
        wkv = sb(c, "a0_wkv", [P, DT, 2 * D]); wq = sb(c, "a0_wq", [P, DT, D])
        w1 = sb(c, "a0_w1", [P, DT, F]); w2 = sb(c, "a0_w2", [P, FT, D])
        bk = sb(c, "a0_bk", [P, DT]); bq = sb(c, "a0_bq", [P, DT]); b1 = sb(c, "a0_b1", [P, FT])
        bv = sb(c, "a0_bv", [1, D]); b2 = sb(c, "a0_b2", [1, D])
        cb = sb(c, "a0_ctxb", [P, DT, SK])
        xn = sb(c, "a0_xn", [P, QT, D]); xT = sb(c, "a0_xT", [P, DT, S])
        qT = sb(c, "a0_qT", [P, DT, S]); kT = sb(c, "a0_kT", [P, DT, SK]); v = sb(c, "a0_v", [P, KT, D])
        pr = sb(c, "a0_pr", [P, 2, SK]); pT = sb(c, "a0_pT", [P, KT, S])
        oT = sb(c, "a0_oT", [P, DT, S]); hT = sb(c, "a0_hT", [P, FT, S])
        st = sb(c, "a0_st", [P, QT, 6]); mv = sb(c, "a0_mv", [P, QT, 2])
        std = sb(c, "a0_std", [P, QT]); rstd = sb(c, "a0_rstd", [P, QT])
        nmax = sb(c, "a0_nmax", [P, QT]); psum_ = sb(c, "a0_sum", [P, QT]); rsum = sb(c, "a0_rsum", [P, QT])
        w_in, ch_s, std_s, mv_s, xn_s, cb_s = (sem("a0_" + n) for n in (
            "weights_in", "dve_chain", "std_ready", "var_ready", "xn_ready", "ctx_copied"))
        s_full, s_max, s_exp, p_norm = (sem("a0_" + n) for n in ("scores_full", "max_ready", "exp_done", "probs_scaled"))
        A = Ring([PS[:, 0, :], PS[:, 1, :]], sem("a0_act_full"), sem("a0_act_free"), N_ACT)
        V = Ring([PS[:, 2, :], PS[:, 3, :]], sem("a0_dve_full"), sem("a0_dve_free"), N_DVE)
        scores = [PS[:, 4:6, :], PS[:, 6:8, :]]
        N_W = 16 * 9
        with nc.Block() as block:
            @block.sync
            def _(sp):
                for dst, src in (
                    (wkv[:], t["L0_xattn_W_kv"].rearrange("(k p) n -> p k n", p=P)),
                    (wq[:], t["L0_xattn_W_q"].rearrange("(k p) n -> p k n", p=P)),
                    (bk[:], t["L0_xattn_b_kv_cols"][:, 0:DT]),
                    (bq[:], t["L0_xattn_b_q_cols"]),
                    (b1[:], t["L0_xattn_b1_cols"]),
                    (bv[:], t["L0_xattn_b_kv"][D:2 * D].rearrange("(a n) -> a n", a=1)),
                    (b2[:], t["L0_xattn_b2"].rearrange("(a n) -> a n", a=1)),
                    (w1[:], t["L0_xattn_W1"].rearrange("(k p) n -> p k n", p=P)),
                    (w2[:], t["L0_xattn_W2"].rearrange("(k p) n -> p k n", p=P)),
                ):
                    sp.dma_start(dst, src).then_inc(w_in, 16)

            @block.gpsimd
            def _(pool):
                A.start(pool)
                V.start(pool)
                with pool.Fori(0, B) as b:
                    V.wait_turns(pool, b)
                    for f in range(DT):
                        pool.tensor_copy(cb[:, f, :], ctxT[:, f, ds(b * SK, SK)]).then_inc(cb_s, 1)

            @block.tensor
            def _(pe):
                pe.wait_ge(w_in, N_W)
                with pe.Fori(0, B) as b:
                    pe.wait_ge(cb_s, b * DT + DT)
                    for m in range(DT):
                        for n in range(2):
                            i = 2 * m + n
                            A.wait_free(pe, b, i)
                            for k in range(DT):
                                mm = pe.matmul(A.bank(i), wkv[:, k, m * P:(m + 1) * P], cb[:, k, n * 512:(n + 1) * 512],
                                               start=(k == 0), stop=(k == DT - 1))
                            mm.then_inc(A.full, 1)
                    for i in range(4):
                        V.wait_free(pe, b, i)
                        for u in range(2):
                            o = V.bank(i)[:, u * D:(u + 1) * D]
                            pe.matmul(o, ones[0:1, :], bv[:], start=True, stop=False, skip_group_check=True)
                            for k in range(DT):
                                mm = pe.matmul(o, cb[:, k, (2 * i + u) * P:(2 * i + u + 1) * P], wkv[:, k, D:2 * D],
                                               start=False, stop=(k == DT - 1), skip_group_check=True)
                        mm.then_inc(V.full, 1)
                    pe.wait_ge(xn_s, b * QT + QT)
                    for f, (R, i) in enumerate(((A, XT_A), (V, XT_D))):
                        R.wait_free(pe, b, i)
                        for k in range(QT):
                            mm = pe.transpose(R.bank(i)[:, k * P:(k + 1) * P], xn[:, k, f * P:(f + 1) * P], ident[:])
                        mm.then_inc(R.full, 1)
                    A.wait_done(pe, b, XT_A)
                    V.wait_done(pe, b, XT_D)
                    for m in range(DT):
                        A.wait_free(pe, b, Q_A + m)
                        for k in range(DT):
                            mm = pe.matmul(A.bank(Q_A + m), wq[:, k, m * P:(m + 1) * P], xT[:, k, :],
                                           start=(k == 0), stop=(k == DT - 1))
                        mm.then_inc(A.full, 1)
                    A.wait_done(pe, b, Q_A + 1)

                    def turn(q):
                        pe.wait_ge(p_norm, b * QT + q + 1)
                        for u in range(2):
                            i = T_D + 2 * q + u
                            V.wait_free(pe, b, i)
                            for k in range(4):
                                mm = pe.transpose(V.bank(i)[:, k * P:(k + 1) * P],
                                                  pr[:, q % 2, (4 * u + k) * P:(4 * u + k + 1) * P], ident[:])
                            mm.then_inc(V.full, 1)

                    for q in range(QT):
                        if q >= 2:
                            pe.wait_ge(s_exp, b * QT + q - 1)
                        for n in range(2):
                            for k in range(DT):
                                mm = pe.matmul(scores[q % 2][:, n, :], qT[:, k, q * P:(q + 1) * P],
                                               kT[:, k, n * 512:(n + 1) * 512], start=(k == 0), stop=(k == DT - 1))
                        mm.then_inc(s_full, 1)
                        if q >= 1:
                            turn(q - 1)
                    turn(QT - 1)
                    V.wait_done(pe, b, T_D + 2 * QT - 1)
                    for m in range(DT):
                        i = O_D + m
                        V.wait_free(pe, b, i)
                        for k in range(KT):
                            mm = pe.matmul(V.bank(i), v[:, k, m * P:(m + 1) * P], pT[:, k, :],
                                           start=(k == 0), stop=(k == KT - 1))
                        mm.then_inc(V.full, 1)
                    V.wait_done(pe, b, O_D + 1)
                    for m in range(FT):
                        i = H_A + m
                        A.wait_free(pe, b, i)
                        for k in range(DT):
                            mm = pe.matmul(A.bank(i), w1[:, k, m * P:(m + 1) * P], oT[:, k, :],
                                           start=(k == 0), stop=(k == DT - 1))
                        mm.then_inc(A.full, 1)
                    A.wait_done(pe, b, H_A + FT - 1)
                    for q in range(QT):
                        i = Y_D + q
                        V.wait_free(pe, b, i)
                        o = V.bank(i)[:, 0:D]
                        pe.matmul(o, ones[0:1, :], b2[:], start=True, stop=False)
                        for k in range(FT):
                            mm = pe.matmul(o, hT[:, k, q * P:(q + 1) * P], w2[:, k, :], start=False, stop=(k == FT - 1))
                        mm.then_inc(V.full, 1)

            @block.scalar
            def _(act):
                act.wait_ge(w_in, N_W)
                with act.Fori(0, B) as b:
                    V.wait_turns(act, b)
                    act.wait_ge(mv_s, b + 1)
                    act.activation(std[:], mv[:, :, 1], ACT.Sqrt, bias=eps[:]).then_inc(std_s, 1)
                    for m in range(DT):
                        for n in range(2):
                            A.wait_full(act, b, 2 * m + n)
                            act.activation(kT[:, m, n * 512:(n + 1) * 512], A.bank(2 * m + n), ACT.Identity,
                                           bias=bk[:, m:m + 1]).then_inc(A.free, 1)
                    A.wait_full(act, b, XT_A)
                    act.copy(xT[:, 0, :], A.bank(XT_A)).then_inc(A.free, 1)
                    for m in range(DT):
                        A.wait_full(act, b, Q_A + m)
                        act.activation(qT[:, m, :], A.bank(Q_A + m), ACT.Identity, bias=bq[:, m:m + 1]).then_inc(A.free, 1)
                    for q in range(QT):
                        act.wait_ge(s_max, b * QT + q + 1)
                        if q >= 2:
                            V.wait_done(act, b, T_D + 2 * (q - 2) + 1)
                        act.activation(pr[:, q % 2, :], scores[q % 2], ACT.Exp, bias=nmax[:, q:q + 1],
                                       accum_out=psum_[:, q:q + 1]).then_inc(s_exp, 1)
                    for m in range(FT):
                        A.wait_full(act, b, H_A + m)
                        act.activation(hT[:, m, :], A.bank(H_A + m), ACT.Gelu, bias=b1[:, m:m + 1]).then_inc(A.free, 1)

            @block.vector
            def _(dve):
                with dve.Fori(0, B) as b:
                    ch = Chain(dve, ch_s, b * N_CH)
                    V.wait_turns(dve, b)
                    split_wait(dve, K["passed"])
                    src = lambda k: X[:, ds(b * QT + k, 1), :]
                    for k in range(QT):
                        ch.mark(dve.bn_stats(st[:, k, :], src(k)))
                    ch.wait()
                    split_wait(dve, K["passed"])
                    for k in range(QT):
                        ins = dve.bn_aggr(mv[:, k, :], st[:, k, :])
                        if k < QT - 1:
                            ch.mark(ins)
                    ins.then_inc(mv_s, 1)
                    dve.wait_ge(mv_s, b + 1)
                    dve.wait_ge(std_s, b + 1)
                    ln_apply(dve, ch, src, mv, std, rstd, xn, xn_s)
                    for i in range(4):
                        V.wait_full(dve, b, i)
                        dve.tensor_copy(v[:, 2 * i:2 * i + 2, :], V.bank(i).rearrange("p (u d) -> p u d", u=2)).then_inc(V.free, 1)
                    V.wait_full(dve, b, XT_D)
                    dve.tensor_copy(xT[:, 1, :], V.bank(XT_D)).then_inc(V.free, 1)

                    def max_of(q):
                        dve.wait_ge(s_full, b * QT + q + 1)
                        dve.tensor_reduce(nmax[:, q:q + 1], scores[q % 2], AX.XY, ALU.max, negate=True).then_inc(s_max, 1)

                    def scale(q):
                        dve.wait_ge(s_exp, b * QT + q + 1)
                        ch.mark(dve.reciprocal(rsum[:, q:q + 1], psum_[:, q:q + 1]))
                        ch.wait()
                        dve.tensor_scalar(pr[:, q % 2, :], pr[:, q % 2, :], rsum[:, q:q + 1], None,
                                          ALU.mult).then_inc(p_norm, 1)

                    def turned(q):
                        for u in range(2):
                            i = T_D + 2 * q + u
                            V.wait_full(dve, b, i)
                            dve.tensor_copy(pT[:, 4 * u:4 * u + 4, q * P:(q + 1) * P],
                                            V.bank(i).rearrange("p (k n) -> p k n", k=4)).then_inc(V.free, 1)

                    for q in range(QT):
                        max_of(q)
                        if q >= 1:
                            scale(q - 1)
                            turned(q - 1)
                    scale(QT - 1)
                    turned(QT - 1)
                    for m in range(DT):
                        V.wait_full(dve, b, O_D + m)
                        dve.tensor_copy(oT[:, m, :], V.bank(O_D + m)).then_inc(V.free, 1)
                    for q in range(QT):
                        V.wait_full(dve, b, Y_D + q)
                        x = X[:, ds(b * QT + q, 1), :]
                        dve.tensor_tensor(x, x, V.bank(Y_D + q)[:, None, 0:D], ALU.add).then_inc(V.free, 1)
                    assert ch.n == N_CH, ch.n


def coupled_ffn(K):
    nc, t, sb, sem, PS, X = (K[n] for n in ("nc", "t", "sb", "sem", "PS", "X"))
    ident, ones, eps = K["ident"], K["ones"], K["eps"]
    TURNS = 3
    H3 = 64
    N_ACT = 1 + 3 + TURNS * 5
    N_DVE = 1 + QT
    N_CH = 2 * QT - 1 + 1 + 1 + 2 + TURNS * 3
    with ExitStack() as c:
        w1 = sb(c, "f0_w1", [P, DT, D]); w2 = sb(c, "f0_w2", [P, DT, P]); w3 = sb(c, "f0_w3", [P, H3])
        w4 = sb(c, "f0_w4", [H3, 1]); w4b = sb(c, "f0_w4b", [H3, P])
        g1w = sb(c, "f0_g1w", [P, DT, P]); g2w = sb(c, "f0_g2w", [P, H3]); g3w = sb(c, "f0_g3w", [H3, 1])
        b1 = sb(c, "f0_b1", [P, DT]); b2 = sb(c, "f0_b2", [P, 1]); b3 = sb(c, "f0_b3", [H3, 1])
        gb1 = sb(c, "f0_gb1", [P, 1]); gb2 = sb(c, "f0_gb2", [H3, 1])
        row = sb(c, "f0_row", [1, 3]); sc = sb(c, "f0_sc", [P, 3]); slope = sb(c, "f0_slope", [P, 1])
        sign = sb(c, "f0_sign", [P, 2])
        xn = sb(c, "f0_xn", [P, QT, D]); y = sb(c, "f0_y", [P, DT, S])
        mean = sb(c, "f0_mean", [P, DT]); g1 = sb(c, "f0_g1", [P, 1]); g2 = sb(c, "f0_g2", [H3, 1])
        g2b = sb(c, "f0_g2b", [H3, P]); gf = sb(c, "f0_gf", [P, 1]); off = sb(c, "f0_off", [P, 2])
        h1 = sb(c, "f0_h1", [P, DT, S]); h2 = sb(c, "f0_h2", [P, S]); h3 = sb(c, "f0_h3", [H3, S])
        tf = sb(c, "f0_tf", [P, S]); cp = sb(c, "f0_cp", [P, S]); tw = sb(c, "f0_tw", [P, DT, S])
        st = sb(c, "f0_st", [P, QT, 6]); mv = sb(c, "f0_mv", [P, QT, 2])
        std = sb(c, "f0_std", [P, QT]); rstd = sb(c, "f0_rstd", [P, QT])
        w_in, made, ch_s, std_s, mv_s, xn_s, mean_s, g2b_s, y_s, sc_full, sc_s = (sem("f0_" + n) for n in (
            "weights_in", "constants_made", "dve_chain", "std_ready", "var_ready", "xn_ready", "mean_ready",
            "g2_spread", "y_updated", "scalars_full", "scalars_ready"))
        A = Ring([PS[:, i, :] for i in range(4)], sem("f0_act_full"), sem("f0_act_free"), N_ACT)
        V = Ring([PS[:, i, :] for i in range(4, 7)], sem("f0_dve_full"), sem("f0_dve_free"), N_DVE)
        loads = [(w1[:], t["L0_ffn_cn_w1"].rearrange("(k p) n -> p k n", p=P)),
                 (w2[:], t["L0_ffn_cn_w2"].rearrange("(k p) n -> p k n", p=P)),
                 (w3[:], t["L0_ffn_cn_w3"]), (w4[:], t["L0_ffn_cn_w4"]),
                 (g1w[:], t["L0_ffn_gc_w1"].rearrange("(k p) n -> p k n", p=P)),
                 (g2w[:], t["L0_ffn_gc_w2"]), (g3w[:], t["L0_ffn_gc_w3"]),
                 (b1[:], t["L0_ffn_cn_b1_cols"]), (b2[:], t["L0_ffn_cn_b2_cols"]),
                 (b3[:], t["L0_ffn_cn_b3"].rearrange("(p a) -> p a", a=1)),
                 (gb1[:], t["L0_ffn_gc_b1_cols"]), (gb2[:], t["L0_ffn_gc_b2"].rearrange("(p a) -> p a", a=1)),
                 (row[:, 0:1], t["L0_ffn_cn_b4"].rearrange("(a n) -> a n", a=1)),
                 (row[:, 1:2], t["L0_ffn_gc_b3"].rearrange("(a n) -> a n", a=1)),
                 (row[:, 2:3], t["L0_ffn_adaptive_range"].rearrange("(a n) -> a n", a=1))]
        with nc.Block() as block:
            @block.sync
            def _(sp):
                for dst, src in loads:
                    sp.dma_start(dst, src).then_inc(w_in, 16)

            @block.gpsimd
            def _(pool):
                A.start(pool)
                V.start(pool)
                pool.memset(sign[0:64, 0:1], 1.0).then_inc(made, 1)
                pool.memset(sign[64:128, 0:1], -1.0).then_inc(made, 1)
                pool.memset(sign[0:64, 1:2], -1.0).then_inc(made, 1)
                pool.memset(sign[64:128, 1:2], 1.0).then_inc(made, 1)

            @block.tensor
            def _(pe):
                pe.wait_ge(w_in, 16 * len(loads))
                pe.matmul(PS[:, 7, 0:3], ones[0:1, :], row[:], start=True, stop=True).then_inc(sc_full, 1)
                pe.wait_ge(sc_s, 3)
                with pe.Fori(0, B) as b:
                    pe.wait_ge(xn_s, b * QT + QT)
                    for f, R in enumerate((A, V)):
                        for k in range(QT):
                            mm = pe.transpose(R.bank(0)[:, k * P:(k + 1) * P], xn[:, k, f * P:(f + 1) * P], ident[:])
                        mm.then_inc(R.full, 1)
                    i = 1
                    pe.wait_ge(mean_s, b + 1)
                    for k in range(DT):
                        mm = pe.matmul(A.bank(i)[:, 0:1], g1w[:, k, :], mean[:, k:k + 1], start=(k == 0), stop=(k == DT - 1))
                    mm.then_inc(A.full, 1)
                    A.wait_done(pe, b, i)
                    i += 1
                    pe.matmul(A.bank(i)[0:H3, 0:1], g2w[:], g1[:], start=True, stop=True).then_inc(A.full, 1)
                    i += 1
                    pe.wait_ge(g2b_s, b + 1)
                    pe.matmul(A.bank(i)[:, 0:1], g2b[:], g3w[:], start=True, stop=True).then_inc(A.full, 1)
                    i += 1
                    for r in range(TURNS):
                        if r:
                            pe.wait_ge(y_s, b * TURNS * DT + DT * r)
                        for m in range(DT):
                            A.wait_free(pe, b, i)
                            for k in range(DT):
                                mm = pe.matmul(A.bank(i), w1[:, k, m * P:(m + 1) * P], y[:, k, :],
                                               start=(k == 0), stop=(k == DT - 1))
                            mm.then_inc(A.full, 1)
                            i += 1
                        A.wait_done(pe, b, i - 1)
                        for k in range(DT):
                            mm = pe.matmul(A.bank(i), w2[:, k, :], h1[:, k, :], start=(k == 0), stop=(k == DT - 1))
                        mm.then_inc(A.full, 1)
                        A.wait_done(pe, b, i)
                        i += 1
                        pe.matmul(A.bank(i)[0:H3, :], w3[:], h2[:], start=True, stop=True).then_inc(A.full, 1)
                        A.wait_done(pe, b, i)
                        i += 1
                        pe.matmul(A.bank(i), w4b[:], h3[:], start=True, stop=True).then_inc(A.full, 1)
                        i += 1
                    assert i == N_ACT
                    pe.wait_ge(y_s, b * TURNS * DT + DT * TURNS)
                    for q in range(QT):
                        V.wait_free(pe, b, 1 + q)
                        for f in range(DT):
                            mm = pe.transpose(V.bank(1 + q)[:, f * P:(f + 1) * P], y[:, f, q * P:(q + 1) * P], ident[:])
                        mm.then_inc(V.full, 1)

            @block.scalar
            def _(act):
                act.wait_ge(w_in, 16 * len(loads))
                act.wait_ge(sc_s, 3)
                with act.Fori(0, B) as b:
                    V.wait_turns(act, b)
                    act.wait_ge(mv_s, b + 1)
                    act.activation(std[:], mv[:, :, 1], ACT.Sqrt, bias=eps[:]).then_inc(std_s, 1)
                    i = 0

                    def job(dst, src, func, bias):
                        nonlocal i
                        A.wait_full(act, b, i)
                        if bias is None:
                            act.copy(dst, src(A.bank(i))).then_inc(A.free, 1)
                        else:
                            act.activation(dst, src(A.bank(i)), func, bias=bias).then_inc(A.free, 1)
                        i += 1

                    job(y[:, 0, :], lambda o: o, None, None)
                    job(g1[:], lambda o: o[:, 0:1], ACT.Gelu, gb1[:])
                    job(g2[:], lambda o: o[0:H3, 0:1], ACT.Gelu, gb2[:])
                    job(gf[:], lambda o: o[:, 0:1], ACT.Sigmoid, sc[:, 1:2])
                    for r in range(TURNS):
                        job(h1[:, 0, :], lambda o: o, ACT.Gelu, b1[:, 0:1])
                        job(h1[:, 1, :], lambda o: o, ACT.Gelu, b1[:, 1:2])
                        job(h2[:], lambda o: o, ACT.Gelu, b2[:])
                        job(h3[:], lambda o: o[0:H3, :], ACT.Gelu, b3[:])
                        job(tf[:], lambda o: o, ACT.Sigmoid, sc[:, 0:1])

            @block.vector
            def _(dve):
                dve.wait_ge(w_in, 16 * len(loads))
                dve.wait_ge(made, 4)
                dve.tensor_copy(w4b[:], w4[:].broadcast_to([H3, P])).then_inc(sc_s, 1)
                dve.wait_ge(sc_full, 1)
                dve.tensor_copy(sc[:], PS[:, 7, 0:3]).then_inc(sc_s, 1)
                dve.wait_ge(sc_s, 2)
                dve.tensor_scalar(slope[:], sc[:, 2:3], 0.6, None, ALU.mult).then_inc(sc_s, 1)
                dve.wait_ge(sc_s, 3)
                with dve.Fori(0, B) as b:
                    ch = Chain(dve, ch_s, b * N_CH)
                    V.wait_turns(dve, b)
                    split_wait(dve, K["passed"])
                    src = lambda k: X[:, ds(b * QT + k, 1), :]
                    for k in range(QT):
                        ch.mark(dve.bn_stats(st[:, k, :], src(k)))
                    ch.wait()
                    split_wait(dve, K["passed"])
                    for k in range(QT):
                        ins = dve.bn_aggr(mv[:, k, :], st[:, k, :])
                        if k < QT - 1:
                            ch.mark(ins)
                    ins.then_inc(mv_s, 1)
                    dve.wait_ge(mv_s, b + 1)
                    dve.wait_ge(std_s, b + 1)
                    ln_apply(dve, ch, src, mv, std, rstd, xn, xn_s)
                    V.wait_full(dve, b, 0)
                    dve.tensor_copy(y[:, 1, :], V.bank(0)).then_inc(V.free, 1)
                    A.wait_done(dve, b, 0)
                    V.wait_done(dve, b, 0)
                    ch.mark(dve.tensor_reduce(mean[:, 0:2], y[:], AX.X, ALU.add))
                    ch.wait()
                    dve.tensor_scalar(mean[:], mean[:], 1.0 / S, None, ALU.mult).then_inc(mean_s, 1)
                    A.wait_done(dve, b, 2)
                    dve.tensor_copy(g2b[:], g2[:].broadcast_to([H3, P])).then_inc(g2b_s, 1)
                    A.wait_done(dve, b, 3)
                    ch.mark(dve.tensor_scalar(off[:, 0:1], gf[:], 1.4, -1.0, ALU.mult, ALU.add))
                    ch.wait()
                    ch.mark(dve.tensor_scalar(off[:, 1:2], off[:, 0:1], sc[:, 2:3], 0.1, ALU.mult, ALU.add))
                    ch.wait()
                    for r in range(TURNS):
                        A.wait_done(dve, b, 3 + 5 * (r + 1))
                        ch.mark(dve.tensor_scalar(cp[:], tf[:], slope[:], off[:, 1:2], ALU.mult, ALU.add))
                        ch.wait()
                        for f in range(DT):
                            ch.mark(dve.scalar_tensor_tensor(out=tw[:, f, :], in0=y[:, 1 - f, :], scalar=sign[:, f:f + 1],
                                                             in1=cp[:], op0=ALU.mult, op1=ALU.mult))
                        ch.wait()
                        for f in range(DT):
                            dve.tensor_tensor(y[:, f, :], y[:, f, :], tw[:, f, :], ALU.add).then_inc(y_s, 1)
                        dve.wait_ge(y_s, b * TURNS * DT + DT * (r + 1))
                    for q in range(QT):
                        V.wait_full(dve, b, 1 + q)
                        x = X[:, ds(b * QT + q, 1), :]
                        dve.tensor_tensor(x, x, V.bank(1 + q)[:, None, 0:D], ALU.add).then_inc(V.free, 1)
                    assert ch.n == N_CH, ch.n


def head_attention(K, name, scale, biased, masked):
    nc, t, sb, sem, PS, X, ctxT = (K[n] for n in ("nc", "t", "sb", "sem", "PS", "X", "ctxT"))
    ident, identb, ones, eps = K["ident"], K["identb"], K["ones"], K["eps"]
    HD = D // H
    G = H // 4
    TERMS = ((0, 0), (1, 0), (0, 1), (2, 0), (0, 2), (1, 1))
    ROWS = HD * len(TERMS)
    CW = 32
    N_MAX = 4 * QT * 2
    UNITS = 4 * 4
    NE = 8
    N_ACT = 4 + 1 + 2
    V_V, V_XT, V_M = 0, 4, 5
    vjobs = [("v", i) for i in range(4)] + [("xT",)] + [("max", 0, i) for i in range(N_MAX)] + [("neg", 0)]
    for g in range(G):
        for n in range(UNITS):
            if g >= 1 and n == 3:
                vjobs.append(("sum", g - 1))
            if g + 1 < G:
                vjobs += [("max", g + 1, i) for i in range(3 * n, min(3 * n + 3, N_MAX))]
                if n == 12:
                    vjobs.append(("neg", g + 1))
    vjobs += [("sum", G - 1)] + [("y", q) for q in range(QT)]
    N_DVE = len(vjobs)
    vat = {j: i for i, j in enumerate(vjobs)}
    Wt = "%s_xattn_W" % name
    with ExitStack() as c:
        pre = name + "a_"
        wq = sb(c, pre + "wq", [P, DT, D]); wk = sb(c, pre + "wk", [P, DT, D]); wv = sb(c, pre + "wv", [P, DT, D])
        wo = sb(c, pre + "wo", [P, G, D]); sel = sb(c, pre + "sel", [P, P])
        bq = sb(c, pre + "bq", [P, DT]); bk = sb(c, pre + "bk", [P, DT])
        bv = sb(c, pre + "bv", [1, D]); bo = sb(c, pre + "bo", [1, D])
        cb = sb(c, pre + "cb", [P, DT, SK])
        ex = sb(c, pre + "ex", [P, NE, SK])
        exw = ex[:, :, :].rearrange("p e n -> p (e n)")
        kf = exw[:, 0:DT * SK].rearrange("p (k n) -> p k n", k=DT)
        ks = exw[:, 2048:5120].bitcast(BF16).rearrange("p (i k n) -> p i k n", i=3, k=DT)
        qf = exw[:, 5120:6144].rearrange("p (k n) -> p k n", k=DT)
        qs = exw[:, 6144:7680].bitcast(BF16).rearrange("p (i k n) -> p i k n", i=3, k=DT)
        xT = sb(c, pre + "xT", [P, DT, S])
        kst = sb(c, pre + "kst", [P, H, SK], BF16); qst = sb(c, pre + "qst", [P, H, S], BF16)
        v = sb(c, pre + "v", [P, KT, G, 4, CW])
        mx = sb(c, pre + "mx", [P, QT, 4, 2]); nm = sb(c, pre + "nm", [P, QT, 4]); nr = sb(c, pre + "nr", [P, QT, 4])
        nr2 = sb(c, pre + "nr2", [P, QT, 4]); nsp = sb(c, pre + "nsp", [P, QT, 3, 4], BF16); nT = sb(c, pre + "nT", [12, S], BF16)
        osb = sb(c, pre + "osb", [P, 2, S]); rc = sb(c, pre + "rc", [P, S]); aT = sb(c, pre + "aT", [P, G, S])
        kr = aT[:, :, :].rearrange("p g n -> p (g n)").rearrange("p (k n) -> p k n", k=DT)
        qr = osb
        xn = osb[:, :, :].rearrange("p a n -> p (a n)").rearrange("p (q d) -> p q d", q=QT)
        st = sb(c, pre + "st", [P, QT, 6]); mv = sb(c, pre + "mv", [P, QT, 2])
        std = sb(c, pre + "std", [P, QT]); rstd = sb(c, pre + "rstd", [P, QT])
        if masked:
            mraw = exw[:, 0:QT * SK // 4].bitcast(U8).rearrange("p (q n) -> p q n", q=QT)
            biasq = sb(c, pre + "biasq", [P, QT, SK], BF16); biask = sb(c, pre + "biask", [P, KT, S], BF16)
            any_ = sb(c, pre + "any", [P, QT]); anyb = aT[:, 0, :].rearrange("p (q n) -> p q n", q=QT)
            flag = sb(c, pre + "flag", [P, S])
        qdram = nc.dram_tensor(pre + "q_parts", (3, D, S), BF16, kind="Internal").ap()
        kdram = nc.dram_tensor(pre + "k_parts", (3, D, SK), BF16, kind="Internal").ap()
        names = ("weights_in", "zeroed", "constants_made", "dve_chain", "pool_chain", "std_ready", "var_ready", "xn_ready",
                 "ctx_copied", "k_split", "q_split", "k_stored", "q_stored", "k_stacked", "q_stacked", "neg_ready",
                 "neg_turned", "neg_in", "scores_full", "exp_done", "pv_done", "attention_ready", "max_ready",
                 "mask_full", "mask_done")
        (w_in, zeroed, made, ch_s, pc_s, std_s, mv_s, xn_s, cb_s, ksp_s, qsp_s, kst_s, qst_s, kin_s, qin_s, nr_s,
         nt_s, nin_s, s_full, s_exp, pv_s, at_s, mx_s, mk_full, mk_s) = (sem(pre + n) for n in names)
        A = Ring([PS[:, 0, :], PS[:, 1, :]], sem(pre + "act_full"), sem(pre + "act_free"), N_ACT)
        V = Ring([PS[:, 2, :], PS[:, 3, :]], sem(pre + "dve_full"), sem(pre + "dve_free"), N_DVE)
        O = Ring([PS[:, 1, :], PS[:, 0, :]], pv_s, sem(pre + "products_free"), G)
        scores = [PS[:, 4:6, :], PS[:, 6:8, :]]
        loads = [(wq[:], t[Wt + "q"].rearrange("(k p) n -> p k n", p=P)),
                 (wk[:], t[Wt + "k"].rearrange("(k p) n -> p k n", p=P)),
                 (wv[:], t[Wt + "v"].rearrange("(k p) n -> p k n", p=P))]
        loads += [(wo[32 * j:32 * j + HD, :, :], t[Wt + "o"].rearrange("(g j d) n -> j d g n", j=4, d=HD)[j]) for j in range(4)]
        if biased:
            loads += [(bq[:], t["L1_xattn_bq_cols"]), (bk[:], t["L1_xattn_bk_cols"]),
                      (bv[:], t["L1_xattn_bv"].rearrange("(a n) -> a n", a=1)),
                      (bo[:], t["L1_xattn_bo"].rearrange("(a n) -> a n", a=1))]
        if masked:
            loads += [(mraw[:], t["mask_SxS2_bk0"].rearrange("(k p) n -> p k n", p=P))]
        N_CH = 2 * QT - 1 + 1 + 1 + 4 * G + (2 if masked else 1) * G
        with nc.Block() as block:
            @block.sync
            def _(sp):
                sp.wait_ge(zeroed, 2)
                for dst, src in loads:
                    sp.dma_start(dst, src).then_inc(w_in, 16)
                with sp.Fori(0, B) as b:
                    V.wait_turns(sp, b)
                    sp.wait_ge(ksp_s, 3 * b + 3)
                    for i in range(3):
                        sp.dma_start(kdram[i].rearrange("(m p) n -> p m n", p=P), ks[:, i, :, :]).then_inc(kst_s, 16)
                    sp.wait_ge(kst_s, 48 * b + 48)
                    for r, (_, i) in enumerate(TERMS):
                        sp.dma_start(kst[HD * r:HD * (r + 1), :, :],
                                     kdram[i].rearrange("(h d) n -> d h n", d=HD)).then_inc(kin_s, 16)
                    sp.wait_ge(qsp_s, 3 * b + 3)
                    for i in range(3):
                        sp.dma_start(qdram[i].rearrange("(m p) n -> p m n", p=P), qs[:, i, :, :]).then_inc(qst_s, 16)
                    sp.wait_ge(qst_s, 48 * b + 48)
                    for r, (i, _) in enumerate(TERMS):
                        sp.dma_start(qst[HD * r:HD * (r + 1), :, :],
                                     qdram[i].rearrange("(h d) n -> d h n", d=HD)).then_inc(qin_s, 16)
                    for g in range(G):
                        sp.wait_ge(nt_s, b * G + g + 1)
                        for i in range(3):
                            sp.dma_start(qst[ROWS + i:ROWS + i + 1, 4 * g:4 * g + 4, :],
                                         nT[4 * i:4 * i + 4, :]).then_inc(nin_s, 16)

            @block.gpsimd
            def _(pool):
                A.start(pool)
                V.start(pool)
                O.start(pool)
                pool.memset(wo[:], 0.0).then_inc(zeroed, 1)
                pool.memset(v[:], 0.0).then_inc(zeroed, 1)
                pool.wait_ge(zeroed, 2)
                pool.memset(kst[ROWS:P, :, :], 1.0).then_inc(made, 1)
                pool.wait_ge(made, 1)
                pool.memset(v[:, :, :, :, HD:HD + 1], 1.0).then_inc(made, 1)
                sv = sel[:].rearrange("p (j c) -> p j c", c=CW)
                pool.affine_select(out=sv, in_=ones[:].rearrange("p (j c) -> p j c", c=CW), compare_op=ALU.is_equal,
                                   fill=0.0, base=-HD, pattern=[[-CW, 4], [0, CW]], channel_multiplier=1).then_inc(made, 1)
                with pool.Fori(0, B) as b:
                    ch = Chain(pool, pc_s, b)
                    V.wait_turns(pool, b)
                    for f in range(DT):
                        pool.tensor_copy(cb[:, f, :], ctxT[:, f, ds(b * SK, SK)]).then_inc(cb_s, 1)
                    A.wait_done(pool, b, 3)
                    split_wait(pool, K["passed"])
                    pool.tensor_copy(ks[:, 0, :, :], kf[:]).then_inc(ksp_s, 1)
                    pool.wait_ge(ksp_s, 3 * b + 1)
                    ch.mark(pool.tensor_tensor(kr[:], kf[:], ks[:, 0, :, :], ALU.subtract))
                    ch.wait()
                    split_wait(pool, K["passed"])
                    pool.tensor_copy(ks[:, 1, :, :], kr[:]).then_inc(ksp_s, 1)
                    pool.wait_ge(ksp_s, 3 * b + 2)
                    pool.tensor_tensor(ks[:, 2, :, :], kr[:], ks[:, 1, :, :], ALU.subtract).then_inc(ksp_s, 1)

            @block.tensor
            def _(pe):
                pe.wait_ge(w_in, 16 * len(loads))
                pe.wait_ge(made, 3)
                if masked:
                    for kt in range(KT):
                        pe.wait_ge(mk_s, 2 if kt < 4 else kt - 1)
                        bank = PS[:, kt % 4, :].bitcast(BF16)
                        for q in range(QT):
                            mm = pe.transpose(bank[:, q * P:(q + 1) * P], biasq[:, q, kt * P:(kt + 1) * P], identb[:])
                        mm.then_inc(mk_full, 1)
                    pe.wait_ge(mk_s, 2 + KT)
                    pe.wait_ge(mk_s, 2 + KT + 1)
                    for q in range(QT):
                        mm = pe.matmul(PS[:, 4, q * P:(q + 1) * P], anyb[:, q, :], ident[:], start=True, stop=True,
                                       skip_group_check=True)
                    mm.then_inc(mk_full, 1)
                with pe.Fori(0, B) as b:
                    V.wait_turns(pe, b)
                    pe.wait_ge(cb_s, b * DT + DT)
                    for m in range(DT):
                        for n in range(2):
                            i = 2 * m + n
                            A.wait_free(pe, b, i)
                            for k in range(DT):
                                mm = pe.matmul(A.bank(i), wk[:, k, m * P:(m + 1) * P], cb[:, k, n * 512:(n + 1) * 512],
                                               start=(k == 0), stop=(k == DT - 1))
                            mm.then_inc(A.full, 1)
                    for i in range(4):
                        V.wait_free(pe, b, i)
                        for u in range(2):
                            o = V.bank(i)[:, u * D:(u + 1) * D]
                            for k in range(DT):
                                mm = pe.matmul(o, cb[:, k, (2 * i + u) * P:(2 * i + u + 1) * P], wv[:, k, :],
                                               start=(k == 0), stop=(k == DT - 1 and not biased), skip_group_check=True)
                            if biased:
                                mm = pe.matmul(o, ones[0:1, :], bv[:], start=False, stop=True, skip_group_check=True)
                        mm.then_inc(V.full, 1)
                    pe.wait_ge(xn_s, b * QT + QT)
                    for f, (R, i) in enumerate(((A, 4), (V, V_XT))):
                        R.wait_free(pe, b, i)
                        for k in range(QT):
                            mm = pe.transpose(R.bank(i)[:, k * P:(k + 1) * P], xn[:, k, f * P:(f + 1) * P], ident[:])
                        mm.then_inc(R.full, 1)
                    A.wait_done(pe, b, 4)
                    V.wait_done(pe, b, V_XT)
                    for m in range(DT):
                        A.wait_free(pe, b, 5 + m)
                        for k in range(DT):
                            mm = pe.matmul(A.bank(5 + m), wq[:, k, m * P:(m + 1) * P], xT[:, k, :],
                                           start=(k == 0), stop=(k == DT - 1))
                        mm.then_inc(A.full, 1)

                    def fill_max(g, i):
                        h, q, n = 4 * g + i // (2 * QT), i // 2 % QT, i % 2
                        at = vat["max", g, i]
                        V.wait_free(pe, b, at)
                        pe.matmul(V.bank(at), qst[0:ROWS, h, q * P:(q + 1) * P], kst[0:ROWS, h, n * 512:(n + 1) * 512],
                                  start=True, stop=True).then_inc(V.full, 1)

                    def fill_neg(g):
                        at = vat["neg", g]
                        V.wait_free(pe, b, at)
                        pe.wait_ge(nr_s, b * G + g + 1)
                        o = V.bank(at).bitcast(BF16)
                        for q in range(QT):
                            mm = pe.transpose(o[0:12, q * P:(q + 1) * P], nsp[:, q, :, :].rearrange("p i j -> p (i j)"), identb[:])
                        mm.then_inc(V.full, 1)

                    def fill_sum(g):
                        at = vat["sum", g]
                        V.wait_free(pe, b, at)
                        O.wait_done(pe, b, g)
                        pe.matmul(V.bank(at), sel[:], osb[:, g % 2, :], start=True, stop=True).then_inc(V.full, 1)

                    def scores_of(g, n):
                        u, j = n // 4, n % 4
                        h, at = 4 * g + j, g * UNITS + n
                        if at >= 2:
                            pe.wait_ge(s_exp, b * G * UNITS + at - 1)
                        for kk in range(2):
                            kt = 2 * u + kk
                            mm = pe.matmul(scores[at % 2][:, kk, :], kst[0:ROWS + 3, h, kt * P:(kt + 1) * P],
                                           qst[0:ROWS + 3, h, :], start=True, stop=not masked)
                            if masked:
                                mm = pe.matmul(scores[at % 2][:, kk, :], identb[:], biask[:, kt, :], start=False, stop=True)
                        mm.then_inc(s_full, 1)

                    def products(g, u):
                        if u == 0:
                            O.wait_free(pe, b, g)
                        pe.wait_ge(s_exp, b * G * UNITS + g * UNITS + 4 * u + 4)
                        for kk in range(2):
                            for j in range(4):
                                kt = 2 * u + kk
                                mm = pe.matmul(O.bank(g)[32 * j:32 * j + CW, :], v[:, kt, g, j, :],
                                               ex[:, (4 * u + j) % NE, kk * 512:(kk + 1) * 512],
                                               start=(kt == 0), stop=(kt == KT - 1), skip_group_check=True)
                        mm.then_inc(pv_s, 1)

                    A.wait_done(pe, b, 6)
                    pe.wait_ge(kin_s, 16 * 6 * (b + 1))
                    pe.wait_ge(qin_s, 16 * 6 * (b + 1))
                    for i in range(N_MAX):
                        fill_max(0, i)
                    fill_neg(0)
                    for g in range(G):
                        pe.wait_ge(nin_s, 48 * (b * G + g + 1))
                        for n in range(UNITS):
                            scores_of(g, n)
                            if g >= 1 and n == 3:
                                fill_sum(g - 1)
                            if g + 1 < G:
                                for i in range(3 * n, min(3 * n + 3, N_MAX)):
                                    fill_max(g + 1, i)
                                if n == 12:
                                    fill_neg(g + 1)
                            if n % 4 == 3 and n >= 7:
                                products(g, n // 4 - 1)
                        products(g, 3)
                    fill_sum(G - 1)
                    pe.wait_ge(at_s, b * G + G)
                    for q in range(QT):
                        at = vat["y", q]
                        V.wait_free(pe, b, at)
                        for g in range(G):
                            mm = pe.matmul(V.bank(at)[:, 0:D], aT[:, g, q * P:(q + 1) * P], wo[:, g, :],
                                           start=(g == 0), stop=(g == G - 1 and not biased))
                        if biased:
                            mm = pe.matmul(V.bank(at)[:, 0:D], ones[0:1, :], bo[:], start=False, stop=True)
                        mm.then_inc(V.full, 1)

            @block.scalar
            def _(act):
                act.wait_ge(w_in, 16 * len(loads))
                with act.Fori(0, B) as b:
                    V.wait_turns(act, b)
                    act.wait_ge(mv_s, b + 1)
                    act.activation(std[:], mv[:, :, 1], ACT.Sqrt, bias=eps[:]).then_inc(std_s, 1)
                    for m in range(DT):
                        for n in range(2):
                            A.wait_full(act, b, 2 * m + n)
                            act.activation(kf[:, m, n * 512:(n + 1) * 512], A.bank(2 * m + n), ACT.Identity,
                                           bias=bk[:, m:m + 1] if biased else 0.0).then_inc(A.free, 1)
                    A.wait_full(act, b, 4)
                    act.copy(xT[:, 0, :], A.bank(4)).then_inc(A.free, 1)
                    for m in range(DT):
                        A.wait_full(act, b, 5 + m)
                        act.activation(qf[:, m, :], A.bank(5 + m), ACT.Identity,
                                       bias=bq[:, m:m + 1] if biased else 0.0).then_inc(A.free, 1)

                    def take(g):
                        act.wait_ge(pv_s, 4 * (b * G + g + 1))
                        act.copy(osb[:, g % 2, :], O.bank(g)).then_inc(O.free, 1)

                    for g in range(G):
                        for n in range(UNITS):
                            at = g * UNITS + n
                            act.wait_ge(s_full, b * G * UNITS + at + 1)
                            if at >= NE:
                                act.wait_ge(pv_s, b * 4 * G + (at - NE) // 4 + 1)
                            act.activation(ex[:, n % NE, :], scores[at % 2], ACT.Exp, scale=scale).then_inc(s_exp, 1)
                            if g >= 1 and n == 1:
                                if g >= 3:
                                    act.wait_ge(at_s, b * G + g - 2)
                                take(g - 1)
                    take(G - 1)

            @block.vector
            def _(dve):
                if masked:
                    dve.wait_ge(w_in, 16 * len(loads))
                    dve.tensor_scalar(biasq[:], mraw[:], BIG, -BIG, ALU.mult, ALU.add).then_inc(mk_s, 1)
                    dve.tensor_reduce(any_[:], mraw[:], AX.X, ALU.max).then_inc(mk_s, 1)
                    for kt in range(KT):
                        dve.wait_ge(mk_full, kt + 1)
                        dve.tensor_copy(biask[:, kt, :], PS[:, kt % 4, :].bitcast(BF16)[:, 0:S]).then_inc(mk_s, 1)
                    dve.wait_ge(mk_s, 2 + KT)
                    dve.tensor_copy(anyb[:], any_[:, :, None].broadcast_to([P, QT, P])).then_inc(mk_s, 1)
                    dve.wait_ge(mk_full, KT + 1)
                    dve.tensor_copy(flag[:], PS[:, 4, :]).then_inc(mk_s, 1)
                    dve.wait_ge(mk_s, 2 + KT + 2)
                with dve.Fori(0, B) as b:
                    ch = Chain(dve, ch_s, b * N_CH)
                    V.wait_turns(dve, b)
                    split_wait(dve, K["passed"])
                    src = lambda k: X[:, ds(b * QT + k, 1), :]
                    for k in range(QT):
                        ch.mark(dve.bn_stats(st[:, k, :], src(k)))
                    ch.wait()
                    split_wait(dve, K["passed"])
                    for k in range(QT):
                        ins = dve.bn_aggr(mv[:, k, :], st[:, k, :])
                        if k < QT - 1:
                            ch.mark(ins)
                    ins.then_inc(mv_s, 1)
                    dve.wait_ge(mv_s, b + 1)
                    dve.wait_ge(std_s, b + 1)
                    ln_apply(dve, ch, src, mv, std, rstd, xn, xn_s)
                    for at, job in enumerate(vjobs):
                        if job[0] == "max" and job[2] == 0 and job[1] == 0:
                            A.wait_done(dve, b, 6)
                            dve.tensor_copy(qs[:, 0, :, :], qf[:]).then_inc(qsp_s, 1)
                            dve.wait_ge(qsp_s, 3 * b + 1)
                            ch.mark(dve.tensor_tensor(qr[:], qf[:], qs[:, 0, :, :], ALU.subtract))
                            ch.wait()
                            dve.tensor_copy(qs[:, 1, :, :], qr[:]).then_inc(qsp_s, 1)
                            dve.wait_ge(qsp_s, 3 * b + 2)
                            dve.tensor_tensor(qs[:, 2, :, :], qr[:], qs[:, 1, :, :], ALU.subtract).then_inc(qsp_s, 1)
                        if job[0] == "neg":
                            g = job[1]
                            V.wait_done(dve, b, at - 1)
                            ch.mark(dve.tensor_reduce(nm[:], mx[:], AX.X, ALU.max, negate=True))
                            ch.wait()
                            ch.mark(dve.tensor_copy(nsp[:, :, 0, :], nm[:]))
                            ch.wait()
                            ch.mark(dve.tensor_tensor(nr[:], nm[:], nsp[:, :, 0, :], ALU.subtract))
                            ch.wait()
                            ch.mark(dve.tensor_copy(nsp[:, :, 1, :], nr[:]))
                            ch.wait()
                            dve.tensor_tensor(nsp[:, :, 2, :], nr[:], nsp[:, :, 1, :], ALU.subtract).then_inc(nr_s, 1)
                        V.wait_full(dve, b, at)
                        o = V.bank(at)
                        if job[0] == "v":
                            for u in range(2):
                                ins = dve.tensor_copy(v[:, 2 * job[1] + u, :, :, 0:HD],
                                                      o[:, u * D:(u + 1) * D].rearrange("p (g j d) -> p g j d", g=G, j=4))
                            ins.then_inc(V.free, 1)
                        elif job[0] == "xT":
                            dve.tensor_copy(xT[:, 1, :], o).then_inc(V.free, 1)
                        elif job[0] == "max":
                            i = job[2]
                            j, q, n = i // (2 * QT), i // 2 % QT, i % 2
                            if masked:
                                split_wait(dve, K["passed"])
                                dve.tensor_tensor_reduce(o, o, biasq[:, q, n * 512:(n + 1) * 512], 1.0, -3e38,
                                                         ALU.add, ALU.max, mx[:, q, j, n:n + 1]).then_inc(V.free, 1)
                            else:
                                dve.reduce_max(mx[:, q, j, n:n + 1], o, AX.X).then_inc(V.free, 1)
                        elif job[0] == "neg":
                            if job[1]:
                                dve.wait_ge(nin_s, 48 * (b * G + job[1]))
                            dve.tensor_copy(nT[:], o.bitcast(BF16)[0:12, 0:S]).then_inc(nt_s, 1)
                            dve.wait_ge(nt_s, b * G + job[1] + 1)
                            dve.sem_inc(V.free, 1)
                        elif job[0] == "sum":
                            g = job[1]
                            if g:
                                dve.wait_ge(at_s, b * G + g)
                            ch.mark(dve.reciprocal(rc[:], o))
                            ch.wait()
                            dve.sem_inc(V.free, 1)
                            if masked:
                                ch.mark(dve.tensor_tensor(rc[:], rc[:], flag[:], ALU.mult))
                                ch.wait()
                            dve.tensor_tensor(aT[:, g, :], osb[:, g % 2, :], rc[:], ALU.mult).then_inc(at_s, 1)
                        else:
                            x = X[:, ds(b * QT + job[1], 1), :]
                            dve.tensor_tensor(x, x, o[:, None, 0:D], ALU.add).then_inc(V.free, 1)
                    assert ch.n == N_CH, ch.n


def experts(K, name, act_fn, by_expert):
    nc, t, sb, sem, PS, X = (K[n] for n in ("nc", "t", "sb", "sem", "PS", "X"))
    ident, ones, eps = K["ident"], K["ones"], K["eps"]
    pre = name + "f_"
    names = {"L1": ("L1_ffn_router_w", "L1_ffn_w1", "L1_ffn_b1", "L1_ffn_w2", "L1_ffn_b2"),
             "L2": ("L2_ffn_gate_w", "L2_ffn_fc1s", "L2_ffn_b1s", "L2_ffn_fc2s", "L2_ffn_b2s"),
             "L3": ("L3_ffn_router_w", "L3_ffn_expert_w1", "L3_ffn_expert_b1", "L3_ffn_expert_w2", "L3_ffn_expert_b2")}[name]
    t_r, t_w1, t_b1, t_w2, t_b2 = (t[n] for n in names)
    t_b1c = t[names[2] + "_cols"]
    with ExitStack() as c:
        yT = sb(c, pre + "yT", [P, DT, NT * P])
        gate = sb(c, pre + "gate", [P, NT, E])
        route(K, name, pre, t_r, yT, gate, by_expert)
        if by_expert:
            choose_tokens(K, pre, gate)
        w1 = sb(c, pre + "w1", [P, 2, DT, F]); w2 = sb(c, pre + "w2", [P, 2, FT, D])
        b1 = sb(c, pre + "b1", [P, 2, FT]); b2 = sb(c, pre + "b2", [1, 2, D])
        hT = sb(c, pre + "hT", [P, 2, FT, S])
        N_A, N_V = 2 * B * FT, 2 * B * QT
        A = Ring([PS[:, i, :] for i in range(4)], sem(pre + "act_full"), sem(pre + "act_free"), N_A)
        V = Ring([PS[:, i, :] for i in range(4, 8)], sem(pre + "dve_full"), sem(pre + "dve_free"), N_V)
        w_in = [sem(pre + "weights_in%d" % i) for i in range(2)]
        with nc.Block() as block:
            @block.sync
            def _(sp):
                with sp.Fori(0, E // 2) as i:
                    for e in range(2):
                        V.wait_turns(sp, i)
                        x = i * 2 + e
                        for dst, src in ((w1[:, e, :, :], t_w1[ds(x, 1)].rearrange("a (k p) n -> p (a k) n", p=P)),
                                         (w2[:, e, :, :], t_w2[ds(x, 1)].rearrange("a (k p) n -> p (a k) n", p=P)),
                                         (b1[:, e, :], t_b1c[ds(x, 1)].rearrange("a p k -> p (a k)")),
                                         (b2[:, e, :], t_b2[ds(x, 1)])):
                            sp.dma_start(dst, src).then_inc(w_in[e], 16)

            @block.gpsimd
            def _(pool):
                A.start(pool)
                V.start(pool)

            @block.tensor
            def _(pe):
                with pe.Fori(0, E // 2) as i:
                    V.wait_turns(pe, i)

                    def hidden(e, g):
                        for m in range(FT):
                            at = (B * e + g) * FT + m
                            A.wait_free(pe, i, at)
                            for k in range(DT):
                                mm = pe.matmul(A.bank(at), w1[:, e, k, m * P:(m + 1) * P], yT[:, k, g * S:(g + 1) * S],
                                               start=(k == 0), stop=(k == DT - 1))
                            mm.then_inc(A.full, 1)

                    def outward(e, g):
                        A.wait_done(pe, i, (B * e + g) * FT + FT - 1)
                        for q in range(QT):
                            at = (B * e + g) * QT + q
                            V.wait_free(pe, i, at)
                            o = V.bank(at)[:, 0:D]
                            for k in range(FT):
                                pe.matmul(o, hT[:, g % 2, k, q * P:(q + 1) * P], w2[:, e, k, :], start=(k == 0), stop=False)
                            pe.matmul(o, ones[0:1, :], b2[:, e, :], start=False, stop=True).then_inc(V.full, 1)

                    steps = [(e, g) for e in range(2) for g in range(B)]
                    for n, (e, g) in enumerate(steps):
                        if g == 0:
                            pe.wait_ge(w_in[e], i * 64 + 64)
                        hidden(e, g)
                        if n:
                            outward(*steps[n - 1])
                    outward(*steps[-1])

            @block.scalar
            def _(act):
                with act.Fori(0, E // 2) as i:
                    for e in range(2):
                        act.wait_ge(w_in[e], i * 64 + 64)
                        for g in range(B):
                            if B * e + g >= 2:
                                V.wait_done(act, i, (B * e + g - 1) * QT - 1)
                            for m in range(FT):
                                at = (B * e + g) * FT + m
                                A.wait_full(act, i, at)
                                act.activation(hT[:, g % 2, m, :], A.bank(at), act_fn, bias=b1[:, e, m:m + 1]).then_inc(A.free, 1)

            @block.vector
            def _(dve):
                with dve.Fori(0, E // 2) as i:
                    for e in range(2):
                        for q in range(NT):
                            at = e * NT + q
                            V.wait_full(dve, i, at)
                            if e:
                                V.wait_done(dve, i, at - NT)
                            dve.scalar_tensor_tensor(out=X[:, q, :], in0=V.bank(at)[:, 0:D], scalar=gate[:, q, ds(i * 2 + e, 1)],
                                                     in1=X[:, q, :], op0=ALU.mult, op1=ALU.add).then_inc(V.free, 1)


def route(K, name, pre, t_r, yT, gate, by_expert):
    nc, t, sb, sem, PS, X = (K[n] for n in ("nc", "t", "sb", "sem", "PS", "X"))
    ident, eps = K["ident"], K["eps"]
    with ExitStack() as c:
        rw = sb(c, pre + "rw", [P, DT, E])
        xn = sb(c, pre + "xn", [P, QT, D]); xT = sb(c, pre + "xT", [P, DT, S])
        st = sb(c, pre + "st", [P, QT, 6]); mv = sb(c, pre + "mv", [P, QT, 2])
        std = sb(c, pre + "std", [P, QT]); rstd = sb(c, pre + "rstd", [P, QT])
        lg = sb(c, pre + "lg", [P, QT, E]); lm = sb(c, pre + "lm", [P, QT]); le = sb(c, pre + "le", [P, QT, E])
        ls = sb(c, pre + "ls", [P, QT]); pb = sb(c, pre + "pb", [P, QT, E])
        gt = sb(c, pre + "gt", [P, QT, E, E]); eq = sb(c, pre + "eq", [P, QT, E, E]); first = sb(c, pre + "first", [P, QT, E, E])
        rank = sb(c, pre + "rank", [P, QT, E])
        if by_expert:
            lnw = sb(c, pre + "lnw", [P, DT]); lnb = sb(c, pre + "lnb", [P, DT])
            st2 = sb(c, pre + "st2", [P, QT, 6]); mv2 = sb(c, pre + "mv2", [P, QT, 2])
            std2 = sb(c, pre + "std2", [P, QT]); rstd2 = sb(c, pre + "rstd2", [P, QT]); xn2 = sb(c, pre + "xn2", [P, QT, D])
            zT = sb(c, pre + "zT", [P, DT, S])
        w_in, made, ch_s, ch2_s, std_s, mv_s, xn_s, lg_s, le_s, cp_s, end_s, st2_s, xn2_s = (sem(pre + n) for n in (
            "router_in", "order_made", "dve_chain", "dve_chain2", "std_ready", "var_ready", "xn_ready", "logits_shifted", "exp_ready",
            "input_copied", "gates_ready", "std2_ready", "xn2_ready"))
        N_A = 2 if by_expert else 1
        N_V = 3 if by_expert else 2
        A = Ring([PS[:, 0, :], PS[:, 1, :]], sem(pre + "r_act_full"), sem(pre + "r_act_free"), N_A)
        V = Ring([PS[:, 2, :], PS[:, 3, :], PS[:, 4, :]], sem(pre + "r_dve_full"), sem(pre + "r_dve_free"), N_V)
        N_W = 48 if by_expert else 16
        src_T = zT if by_expert else xT
        with nc.Block() as block:
            @block.sync
            def _(sp):
                sp.dma_start(rw[:], t_r.rearrange("(k p) n -> p k n", p=P)).then_inc(w_in, 16)
                if by_expert:
                    sp.dma_start(lnw[:], t["L2_ffn_ln_w_cols"]).then_inc(w_in, 16)
                    sp.dma_start(lnb[:], t["L2_ffn_ln_b_cols"]).then_inc(w_in, 16)

            @block.gpsimd
            def _(pool):
                A.start(pool)
                V.start(pool)
                pool.sem_inc(end_s, 1)
                pool.sem_inc(cp_s, 1)
                pool.memset(eq[:], 1.0).then_inc(made, 1)
                pool.wait_ge(made, 1)
                pool.affine_select(out=first[:], in_=eq[:], compare_op=ALU.is_gt, fill=0.0, base=0,
                                   pattern=[[0, QT], [1, E], [-1, E]], channel_multiplier=0).then_inc(made, 1)
                with pool.Fori(0, B) as b:
                    if by_expert:
                        A.wait_done(pool, b, 1)
                        V.wait_done(pool, b, 2)
                    else:
                        A.wait_done(pool, b, 0)
                        V.wait_done(pool, b, 0)
                    pool.tensor_copy(yT[:, :, ds(b * S, S)], src_T[:]).then_inc(cp_s, 1)
                pool.wait_ge(cp_s, B + 1)

            @block.tensor
            def _(pe):
                pe.wait_ge(w_in, N_W)
                with pe.Fori(0, B) as b:
                    pe.wait_ge(xn_s, b * QT + QT)
                    for f, R in enumerate((A, V)):
                        for k in range(QT):
                            mm = pe.transpose(R.bank(0)[:, k * P:(k + 1) * P], xn[:, k, f * P:(f + 1) * P], ident[:])
                        mm.then_inc(R.full, 1)
                    A.wait_done(pe, b, 0)
                    V.wait_done(pe, b, 0)
                    for q in range(QT):
                        for k in range(DT):
                            mm = pe.matmul(V.bank(1)[:, q * E:(q + 1) * E], xT[:, k, q * P:(q + 1) * P], rw[:, k, :],
                                           start=(k == 0), stop=(k == DT - 1), skip_group_check=True)
                    mm.then_inc(V.full, 1)
                    if by_expert:
                        pe.wait_ge(xn2_s, b * QT + QT)
                        for f, (R, i) in enumerate(((A, 1), (V, 2))):
                            for k in range(QT):
                                mm = pe.transpose(R.bank(i)[:, k * P:(k + 1) * P], xn2[:, k, f * P:(f + 1) * P], ident[:])
                            mm.then_inc(R.full, 1)

            @block.scalar
            def _(act):
                act.wait_ge(w_in, N_W)
                with act.Fori(0, B) as b:
                    act.wait_ge(end_s, b + 1)
                    act.wait_ge(mv_s, b + 1)
                    act.activation(std[:], mv[:, :, 1], ACT.Sqrt, bias=eps[:]).then_inc(std_s, 1)
                    A.wait_full(act, b, 0)
                    if not by_expert:
                        act.wait_ge(cp_s, b + 1)
                    act.copy(xT[:, 0, :], A.bank(0)).then_inc(A.free, 1)
                    if by_expert:
                        act.wait_ge(st2_s, 2 * b + 1)
                        act.activation(std2[:], mv2[:, :, 1], ACT.Sqrt, bias=eps[:]).then_inc(st2_s, 1)
                    act.wait_ge(lg_s, b + 1)
                    act.activation(le[:], lg[:], ACT.Exp).then_inc(le_s, 1)
                    if by_expert:
                        A.wait_full(act, b, 1)
                        act.wait_ge(cp_s, b + 1)
                        act.activation(zT[:, 0, :], A.bank(1), ACT.Identity, scale=lnw[:, 0:1], bias=lnb[:, 0:1]).then_inc(A.free, 1)

            @block.vector
            def _(dve):
                dve.wait_ge(made, 2)
                dve.wait_ge(w_in, N_W)
                N_CH = 2 * QT - 1 + 1 + 1 + 2 + (2 * QT - 1 + 1 + QT if by_expert else 10)
                with dve.Fori(0, B) as b:
                    ch = Chain(dve, ch_s, b * N_CH)
                    dve.wait_ge(end_s, b + 1)
                    split_wait(dve, K["passed"])
                    src = lambda k: X[:, ds(b * QT + k, 1), :]
                    for k in range(QT):
                        ch.mark(dve.bn_stats(st[:, k, :], src(k)))
                    ch.wait()
                    split_wait(dve, K["passed"])
                    for k in range(QT):
                        ins = dve.bn_aggr(mv[:, k, :], st[:, k, :])
                        if k < QT - 1:
                            ch.mark(ins)
                    ins.then_inc(mv_s, 1)
                    dve.wait_ge(mv_s, b + 1)
                    dve.wait_ge(std_s, b + 1)
                    ln_apply(dve, ch, src, mv, std, rstd, xn, xn_s)
                    if by_expert:
                        dve.wait_ge(xn_s, b * QT + QT)
                        split_wait(dve, K["passed"])
                        for k in range(QT):
                            ch.mark(dve.bn_stats(st2[:, k, :], xn[:, k, :]))
                        ch.wait()
                        split_wait(dve, K["passed"])
                        for k in range(QT):
                            ins = dve.bn_aggr(mv2[:, k, :], st2[:, k, :])
                            if k < QT - 1:
                                ch.mark(ins)
                        ins.then_inc(st2_s, 1)
                        dve.wait_ge(st2_s, 2 * b + 2)
                        ch.mark(dve.reciprocal(rstd2[:], std2[:]))
                        ch.wait()
                        for k in range(QT):
                            dve.tensor_scalar(xn2[:, k, :], xn[:, k, :], mv2[:, k, 0:1], rstd2[:, k:k + 1],
                                              ALU.subtract, ALU.mult).then_inc(xn2_s, 1)
                        for k in range(QT):
                            ch.mark(dve.tensor_tensor(src(k), src(k), xn[:, k:k + 1, :], ALU.add))
                    V.wait_full(dve, b, 0)
                    if not by_expert:
                        dve.wait_ge(cp_s, b + 1)
                    dve.tensor_copy(xT[:, 1, :], V.bank(0)).then_inc(V.free, 1)
                    V.wait_full(dve, b, 1)
                    o = V.bank(1)[:, 0:QT * E].rearrange("p (q e) -> p q e", q=QT)
                    ch.mark(dve.tensor_reduce(lm[:], o, AX.X, ALU.max))
                    ch.wait()
                    dve.tensor_tensor(lg[:], o, lm[:, :, None].broadcast_to([P, QT, E]), ALU.subtract).then_inc(lg_s, 1)
                    dve.wait_ge(lg_s, b + 1)
                    dve.sem_inc(V.free, 1)
                    dve.wait_ge(le_s, b + 1)
                    ch.mark(dve.tensor_reduce(ls[:], le[:], AX.X, ALU.add))
                    ch.wait()
                    ch.mark(dve.reciprocal(ls[:], ls[:]))
                    ch.wait()
                    lb = ls[:, :, None].broadcast_to([P, QT, E])
                    if by_expert:
                        dve.tensor_tensor(gate[:, ds(b * QT, QT), :], le[:], lb, ALU.mult).then_inc(end_s, 1)
                        V.wait_full(dve, b, 2)
                        dve.wait_ge(cp_s, b + 1)
                        dve.tensor_scalar(zT[:, 1, :], V.bank(2), lnw[:, 1:2], lnb[:, 1:2], ALU.mult, ALU.add).then_inc(V.free, 1)
                    else:
                        ch.mark(dve.tensor_tensor(pb[:], le[:], lb, ALU.mult))
                        ch.wait()
                        mine = pb[:, :, :, None].broadcast_to([P, QT, E, E])
                        other = pb[:, :, None, :].broadcast_to([P, QT, E, E])
                        ch.mark(dve.tensor_tensor(gt[:], other, mine, ALU.is_gt))
                        ch.mark(dve.tensor_tensor(eq[:], other, mine, ALU.is_equal))
                        ch.wait()
                        ch.mark(dve.tensor_tensor(eq[:], eq[:], first[:], ALU.mult))
                        ch.wait()
                        ch.mark(dve.tensor_tensor(gt[:], gt[:], eq[:], ALU.add))
                        ch.wait()
                        ch.mark(dve.tensor_reduce(rank[:], gt[:], AX.X, ALU.add))
                        ch.wait()
                        ch.mark(dve.scalar_tensor_tensor(out=pb[:], in0=rank[:], scalar=1.5, in1=pb[:], op0=ALU.is_lt, op1=ALU.mult))
                        ch.wait()
                        ch.mark(dve.tensor_reduce(lm[:], pb[:], AX.X, ALU.add))
                        ch.wait()
                        ch.mark(dve.tensor_scalar(lm[:], lm[:], 1e-9, None, ALU.add))
                        ch.wait()
                        ch.mark(dve.reciprocal(ls[:], lm[:]))
                        ch.wait()
                        dve.tensor_tensor(gate[:, ds(b * QT, QT), :], pb[:], lb, ALU.mult).then_inc(end_s, 1)
                    assert ch.n == N_CH, (ch.n, N_CH)


def choose_tokens(K, pre, gate):
    nc, sb, sem, PS, ones = (K[n] for n in ("nc", "sb", "sem", "PS", "ones"))
    KEEP = NT * P // E
    with ExitStack() as c:
        thr = sb(c, pre + "thr", [P, E]); bit = sb(c, pre + "bit", [P, E], I32); cand = sb(c, pre + "cand", [P, E])
        ge = sb(c, pre + "ge", [P, NT, E]); cnt = sb(c, pre + "cnt", [P, E]); ok = sb(c, pre + "ok", [P, E])
        above = sb(c, pre + "above", [P, NT, E]); tie = sb(c, pre + "tie", [P, NT, E]); need = sb(c, pre + "need", [P, E])
        seen = sb(c, pre + "seen", [P, NT, E]); tot = sb(c, pre + "tot", [P, NT, E]); low = sb(c, pre + "low", [P, P])
        ch_s, cnt_s, sum_s, made = (sem(pre + n) for n in ("c_chain", "count_ready", "count_summed", "c_made"))
        BITS = 30
        PER = 6
        with nc.Block() as block:
            @block.gpsimd
            def _(pool):
                pool.affine_select(out=low[:], in_=ones[:], compare_op=ALU.is_gt, fill=0.0, base=0,
                                   pattern=[[1, P]], channel_multiplier=-1).then_inc(made, 1)

            @block.tensor
            def _(pe):
                with pe.Fori(0, BITS) as i:
                    pe.wait_ge(cnt_s, i + 1)
                    pe.matmul(PS[:, 0, 0:E], ones[:], cnt[:], start=True, stop=True).then_inc(sum_s, 1)
                pe.wait_ge(cnt_s, BITS + 1)
                pe.matmul(PS[:, 0, 0:E], ones[:], cnt[:], start=True, stop=True).then_inc(sum_s, 1)
                pe.wait_ge(cnt_s, BITS + 2)
                pe.wait_ge(made, 1)
                pe.matmul(PS[:, 1, 0:NT * E], low[:], tie[:].rearrange("p t e -> p (t e)"), start=True, stop=True).then_inc(sum_s, 1)
                pe.matmul(PS[:, 2, 0:NT * E], ones[:], tie[:].rearrange("p t e -> p (t e)"), start=True, stop=True).then_inc(sum_s, 1)

            @block.vector
            def _(dve):
                spread = lambda a: a[:, None, :].broadcast_to([P, NT, E])
                dve.memset(thr[:], 0.0).then_inc(ch_s, 1)
                dve.memset(bit[:], 1 << (BITS - 1)).then_inc(ch_s, 1)
                dve.wait_ge(ch_s, 2)
                with dve.Fori(0, BITS) as i:
                    ch = Chain(dve, ch_s, i * PER + 2)
                    ch.mark(dve.tensor_tensor(cand[:].bitcast(I32), thr[:].bitcast(I32), bit[:], ALU.bitwise_or))
                    ch.wait()
                    ch.mark(dve.tensor_tensor(ge[:], gate[:], spread(cand), ALU.is_ge))
                    ch.mark(dve.tensor_single_scalar(bit[:], bit[:], 1, ALU.logical_shift_right))
                    ch.wait()
                    dve.tensor_reduce(cnt[:], ge[:].rearrange("p t e -> p e t"), AX.X, ALU.add).then_inc(cnt_s, 1)
                    dve.wait_ge(sum_s, i + 1)
                    ch.mark(dve.tensor_scalar(ok[:], PS[:, 0, 0:E], KEEP - 0.5, None, ALU.is_ge))
                    ch.wait()
                    ch.mark(dve.tensor_tensor(cand[:], cand[:], ok[:], ALU.mult))
                    ch.wait()
                    ch.mark(dve.tensor_tensor(thr[:], thr[:], cand[:], ALU.max))
                    ch.wait()
                    assert ch.n == PER, ch.n
                ch = Chain(dve, ch_s, 2 + PER * BITS)
                ch.wait()
                ch.mark(dve.tensor_tensor(above[:], gate[:], spread(thr), ALU.is_gt))
                ch.mark(dve.tensor_tensor(tie[:], gate[:], spread(thr), ALU.is_equal))
                ch.wait()
                dve.tensor_reduce(cnt[:], above[:].rearrange("p t e -> p e t"), AX.X, ALU.add).then_inc(cnt_s, 2)
                dve.wait_ge(sum_s, BITS + 1)
                ch.mark(dve.tensor_scalar(need[:], PS[:, 0, 0:E], -1.0, float(KEEP), ALU.mult, ALU.add))
                dve.wait_ge(sum_s, BITS + 3)
                ch.mark(dve.tensor_copy(tot[:].rearrange("p t e -> p (t e)"), PS[:, 2, 0:NT * E]))
                ch.mark(dve.memset(seen[:, 0, :], 0.0))
                ch.wait()
                for k in range(1, NT):
                    ch.mark(dve.tensor_tensor(seen[:, k, :], seen[:, k - 1, :], tot[:, k - 1, :], ALU.add))
                    ch.wait()
                ch.mark(dve.tensor_tensor(seen[:], seen[:], PS[:, 1, 0:NT * E].rearrange("p (t e) -> p t e", t=NT), ALU.add))
                ch.wait()
                ch.mark(dve.tensor_tensor(seen[:], seen[:], spread(need), ALU.is_lt))
                ch.wait()
                ch.mark(dve.tensor_tensor(tie[:], tie[:], seen[:], ALU.mult))
                ch.wait()
                ch.mark(dve.tensor_tensor(above[:], above[:], tie[:], ALU.add))
                ch.wait()
                ch.mark(dve.tensor_tensor(gate[:], gate[:], above[:], ALU.mult))
                ch.wait()


def causal_attention(K):
    nc, t, sb, sem, PS, X, ctxT = (K[n] for n in ("nc", "t", "sb", "sem", "PS", "X", "ctxT"))
    ident, ones, eps = K["ident"], K["ones"], K["eps"]
    HD = 64
    M = H * HD // P
    SCALE = HD ** -0.5
    pre = "L3a_"
    ajobs = [("k", m) for m in range(M)] + [("xT",)] + [("q", m) for m in range(M)]
    vjobs = [("v", k, n) for k in range(QT) for n in range(2)] + [("xT",)]
    for h in range(H):
        ajobs += [("turn", h, q) for q in (1, 3)]
        vjobs += [("turn", h, q) for q in (0, 2)]
        if h % 2:
            vjobs += [("out", h // 2)]
    vjobs += [("y", q) for q in range(QT)]
    aat = {j: i for i, j in enumerate(ajobs)}
    vat = {j: i for i, j in enumerate(vjobs)}
    with ExitStack() as c:
        wq = sb(c, pre + "wq", [P, DT, H * HD]); wk = sb(c, pre + "wk", [P, DT, H * HD]); wv = sb(c, pre + "wv", [P, DT, H * HD])
        wo = sb(c, pre + "wo", [P, M, D])
        cb = sb(c, pre + "cb", [P, DT, S])
        xn = sb(c, pre + "xn", [P, QT, D]); xT = sb(c, pre + "xT", [P, DT, S])
        qT = sb(c, pre + "qT", [P, M, S]); kT = sb(c, pre + "kT", [P, M, S]); v = sb(c, pre + "v", [P, QT, H * HD])
        keep = sb(c, pre + "keep", [P, S]); padi = sb(c, pre + "padi", [1, S], I32); padf = sb(c, pre + "padf", [1, S])
        bias = sb(c, pre + "bias", [P, QT, S], BF16); seen = sb(c, pre + "seen", [P, QT]); vis = sb(c, pre + "vis", [P, QT, S], BF16)
        causal = sb(c, pre + "causal", [P, QT, S], BF16)
        sm = sb(c, pre + "sm", [P, 4, S]); pT = sb(c, pre + "pT", [P, 2, QT, S])
        nmx = sb(c, pre + "nmx", [P, 4]); mx = sb(c, pre + "mx", [P, 4]); su = sb(c, pre + "su", [P, 4]); rs = sb(c, pre + "rs", [P, 4])
        aT = sb(c, pre + "aT", [P, M, S])
        st = sb(c, pre + "st", [P, QT, 6]); mv = sb(c, pre + "mv", [P, QT, 2])
        std = sb(c, pre + "std", [P, QT]); rstd = sb(c, pre + "rstd", [P, QT])
        (w_in, made, ch_s, std_s, mv_s, xn_s, cb_s, pad_s, padf_s, keep_s, bias_s, s_full, mx_s, s_free, exp_s, pn_s) = (
            sem(pre + n) for n in ("weights_in", "constants_made", "dve_chain", "std_ready", "var_ready", "xn_ready",
                                   "ctx_copied", "pad_in", "pad_ready", "keep_full", "bias_ready", "scores_full",
                                   "max_ready", "scores_read", "exp_done", "probs_scaled"))
        A = Ring([PS[:, 0, :], PS[:, 1, :]], sem(pre + "act_full"), sem(pre + "act_free"), len(ajobs))
        V = Ring([PS[:, 2, :], PS[:, 3, :]], sem(pre + "dve_full"), sem(pre + "dve_free"), len(vjobs))
        scores = [PS[:, 4 + i, :] for i in range(3)]
        keepbank = PS[:, 7, :]
        with nc.Block() as block:
            @block.sync
            def _(sp):
                for dst, src in ((wq, t["L3_xattn_Wq"]), (wk, t["L3_xattn_Wk"]), (wv, t["L3_xattn_Wv"]), (wo, t["L3_xattn_Wo"])):
                    sp.dma_start(dst[:], src.rearrange("(k p) n -> p k n", p=P)).then_inc(w_in, 16)
                with sp.Fori(0, B) as b:
                    V.wait_turns(sp, b)
                    sp.dma_start(padi[:], t["mask_BxS2_if1"][ds(b, 1), 0:S]).then_inc(pad_s, 16)

            @block.gpsimd
            def _(pool):
                A.start(pool)
                V.start(pool)
                pool.memset(vis[:], 1.0).then_inc(made, 1)
                pool.wait_ge(made, 1)
                pool.affine_select(out=causal[:], in_=vis[:], compare_op=ALU.is_ge, fill=0.0, base=0,
                                   pattern=[[P, QT], [-1, S]], channel_multiplier=1).then_inc(made, 1)
                with pool.Fori(0, B) as b:
                    V.wait_turns(pool, b)
                    split_wait(pool, K["passed"])
                    pool.tensor_copy(cb[:], ctxT[:, :, ds(b * SK, S)]).then_inc(cb_s, 1)

            @block.tensor
            def _(pe):
                pe.wait_ge(w_in, 64)
                with pe.Fori(0, B) as b:
                    V.wait_turns(pe, b)
                    pe.wait_ge(cb_s, b + 1)
                    for m in range(M):
                        at = aat["k", m]
                        A.wait_free(pe, b, at)
                        for k in range(DT):
                            mm = pe.matmul(A.bank(at), wk[:, k, m * P:(m + 1) * P], cb[:, k, :], start=(k == 0), stop=(k == DT - 1))
                        mm.then_inc(A.full, 1)
                    pe.wait_ge(padf_s, b + 1)
                    pe.matmul(keepbank, ones[0:1, :], padf[:], start=True, stop=True).then_inc(keep_s, 1)
                    for kt in range(QT):
                        for n in range(2):
                            at = vat["v", kt, n]
                            V.wait_free(pe, b, at)
                            for k in range(DT):
                                mm = pe.matmul(V.bank(at), cb[:, k, kt * P:(kt + 1) * P], wv[:, k, n * 512:(n + 1) * 512],
                                               start=(k == 0), stop=(k == DT - 1))
                            mm.then_inc(V.full, 1)
                    pe.wait_ge(xn_s, b * QT + QT)
                    for f, (R, i) in enumerate(((A, aat["xT",]), (V, vat["xT",]))):
                        R.wait_free(pe, b, i)
                        for k in range(QT):
                            mm = pe.transpose(R.bank(i)[:, k * P:(k + 1) * P], xn[:, k, f * P:(f + 1) * P], ident[:])
                        mm.then_inc(R.full, 1)
                    A.wait_done(pe, b, aat["xT",])
                    V.wait_done(pe, b, vat["xT",])
                    for m in range(M):
                        at = aat["q", m]
                        A.wait_free(pe, b, at)
                        for k in range(DT):
                            mm = pe.matmul(A.bank(at), wq[:, k, m * P:(m + 1) * P], xT[:, k, :], start=(k == 0), stop=(k == DT - 1))
                        mm.then_inc(A.full, 1)
                    A.wait_done(pe, b, aat["q", M - 1])

                    def score(h, q):
                        at = h * QT + q
                        if at >= 3:
                            pe.wait_ge(s_free, b * H * QT + at - 2)
                        p0, n = HD * (h % 2), (q + 1) * P
                        pe.matmul(scores[at % 3][:, 0:n], qT[p0:p0 + HD, h // 2, q * P:(q + 1) * P], kT[p0:p0 + HD, h // 2, 0:n],
                                  start=True, stop=True).then_inc(s_full, 1)

                    def turn(h, q):
                        R, at = (A, aat["turn", h, q]) if q % 2 else (V, vat["turn", h, q])
                        R.wait_free(pe, b, at)
                        pe.wait_ge(pn_s, b * H * QT + h * QT + q + 1)
                        for k in range(q + 1):
                            mm = pe.transpose(R.bank(at)[:, k * P:(k + 1) * P], sm[:, q, k * P:(k + 1) * P], ident[:])
                        mm.then_inc(R.full, 1)

                    def product(h):
                        at = vat["out", h // 2]
                        if h % 2 == 0:
                            V.wait_free(pe, b, at)
                        A.wait_done(pe, b, aat["turn", h, 3])
                        V.wait_done(pe, b, vat["turn", h, 2])
                        p0 = HD * (h % 2)
                        for k in range(QT):
                            mm = pe.matmul(V.bank(at)[p0:p0 + HD, k * P:S], v[:, k, h * HD:(h + 1) * HD],
                                           pT[:, h % 2, k, k * P:S], start=(k == 0), stop=(k == QT - 1), skip_group_check=True)
                        if h % 2:
                            mm.then_inc(V.full, 1)

                    for h in range(H + 1):
                        for q in range(QT):
                            if h < H:
                                score(h, q)
                            if h >= 1:
                                turn(h - 1, q)
                        if h >= 2 and h % 2 == 0:
                            product(h - 2)
                            product(h - 1)
                    for q in range(QT):
                        at = vat["y", q]
                        V.wait_free(pe, b, at)
                        V.wait_done(pe, b, vat["out", M - 1])
                        for m in range(M):
                            mm = pe.matmul(V.bank(at)[:, 0:D], aT[:, m, q * P:(q + 1) * P], wo[:, m, :],
                                           start=(m == 0), stop=(m == M - 1))
                        mm.then_inc(V.full, 1)

            @block.scalar
            def _(act):
                with act.Fori(0, B) as b:
                    V.wait_turns(act, b)
                    act.wait_ge(mv_s, b + 1)
                    act.activation(std[:], mv[:, :, 1], ACT.Sqrt, bias=eps[:]).then_inc(std_s, 1)

                    def empty(job, dst, src=lambda o: o):
                        A.wait_full(act, b, aat[job])
                        act.copy(dst, src(A.bank(aat[job]))).then_inc(A.free, 1)

                    for m in range(M):
                        empty(("k", m), kT[:, m, :])
                    empty(("xT",), xT[:, 0, :])
                    for m in range(M):
                        empty(("q", m), qT[:, m, :])
                    for h in range(H + 1):
                        for q in range(QT):
                            if h < H:
                                n, at = (q + 1) * P, h * QT + q
                                act.wait_ge(mx_s, b * H * QT + at + 1)
                                act.activation(sm[:, q, 0:n], sm[:, q, 0:n], ACT.Exp, bias=nmx[:, q:q + 1], scale=SCALE,
                                               accum_out=su[:, q:q + 1]).then_inc(exp_s, 1)
                            if h >= 1 and q % 2:
                                if h >= 3:
                                    V.wait_done(act, b, vat["out", (h - 3) // 2])
                                empty(("turn", h - 1, q), pT[:, (h - 1) % 2, 0:q + 1, q * P:(q + 1) * P],
                                      lambda o: o[:, 0:(q + 1) * P].rearrange("p (k n) -> p k n", n=P))

            @block.vector
            def _(dve):
                dve.wait_ge(made, 2)
                N_CH = 2 * QT - 1 + 1 + 3 + H * QT * 4
                with dve.Fori(0, B) as b:
                    ch = Chain(dve, ch_s, b * N_CH)
                    V.wait_turns(dve, b)
                    split_wait(dve, K["passed"])
                    src = lambda k: X[:, ds(b * QT + k, 1), :]
                    for k in range(QT):
                        ch.mark(dve.bn_stats(st[:, k, :], src(k)))
                    ch.wait()
                    split_wait(dve, K["passed"])
                    for k in range(QT):
                        ins = dve.bn_aggr(mv[:, k, :], st[:, k, :])
                        if k < QT - 1:
                            ch.mark(ins)
                    ins.then_inc(mv_s, 1)
                    dve.wait_ge(mv_s, b + 1)
                    dve.wait_ge(std_s, b + 1)
                    ln_apply(dve, ch, src, mv, std, rstd, xn, xn_s)
                    dve.wait_ge(pad_s, 16 * b + 16)
                    dve.tensor_scalar(padf[:], padi[:], 0.0, None, ALU.not_equal).then_inc(padf_s, 1)
                    dve.wait_ge(keep_s, b + 1)
                    ch.mark(dve.tensor_copy(keep[:], keepbank))
                    ch.wait()
                    ch.mark(dve.tensor_tensor(vis[:], causal[:], keep[:, None, :].broadcast_to([P, QT, S]), ALU.mult))
                    ch.wait()
                    ch.mark(dve.tensor_reduce(seen[:], vis[:], AX.X, ALU.max))
                    dve.tensor_scalar(bias[:], vis[:], BIG, -BIG, ALU.mult, ALU.add).then_inc(bias_s, 1)

                    def empty(job, dst, src=lambda o: o):
                        V.wait_full(dve, b, vat[job])
                        dve.tensor_copy(dst, src(V.bank(vat[job]))).then_inc(V.free, 1)

                    for k in range(QT):
                        for n in range(2):
                            empty(("v", k, n), v[:, k, n * 512:(n + 1) * 512])
                    empty(("xT",), xT[:, 1, :])
                    dve.wait_ge(bias_s, b + 1)

                    def largest(h, q):
                        n, at = (q + 1) * P, h * QT + q
                        dve.wait_ge(s_full, b * H * QT + at + 1)
                        if h >= 1:
                            (A if q % 2 else V).wait_full(dve, b, (aat if q % 2 else vat)["turn", h - 1, q])
                        split_wait(dve, K["passed"])
                        dve.tensor_tensor_reduce(sm[:, q, 0:n], scores[at % 3][:, 0:n], bias[:, q, 0:n], 1.0, -3e38,
                                                 ALU.add, ALU.max, mx[:, q:q + 1]).then_inc(s_free, 1)
                        dve.wait_ge(s_free, b * H * QT + at + 1)
                        dve.tensor_scalar(nmx[:, q:q + 1], mx[:, q:q + 1], -SCALE, None, ALU.mult).then_inc(mx_s, 1)

                    def scale(h, q):
                        n, at = (q + 1) * P, h * QT + q
                        dve.wait_ge(exp_s, b * H * QT + at + 1)
                        ch.mark(dve.tensor_tensor(rs[:, q:q + 1], su[:, q:q + 1], seen[:, q:q + 1], ALU.mult))
                        ch.wait()
                        ch.mark(dve.reciprocal(rs[:, q:q + 1], rs[:, q:q + 1]))
                        ch.wait()
                        ch.mark(dve.tensor_tensor(rs[:, q:q + 1], rs[:, q:q + 1], seen[:, q:q + 1], ALU.mult))
                        ch.wait()
                        ch.mark(dve.tensor_scalar(sm[:, q, 0:n], sm[:, q, 0:n], rs[:, q:q + 1], None, ALU.mult))
                        ch.wait()
                        dve.sem_inc(pn_s, 1)

                    for h in range(H + 1):
                        for q in range(QT):
                            if h < H:
                                largest(h, q)
                            if h >= 1 and q % 2 == 0:
                                if h >= 3:
                                    V.wait_done(dve, b, vat["out", (h - 3) // 2])
                                empty(("turn", h - 1, q), pT[:, (h - 1) % 2, 0:q + 1, q * P:(q + 1) * P],
                                      lambda o: o[:, 0:(q + 1) * P].rearrange("p (k n) -> p k n", n=P))
                            if h < H:
                                if q >= 1:
                                    scale(h, q - 1)
                        if h < H:
                            scale(h, QT - 1)
                        if h >= 2 and h % 2 == 0:
                            empty(("out", h // 2 - 1), aT[:, h // 2 - 1, :])
                    for q in range(QT):
                        V.wait_full(dve, b, vat["y", q])
                        x = X[:, ds(b * QT + q, 1), :]
                        dve.tensor_tensor(x, x, V.bank(vat["y", q])[:, None, 0:D], ALU.add).then_inc(V.free, 1)
                    assert ch.n == N_CH, ch.n


_OUTS = [((4, 512, 256), 'float32')]
_SWAPPED = ("L1_xattn_Wq", "L1_xattn_Wk", "L1_xattn_Wv", "L1_xattn_Wo", "L2_xattn_Wq", "L2_xattn_Wk",
            "L2_xattn_Wv", "L2_xattn_Wo", "L1_ffn_router_w", "L1_ffn_w1", "L1_ffn_w2", "L2_ffn_gate_w",
            "L2_ffn_fc1s", "L2_ffn_fc2s", "L3_ffn_router_w", "L3_ffn_expert_w1", "L3_ffn_expert_w2")
_COLUMNS = ("L0_xattn_b_kv", "L0_xattn_b_q", "L0_xattn_b1", "L0_ffn_cn_b1", "L0_ffn_cn_b2", "L0_ffn_gc_b1",
            "L1_xattn_bq", "L1_xattn_bk", "L1_ffn_b1", "L2_ffn_ln_w", "L2_ffn_ln_b", "L2_ffn_b1s", "L3_ffn_expert_b1")


def kernel(**inputs):
    import numpy as _np
    import concourse.bacc as _bacc
    from concourse import mybir as _mybir
    from concourse.bass_utils import run_bass_kernel_spmd as _run

    nc = _bacc.Bacc("TRN2", target_bir_lowering=False, num_devices=1)
    arrays, args = {}, {}
    for name in inputs:
        a = _np.asarray(inputs[name])
        if name in _SWAPPED:
            a = _np.swapaxes(a, -1, -2)
        a = _np.ascontiguousarray(a)
        laid = {name: a}
        if name in _COLUMNS:
            laid[name + "_cols"] = _np.ascontiguousarray(_np.swapaxes(a.reshape(*a.shape[:-1], -1, 128), -1, -2))
        for key, a in laid.items():
            arrays[f"in_{key}_dram"] = a
            args[key] = nc.dram_tensor(f"in_{key}_dram", a.shape, _mybir.dt.from_np(a.dtype), kind="ExternalInput").ap()
    outs = []
    for i, (shape, dtype) in enumerate(_OUTS):
        dt = _mybir.dt.from_np(_np.dtype(dtype))
        outs.append(nc.dram_tensor(f"out_{i}_dram", shape, dt, kind="ExternalOutput").ap())
    program(nc, args, outs[0], STAGES)
    r = _run(nc, [arrays], core_ids=[0])
    return r.results[0]["out_0_dram"]


STAGES = range(8)
```

```python
from contextlib import ExitStack

import concourse.bass as bass
from concourse import mybir

F32 = mybir.dt.float32
BF16 = mybir.dt.bfloat16
I32 = mybir.dt.int32
U8 = mybir.dt.uint8
ACT = mybir.ActivationFunctionType
ALU = mybir.AluOpType
AX = mybir.AxisListType
ds = bass.ds

P = 128
B = 4
S = 512
SK = 1024
D = 256
DT = D // P
QT = S // P
KT = SK // P
NT = B * QT
F = 1024
FT = F // P
E = 8
H = 16
LN_EPS = 1e-5
BIG = 2.0 ** 30


class Chain:

    def __init__(self, eng, sem, base=0):
        self.eng, self.sem, self.base, self.n = eng, sem, base, 0

    def mark(self, ins):
        ins.then_inc(self.sem, 1)
        self.n += 1
        return self.n

    def wait(self, k=None):
        self.eng.wait_ge(self.sem, self.base + (self.n if k is None else k))


class Ring:

    def __init__(self, banks, full, free, per):
        self.banks, self.full, self.free, self.per = banks, full, free, per

    def start(self, eng):
        eng.sem_inc(self.free, 1)

    def bank(self, n):
        return self.banks[n % len(self.banks)]

    def wait_turns(self, eng, b):
        eng.wait_ge(self.free, b * self.per + 1)

    def wait_free(self, pe, b, n):
        if n >= len(self.banks):
            pe.wait_ge(self.free, b * self.per + n - len(self.banks) + 2)

    def wait_full(self, eng, b, n):
        eng.wait_ge(self.full, b * self.per + n + 1)

    def wait_done(self, eng, b, n):
        eng.wait_ge(self.free, b * self.per + n + 2)


def split_wait(eng, sem):
    eng.sem_inc(sem, 1)


def program(nc, t, out, stages):
    ctx = ExitStack()
    with ctx:
        def sb(c, name, shape, dt=F32):
            return c.enter_context(nc.sbuf_tensor(name, shape, dt))

        taken = []

        def sem(name):
            taken.append(nc.alloc_semaphore(name))
            return taken[-1]

        def end_layer():
            nc.clear_and_free_semaphores(taken)
            taken.clear()
            nc.all_engine_barrier()

        K = {"nc": nc, "t": t, "sb": sb, "sem": sem}
        K["PS"] = ctx.enter_context(nc.psum_tensor("PS", [P, 8, 512], F32))
        K["X"] = sb(ctx, "X", [P, NT, D])
        K["ctxT"] = sb(ctx, "ctxT", [P, DT, B * SK])
        K["ident"] = sb(ctx, "ident", [P, P])
        K["identb"] = sb(ctx, "identb", [P, P], BF16)
        K["ones"] = sb(ctx, "ones", [P, P])
        K["eps"] = sb(ctx, "eps", [P, 1])
        K["passed"] = nc.alloc_semaphore("waits_passed")
        load_stage(K)
        layers = (lambda: single_head_attention(K),
                  lambda: coupled_ffn(K),
                  lambda: head_attention(K, "L1", 1.0 / 16.0, True, False),
                  lambda: experts(K, "L1", ACT.Relu, False),
                  lambda: head_attention(K, "L2", 0.25, False, True),
                  lambda: experts(K, "L2", ACT.Gelu_apprx_tanh, True),
                  lambda: causal_attention(K),
                  lambda: experts(K, "L3", ACT.Gelu, False))
        for i in stages:
            layers[i]()
            end_layer()
        store_stage(K, out)


def load_stage(K):
    nc, t, sb, sem, PS = K["nc"], K["t"], K["sb"], K["sem"], K["PS"]
    X, ctxT, ident, identb, ones, eps = (K[n] for n in ("X", "ctxT", "ident", "identb", "ones", "eps"))
    with ExitStack() as c:
        raw = sb(c, "ctx_raw", [P, B * KT, D])
        x_in, ctx_in, made, idm, turned, moved, movedv = (sem(n) for n in (
            "x_in", "ctx_in", "ident_zero", "ident_made", "ctx_turned", "ctx_moved_act", "ctx_moved_dve"))
        with nc.Block() as block:
            @block.sync
            def _(sp):
                for b in range(B):
                    sp.dma_start(raw[:, KT * b:KT * (b + 1), :],
                                 t["ctx_1024"][b].rearrange("(k p) d -> p k d", p=P)).then_inc(ctx_in, 16)
                sp.dma_start(X[:], t["x"].rearrange("b (k p) d -> p (b k) d", p=P)).then_inc(x_in, 16)
                sp.wait_ge(x_in, 16)

            @block.gpsimd
            def _(pool):
                pool.memset(ones[:], 1.0).then_inc(made, 1)
                pool.memset(eps[:], LN_EPS).then_inc(made, 1)
                pool.wait_ge(made, 2)
                pool.affine_select(out=ident[:], in_=ones[:], compare_op=ALU.is_equal, fill=0.0, base=0,
                                   pattern=[[1, P]], channel_multiplier=-1).then_inc(idm, 1)
                pool.wait_ge(idm, 1)
                pool.tensor_copy(identb[:], ident[:]).then_inc(idm, 1)
                pool.wait_ge(idm, 2)

            def half(n):
                return n // DT, n % DT

            @block.tensor
            def _(pe):
                pe.wait_ge(idm, 1)
                for n in range(B * KT // 4 * DT):
                    g, f = half(n)
                    pe.wait_ge(ctx_in, 16 * B)
                    if n >= 8:
                        pe.wait_ge((moved, movedv)[n % 2], (n - 8) // 2 + 1)
                    for k in range(4):
                        mm = pe.transpose(PS[:, n % 8, k * P:(k + 1) * P], raw[:, 4 * g + k, f * P:(f + 1) * P], ident[:])
                    mm.then_inc(turned, 1)

            def move(eng, mine, done, op):
                for n in range(mine, B * KT // 4 * DT, 2):
                    g, f = half(n)
                    eng.wait_ge(turned, n + 1)
                    op(ctxT[:, f, 512 * g:512 * (g + 1)], PS[:, n % 8, :]).then_inc(done, 1)
                eng.wait_ge(done, B * KT // 4 * DT // 2)

            @block.scalar
            def _(act):
                move(act, 0, moved, act.copy)

            @block.vector
            def _(dve):
                move(dve, 1, movedv, dve.tensor_copy)


def store_stage(K, out):
    nc, X = K["nc"], K["X"]
    stored = K["sem"]("stored")
    with nc.Block() as block:
        @block.sync
        def _(sp):
            sp.dma_start(out.rearrange("b (k p) d -> p (b k) d", p=P), X[:]).then_inc(stored, 16)
            sp.wait_ge(stored, 16)


def ln_statistics(dve, ch, src, st, mv):
    for k in range(QT):
        ch.mark(dve.bn_stats(st[:, k, :], src(k)))
    ch.wait()
    for k in range(QT):
        ch.mark(dve.bn_aggr(mv[:, k, :], st[:, k, :]))
    ch.wait()


def ln_apply(dve, ch, src, mv, std, rstd, xn, done):
    ch.mark(dve.reciprocal(rstd[:], std[:]))
    ch.wait()
    for k in range(QT):
        dve.tensor_scalar(xn[:, k, :], src(k), mv[:, k, 0:1], rstd[:, k:k + 1], ALU.subtract, ALU.mult).then_inc(done, 1)


def single_head_attention(K):
    nc, t, sb, sem, PS, X, ctxT = (K[n] for n in ("nc", "t", "sb", "sem", "PS", "X", "ctxT"))
    ident, ones, eps = K["ident"], K["ones"], K["eps"]
    N_ACT = 4 + 1 + 2 + FT
    N_DVE = 4 + 1 + 2 * QT + DT + QT
    XT_A, Q_A, H_A = 4, 5, 7
    XT_D, T_D, O_D, Y_D = 4, 5, 5 + 2 * QT, 5 + 2 * QT + DT
    N_CH = 2 * QT - 1 + 1 + QT
    with ExitStack() as c:
        wkv = sb(c, "a0_wkv", [P, DT, 2 * D]); wq = sb(c, "a0_wq", [P, DT, D])
        w1 = sb(c, "a0_w1", [P, DT, F]); w2 = sb(c, "a0_w2", [P, FT, D])
        bk = sb(c, "a0_bk", [P, DT]); bq = sb(c, "a0_bq", [P, DT]); b1 = sb(c, "a0_b1", [P, FT])
        bv = sb(c, "a0_bv", [1, D]); b2 = sb(c, "a0_b2", [1, D])
        cb = sb(c, "a0_ctxb", [P, DT, SK])
        xn = sb(c, "a0_xn", [P, QT, D]); xT = sb(c, "a0_xT", [P, DT, S])
        qT = sb(c, "a0_qT", [P, DT, S]); kT = sb(c, "a0_kT", [P, DT, SK]); v = sb(c, "a0_v", [P, KT, D])
        pr = sb(c, "a0_pr", [P, 2, SK]); pT = sb(c, "a0_pT", [P, KT, S])
        oT = sb(c, "a0_oT", [P, DT, S]); hT = sb(c, "a0_hT", [P, FT, S])
        st = sb(c, "a0_st", [P, QT, 6]); mv = sb(c, "a0_mv", [P, QT, 2])
        std = sb(c, "a0_std", [P, QT]); rstd = sb(c, "a0_rstd", [P, QT])
        nmax = sb(c, "a0_nmax", [P, QT]); psum_ = sb(c, "a0_sum", [P, QT]); rsum = sb(c, "a0_rsum", [P, QT])
        w_in, ch_s, std_s, mv_s, xn_s, cb_s = (sem("a0_" + n) for n in (
            "weights_in", "dve_chain", "std_ready", "var_ready", "xn_ready", "ctx_copied"))
        s_full, s_max, s_exp, p_norm = (sem("a0_" + n) for n in ("scores_full", "max_ready", "exp_done", "probs_scaled"))
        A = Ring([PS[:, 0, :], PS[:, 1, :]], sem("a0_act_full"), sem("a0_act_free"), N_ACT)
        V = Ring([PS[:, 2, :], PS[:, 3, :]], sem("a0_dve_full"), sem("a0_dve_free"), N_DVE)
        scores = [PS[:, 4:6, :], PS[:, 6:8, :]]
        N_W = 16 * 9
        with nc.Block() as block:
            @block.sync
            def _(sp):
                for dst, src in (
                    (wkv[:], t["L0_xattn_W_kv"].rearrange("(k p) n -> p k n", p=P)),
                    (wq[:], t["L0_xattn_W_q"].rearrange("(k p) n -> p k n", p=P)),
                    (bk[:], t["L0_xattn_b_kv_cols"][:, 0:DT]),
                    (bq[:], t["L0_xattn_b_q_cols"]),
                    (b1[:], t["L0_xattn_b1_cols"]),
                    (bv[:], t["L0_xattn_b_kv"][D:2 * D].rearrange("(a n) -> a n", a=1)),
                    (b2[:], t["L0_xattn_b2"].rearrange("(a n) -> a n", a=1)),
                    (w1[:], t["L0_xattn_W1"].rearrange("(k p) n -> p k n", p=P)),
                    (w2[:], t["L0_xattn_W2"].rearrange("(k p) n -> p k n", p=P)),
                ):
                    sp.dma_start(dst, src).then_inc(w_in, 16)

            @block.gpsimd
            def _(pool):
                A.start(pool)
                V.start(pool)
                with pool.Fori(0, B) as b:
                    V.wait_turns(pool, b)
                    for f in range(DT):
                        pool.tensor_copy(cb[:, f, :], ctxT[:, f, ds(b * SK, SK)]).then_inc(cb_s, 1)

            @block.tensor
            def _(pe):
                pe.wait_ge(w_in, N_W)
                with pe.Fori(0, B) as b:
                    pe.wait_ge(cb_s, b * DT + DT)
                    for m in range(DT):
                        for n in range(2):
                            i = 2 * m + n
                            A.wait_free(pe, b, i)
                            for k in range(DT):
                                mm = pe.matmul(A.bank(i), wkv[:, k, m * P:(m + 1) * P], cb[:, k, n * 512:(n + 1) * 512],
                                               start=(k == 0), stop=(k == DT - 1))
                            mm.then_inc(A.full, 1)
                    for i in range(4):
                        V.wait_free(pe, b, i)
                        for u in range(2):
                            o = V.bank(i)[:, u * D:(u + 1) * D]
                            pe.matmul(o, ones[0:1, :], bv[:], start=True, stop=False, skip_group_check=True)
                            for k in range(DT):
                                mm = pe.matmul(o, cb[:, k, (2 * i + u) * P:(2 * i + u + 1) * P], wkv[:, k, D:2 * D],
                                               start=False, stop=(k == DT - 1), skip_group_check=True)
                        mm.then_inc(V.full, 1)
                    pe.wait_ge(xn_s, b * QT + QT)
                    for f, (R, i) in enumerate(((A, XT_A), (V, XT_D))):
                        R.wait_free(pe, b, i)
                        for k in range(QT):
                            mm = pe.transpose(R.bank(i)[:, k * P:(k + 1) * P], xn[:, k, f * P:(f + 1) * P], ident[:])
                        mm.then_inc(R.full, 1)
                    A.wait_done(pe, b, XT_A)
                    V.wait_done(pe, b, XT_D)
                    for m in range(DT):
                        A.wait_free(pe, b, Q_A + m)
                        for k in range(DT):
                            mm = pe.matmul(A.bank(Q_A + m), wq[:, k, m * P:(m + 1) * P], xT[:, k, :],
                                           start=(k == 0), stop=(k == DT - 1))
                        mm.then_inc(A.full, 1)
                    A.wait_done(pe, b, Q_A + 1)

                    def turn(q):
                        pe.wait_ge(p_norm, b * QT + q + 1)
                        for u in range(2):
                            i = T_D + 2 * q + u
                            V.wait_free(pe, b, i)
                            for k in range(4):
                                mm = pe.transpose(V.bank(i)[:, k * P:(k + 1) * P],
                                                  pr[:, q % 2, (4 * u + k) * P:(4 * u + k + 1) * P], ident[:])
                            mm.then_inc(V.full, 1)

                    for q in range(QT):
                        if q >= 2:
                            pe.wait_ge(s_exp, b * QT + q - 1)
                        for n in range(2):
                            for k in range(DT):
                                mm = pe.matmul(scores[q % 2][:, n, :], qT[:, k, q * P:(q + 1) * P],
                                               kT[:, k, n * 512:(n + 1) * 512], start=(k == 0), stop=(k == DT - 1))
                        mm.then_inc(s_full, 1)
                        if q >= 1:
                            turn(q - 1)
                    turn(QT - 1)
                    V.wait_done(pe, b, T_D + 2 * QT - 1)
                    for m in range(DT):
                        i = O_D + m
                        V.wait_free(pe, b, i)
                        for k in range(KT):
                            mm = pe.matmul(V.bank(i), v[:, k, m * P:(m + 1) * P], pT[:, k, :],
                                           start=(k == 0), stop=(k == KT - 1))
                        mm.then_inc(V.full, 1)
                    V.wait_done(pe, b, O_D + 1)
                    for m in range(FT):
                        i = H_A + m
                        A.wait_free(pe, b, i)
                        for k in range(DT):
                            mm = pe.matmul(A.bank(i), w1[:, k, m * P:(m + 1) * P], oT[:, k, :],
                                           start=(k == 0), stop=(k == DT - 1))
                        mm.then_inc(A.full, 1)
                    A.wait_done(pe, b, H_A + FT - 1)
                    for q in range(QT):
                        i = Y_D + q
                        V.wait_free(pe, b, i)
                        o = V.bank(i)[:, 0:D]
                        pe.matmul(o, ones[0:1, :], b2[:], start=True, stop=False)
                        for k in range(FT):
                            mm = pe.matmul(o, hT[:, k, q * P:(q + 1) * P], w2[:, k, :], start=False, stop=(k == FT - 1))
                        mm.then_inc(V.full, 1)

            @block.scalar
            def _(act):
                act.wait_ge(w_in, N_W)
                with act.Fori(0, B) as b:
                    V.wait_turns(act, b)
                    act.wait_ge(mv_s, b + 1)
                    act.activation(std[:], mv[:, :, 1], ACT.Sqrt, bias=eps[:]).then_inc(std_s, 1)
                    for m in range(DT):
                        for n in range(2):
                            A.wait_full(act, b, 2 * m + n)
                            act.activation(kT[:, m, n * 512:(n + 1) * 512], A.bank(2 * m + n), ACT.Identity,
                                           bias=bk[:, m:m + 1]).then_inc(A.free, 1)
                    A.wait_full(act, b, XT_A)
                    act.copy(xT[:, 0, :], A.bank(XT_A)).then_inc(A.free, 1)
                    for m in range(DT):
                        A.wait_full(act, b, Q_A + m)
                        act.activation(qT[:, m, :], A.bank(Q_A + m), ACT.Identity, bias=bq[:, m:m + 1]).then_inc(A.free, 1)
                    for q in range(QT):
                        act.wait_ge(s_max, b * QT + q + 1)
                        if q >= 2:
                            V.wait_done(act, b, T_D + 2 * (q - 2) + 1)
                        act.activation(pr[:, q % 2, :], scores[q % 2], ACT.Exp, bias=nmax[:, q:q + 1],
                                       accum_out=psum_[:, q:q + 1]).then_inc(s_exp, 1)
                    for m in range(FT):
                        A.wait_full(act, b, H_A + m)
                        act.activation(hT[:, m, :], A.bank(H_A + m), ACT.Gelu, bias=b1[:, m:m + 1]).then_inc(A.free, 1)

            @block.vector
            def _(dve):
                with dve.Fori(0, B) as b:
                    ch = Chain(dve, ch_s, b * N_CH)
                    V.wait_turns(dve, b)
                    split_wait(dve, K["passed"])
                    src = lambda k: X[:, ds(b * QT + k, 1), :]
                    for k in range(QT):
                        ch.mark(dve.bn_stats(st[:, k, :], src(k)))
                    ch.wait()
                    split_wait(dve, K["passed"])
                    for k in range(QT):
                        ins = dve.bn_aggr(mv[:, k, :], st[:, k, :])
                        if k < QT - 1:
                            ch.mark(ins)
                    ins.then_inc(mv_s, 1)
                    dve.wait_ge(mv_s, b + 1)
                    dve.wait_ge(std_s, b + 1)
                    ln_apply(dve, ch, src, mv, std, rstd, xn, xn_s)
                    for i in range(4):
                        V.wait_full(dve, b, i)
                        dve.tensor_copy(v[:, 2 * i:2 * i + 2, :], V.bank(i).rearrange("p (u d) -> p u d", u=2)).then_inc(V.free, 1)
                    V.wait_full(dve, b, XT_D)
                    dve.tensor_copy(xT[:, 1, :], V.bank(XT_D)).then_inc(V.free, 1)

                    def max_of(q):
                        dve.wait_ge(s_full, b * QT + q + 1)
                        dve.tensor_reduce(nmax[:, q:q + 1], scores[q % 2], AX.XY, ALU.max, negate=True).then_inc(s_max, 1)

                    def scale(q):
                        dve.wait_ge(s_exp, b * QT + q + 1)
                        ch.mark(dve.reciprocal(rsum[:, q:q + 1], psum_[:, q:q + 1]))
                        ch.wait()
                        dve.tensor_scalar(pr[:, q % 2, :], pr[:, q % 2, :], rsum[:, q:q + 1], None,
                                          ALU.mult).then_inc(p_norm, 1)

                    def turned(q):
                        for u in range(2):
                            i = T_D + 2 * q + u
                            V.wait_full(dve, b, i)
                            dve.tensor_copy(pT[:, 4 * u:4 * u + 4, q * P:(q + 1) * P],
                                            V.bank(i).rearrange("p (k n) -> p k n", k=4)).then_inc(V.free, 1)

                    for q in range(QT):
                        max_of(q)
                        if q >= 1:
                            scale(q - 1)
                            turned(q - 1)
                    scale(QT - 1)
                    turned(QT - 1)
                    for m in range(DT):
                        V.wait_full(dve, b, O_D + m)
                        dve.tensor_copy(oT[:, m, :], V.bank(O_D + m)).then_inc(V.free, 1)
                    for q in range(QT):
                        V.wait_full(dve, b, Y_D + q)
                        x = X[:, ds(b * QT + q, 1), :]
                        dve.tensor_tensor(x, x, V.bank(Y_D + q)[:, None, 0:D], ALU.add).then_inc(V.free, 1)
                    assert ch.n == N_CH, ch.n


def coupled_ffn(K):
    nc, t, sb, sem, PS, X = (K[n] for n in ("nc", "t", "sb", "sem", "PS", "X"))
    ident, ones, eps = K["ident"], K["ones"], K["eps"]
    TURNS = 3
    H3 = 64
    N_ACT = 1 + 3 + TURNS * 5
    N_DVE = 1 + QT
    N_CH = 2 * QT - 1 + 1 + 1 + 2 + TURNS * 3
    with ExitStack() as c:
        w1 = sb(c, "f0_w1", [P, DT, D]); w2 = sb(c, "f0_w2", [P, DT, P]); w3 = sb(c, "f0_w3", [P, H3])
        w4 = sb(c, "f0_w4", [H3, 1]); w4b = sb(c, "f0_w4b", [H3, P])
        g1w = sb(c, "f0_g1w", [P, DT, P]); g2w = sb(c, "f0_g2w", [P, H3]); g3w = sb(c, "f0_g3w", [H3, 1])
        b1 = sb(c, "f0_b1", [P, DT]); b2 = sb(c, "f0_b2", [P, 1]); b3 = sb(c, "f0_b3", [H3, 1])
        gb1 = sb(c, "f0_gb1", [P, 1]); gb2 = sb(c, "f0_gb2", [H3, 1])
        row = sb(c, "f0_row", [1, 3]); sc = sb(c, "f0_sc", [P, 3]); slope = sb(c, "f0_slope", [P, 1])
        sign = sb(c, "f0_sign", [P, 2])
        xn = sb(c, "f0_xn", [P, QT, D]); y = sb(c, "f0_y", [P, DT, S])
        mean = sb(c, "f0_mean", [P, DT]); g1 = sb(c, "f0_g1", [P, 1]); g2 = sb(c, "f0_g2", [H3, 1])
        g2b = sb(c, "f0_g2b", [H3, P]); gf = sb(c, "f0_gf", [P, 1]); off = sb(c, "f0_off", [P, 2])
        h1 = sb(c, "f0_h1", [P, DT, S]); h2 = sb(c, "f0_h2", [P, S]); h3 = sb(c, "f0_h3", [H3, S])
        tf = sb(c, "f0_tf", [P, S]); cp = sb(c, "f0_cp", [P, S]); tw = sb(c, "f0_tw", [P, DT, S])
        st = sb(c, "f0_st", [P, QT, 6]); mv = sb(c, "f0_mv", [P, QT, 2])
        std = sb(c, "f0_std", [P, QT]); rstd = sb(c, "f0_rstd", [P, QT])
        w_in, made, ch_s, std_s, mv_s, xn_s, mean_s, g2b_s, y_s, sc_full, sc_s = (sem("f0_" + n) for n in (
            "weights_in", "constants_made", "dve_chain", "std_ready", "var_ready", "xn_ready", "mean_ready",
            "g2_spread", "y_updated", "scalars_full", "scalars_ready"))
        A = Ring([PS[:, i, :] for i in range(4)], sem("f0_act_full"), sem("f0_act_free"), N_ACT)
        V = Ring([PS[:, i, :] for i in range(4, 7)], sem("f0_dve_full"), sem("f0_dve_free"), N_DVE)
        loads = [(w1[:], t["L0_ffn_cn_w1"].rearrange("(k p) n -> p k n", p=P)),
                 (w2[:], t["L0_ffn_cn_w2"].rearrange("(k p) n -> p k n", p=P)),
                 (w3[:], t["L0_ffn_cn_w3"]), (w4[:], t["L0_ffn_cn_w4"]),
                 (g1w[:], t["L0_ffn_gc_w1"].rearrange("(k p) n -> p k n", p=P)),
                 (g2w[:], t["L0_ffn_gc_w2"]), (g3w[:], t["L0_ffn_gc_w3"]),
                 (b1[:], t["L0_ffn_cn_b1_cols"]), (b2[:], t["L0_ffn_cn_b2_cols"]),
                 (b3[:], t["L0_ffn_cn_b3"].rearrange("(p a) -> p a", a=1)),
                 (gb1[:], t["L0_ffn_gc_b1_cols"]), (gb2[:], t["L0_ffn_gc_b2"].rearrange("(p a) -> p a", a=1)),
                 (row[:, 0:1], t["L0_ffn_cn_b4"].rearrange("(a n) -> a n", a=1)),
                 (row[:, 1:2], t["L0_ffn_gc_b3"].rearrange("(a n) -> a n", a=1)),
                 (row[:, 2:3], t["L0_ffn_adaptive_range"].rearrange("(a n) -> a n", a=1))]
        with nc.Block() as block:
            @block.sync
            def _(sp):
                for dst, src in loads:
                    sp.dma_start(dst, src).then_inc(w_in, 16)

            @block.gpsimd
            def _(pool):
                A.start(pool)
                V.start(pool)
                pool.memset(sign[0:64, 0:1], 1.0).then_inc(made, 1)
                pool.memset(sign[64:128, 0:1], -1.0).then_inc(made, 1)
                pool.memset(sign[0:64, 1:2], -1.0).then_inc(made, 1)
                pool.memset(sign[64:128, 1:2], 1.0).then_inc(made, 1)

            @block.tensor
            def _(pe):
                pe.wait_ge(w_in, 16 * len(loads))
                pe.matmul(PS[:, 7, 0:3], ones[0:1, :], row[:], start=True, stop=True).then_inc(sc_full, 1)
                pe.wait_ge(sc_s, 3)
                with pe.Fori(0, B) as b:
                    pe.wait_ge(xn_s, b * QT + QT)
                    for f, R in enumerate((A, V)):
                        for k in range(QT):
                            mm = pe.transpose(R.bank(0)[:, k * P:(k + 1) * P], xn[:, k, f * P:(f + 1) * P], ident[:])
                        mm.then_inc(R.full, 1)
                    i = 1
                    pe.wait_ge(mean_s, b + 1)
                    for k in range(DT):
                        mm = pe.matmul(A.bank(i)[:, 0:1], g1w[:, k, :], mean[:, k:k + 1], start=(k == 0), stop=(k == DT - 1))
                    mm.then_inc(A.full, 1)
                    A.wait_done(pe, b, i)
                    i += 1
                    pe.matmul(A.bank(i)[0:H3, 0:1], g2w[:], g1[:], start=True, stop=True).then_inc(A.full, 1)
                    i += 1
                    pe.wait_ge(g2b_s, b + 1)
                    pe.matmul(A.bank(i)[:, 0:1], g2b[:], g3w[:], start=True, stop=True).then_inc(A.full, 1)
                    i += 1
                    for r in range(TURNS):
                        if r:
                            pe.wait_ge(y_s, b * TURNS * DT + DT * r)
                        for m in range(DT):
                            A.wait_free(pe, b, i)
                            for k in range(DT):
                                mm = pe.matmul(A.bank(i), w1[:, k, m * P:(m + 1) * P], y[:, k, :],
                                               start=(k == 0), stop=(k == DT - 1))
                            mm.then_inc(A.full, 1)
                            i += 1
                        A.wait_done(pe, b, i - 1)
                        for k in range(DT):
                            mm = pe.matmul(A.bank(i), w2[:, k, :], h1[:, k, :], start=(k == 0), stop=(k == DT - 1))
                        mm.then_inc(A.full, 1)
                        A.wait_done(pe, b, i)
                        i += 1
                        pe.matmul(A.bank(i)[0:H3, :], w3[:], h2[:], start=True, stop=True).then_inc(A.full, 1)
                        A.wait_done(pe, b, i)
                        i += 1
                        pe.matmul(A.bank(i), w4b[:], h3[:], start=True, stop=True).then_inc(A.full, 1)
                        i += 1
                    assert i == N_ACT
                    pe.wait_ge(y_s, b * TURNS * DT + DT * TURNS)
                    for q in range(QT):
                        V.wait_free(pe, b, 1 + q)
                        for f in range(DT):
                            mm = pe.transpose(V.bank(1 + q)[:, f * P:(f + 1) * P], y[:, f, q * P:(q + 1) * P], ident[:])
                        mm.then_inc(V.full, 1)

            @block.scalar
            def _(act):
                act.wait_ge(w_in, 16 * len(loads))
                act.wait_ge(sc_s, 3)
                with act.Fori(0, B) as b:
                    V.wait_turns(act, b)
                    act.wait_ge(mv_s, b + 1)
                    act.activation(std[:], mv[:, :, 1], ACT.Sqrt, bias=eps[:]).then_inc(std_s, 1)
                    i = 0

                    def job(dst, src, func, bias):
                        nonlocal i
                        A.wait_full(act, b, i)
                        if bias is None:
                            act.copy(dst, src(A.bank(i))).then_inc(A.free, 1)
                        else:
                            act.activation(dst, src(A.bank(i)), func, bias=bias).then_inc(A.free, 1)
                        i += 1

                    job(y[:, 0, :], lambda o: o, None, None)
                    job(g1[:], lambda o: o[:, 0:1], ACT.Gelu, gb1[:])
                    job(g2[:], lambda o: o[0:H3, 0:1], ACT.Gelu, gb2[:])
                    job(gf[:], lambda o: o[:, 0:1], ACT.Sigmoid, sc[:, 1:2])
                    for r in range(TURNS):
                        job(h1[:, 0, :], lambda o: o, ACT.Gelu, b1[:, 0:1])
                        job(h1[:, 1, :], lambda o: o, ACT.Gelu, b1[:, 1:2])
                        job(h2[:], lambda o: o, ACT.Gelu, b2[:])
                        job(h3[:], lambda o: o[0:H3, :], ACT.Gelu, b3[:])
                        job(tf[:], lambda o: o, ACT.Sigmoid, sc[:, 0:1])

            @block.vector
            def _(dve):
                dve.wait_ge(w_in, 16 * len(loads))
                dve.wait_ge(made, 4)
                dve.tensor_copy(w4b[:], w4[:].broadcast_to([H3, P])).then_inc(sc_s, 1)
                dve.wait_ge(sc_full, 1)
                dve.tensor_copy(sc[:], PS[:, 7, 0:3]).then_inc(sc_s, 1)
                dve.wait_ge(sc_s, 2)
                dve.tensor_scalar(slope[:], sc[:, 2:3], 0.6, None, ALU.mult).then_inc(sc_s, 1)
                dve.wait_ge(sc_s, 3)
                with dve.Fori(0, B) as b:
                    ch = Chain(dve, ch_s, b * N_CH)
                    V.wait_turns(dve, b)
                    split_wait(dve, K["passed"])
                    src = lambda k: X[:, ds(b * QT + k, 1), :]
                    for k in range(QT):
                        ch.mark(dve.bn_stats(st[:, k, :], src(k)))
                    ch.wait()
                    split_wait(dve, K["passed"])
                    for k in range(QT):
                        ins = dve.bn_aggr(mv[:, k, :], st[:, k, :])
                        if k < QT - 1:
                            ch.mark(ins)
                    ins.then_inc(mv_s, 1)
                    dve.wait_ge(mv_s, b + 1)
                    dve.wait_ge(std_s, b + 1)
                    ln_apply(dve, ch, src, mv, std, rstd, xn, xn_s)
                    V.wait_full(dve, b, 0)
                    dve.tensor_copy(y[:, 1, :], V.bank(0)).then_inc(V.free, 1)
                    A.wait_done(dve, b, 0)
                    V.wait_done(dve, b, 0)
                    ch.mark(dve.tensor_reduce(mean[:, 0:2], y[:], AX.X, ALU.add))
                    ch.wait()
                    dve.tensor_scalar(mean[:], mean[:], 1.0 / S, None, ALU.mult).then_inc(mean_s, 1)
                    A.wait_done(dve, b, 2)
                    dve.tensor_copy(g2b[:], g2[:].broadcast_to([H3, P])).then_inc(g2b_s, 1)
                    A.wait_done(dve, b, 3)
                    ch.mark(dve.tensor_scalar(off[:, 0:1], gf[:], 1.4, -1.0, ALU.mult, ALU.add))
                    ch.wait()
                    ch.mark(dve.tensor_scalar(off[:, 1:2], off[:, 0:1], sc[:, 2:3], 0.1, ALU.mult, ALU.add))
                    ch.wait()
                    for r in range(TURNS):
                        A.wait_done(dve, b, 3 + 5 * (r + 1))
                        ch.mark(dve.tensor_scalar(cp[:], tf[:], slope[:], off[:, 1:2], ALU.mult, ALU.add))
                        ch.wait()
                        for f in range(DT):
                            ch.mark(dve.scalar_tensor_tensor(out=tw[:, f, :], in0=y[:, 1 - f, :], scalar=sign[:, f:f + 1],
                                                             in1=cp[:], op0=ALU.mult, op1=ALU.mult))
                        ch.wait()
                        for f in range(DT):
                            dve.tensor_tensor(y[:, f, :], y[:, f, :], tw[:, f, :], ALU.add).then_inc(y_s, 1)
                        dve.wait_ge(y_s, b * TURNS * DT + DT * (r + 1))
                    for q in range(QT):
                        V.wait_full(dve, b, 1 + q)
                        x = X[:, ds(b * QT + q, 1), :]
                        dve.tensor_tensor(x, x, V.bank(1 + q)[:, None, 0:D], ALU.add).then_inc(V.free, 1)
                    assert ch.n == N_CH, ch.n


def head_attention(K, name, scale, biased, masked):
    nc, t, sb, sem, PS, X, ctxT = (K[n] for n in ("nc", "t", "sb", "sem", "PS", "X", "ctxT"))
    ident, identb, ones, eps = K["ident"], K["identb"], K["ones"], K["eps"]
    HD = D // H
    G = H // 4
    TERMS = ((0, 0), (1, 0), (0, 1), (2, 0), (0, 2), (1, 1))
    ROWS = HD * len(TERMS)
    CW = 32
    N_MAX = 4 * QT * 2
    UNITS = 4 * 4
    NE = 8
    N_ACT = 4 + 1 + 2
    V_V, V_XT, V_M = 0, 4, 5
    vjobs = [("v", i) for i in range(4)] + [("xT",)] + [("max", 0, i) for i in range(N_MAX)] + [("neg", 0)]
    for g in range(G):
        for n in range(UNITS):
            if g >= 1 and n == 3:
                vjobs.append(("sum", g - 1))
            if g + 1 < G:
                vjobs += [("max", g + 1, i) for i in range(3 * n, min(3 * n + 3, N_MAX))]
                if n == 12:
                    vjobs.append(("neg", g + 1))
    vjobs += [("sum", G - 1)] + [("y", q) for q in range(QT)]
    N_DVE = len(vjobs)
    vat = {j: i for i, j in enumerate(vjobs)}
    Wt = "%s_xattn_W" % name
    with ExitStack() as c:
        pre = name + "a_"
        wq = sb(c, pre + "wq", [P, DT, D]); wk = sb(c, pre + "wk", [P, DT, D]); wv = sb(c, pre + "wv", [P, DT, D])
        wo = sb(c, pre + "wo", [P, G, D]); sel = sb(c, pre + "sel", [P, P])
        bq = sb(c, pre + "bq", [P, DT]); bk = sb(c, pre + "bk", [P, DT])
        bv = sb(c, pre + "bv", [1, D]); bo = sb(c, pre + "bo", [1, D])
        cb = sb(c, pre + "cb", [P, DT, SK])
        ex = sb(c, pre + "ex", [P, NE, SK])
        exw = ex[:, :, :].rearrange("p e n -> p (e n)")
        kf = exw[:, 0:DT * SK].rearrange("p (k n) -> p k n", k=DT)
        ks = exw[:, 2048:5120].bitcast(BF16).rearrange("p (i k n) -> p i k n", i=3, k=DT)
        qf = exw[:, 5120:6144].rearrange("p (k n) -> p k n", k=DT)
        qs = exw[:, 6144:7680].bitcast(BF16).rearrange("p (i k n) -> p i k n", i=3, k=DT)
        xT = sb(c, pre + "xT", [P, DT, S])
        kst = sb(c, pre + "kst", [P, H, SK], BF16); qst = sb(c, pre + "qst", [P, H, S], BF16)
        v = sb(c, pre + "v", [P, KT, G, 4, CW])
        mx = sb(c, pre + "mx", [P, QT, 4, 2]); nm = sb(c, pre + "nm", [P, QT, 4]); nr = sb(c, pre + "nr", [P, QT, 4])
        nr2 = sb(c, pre + "nr2", [P, QT, 4]); nsp = sb(c, pre + "nsp", [P, QT, 3, 4], BF16); nT = sb(c, pre + "nT", [12, S], BF16)
        osb = sb(c, pre + "osb", [P, 2, S]); rc = sb(c, pre + "rc", [P, S]); aT = sb(c, pre + "aT", [P, G, S])
        kr = aT[:, :, :].rearrange("p g n -> p (g n)").rearrange("p (k n) -> p k n", k=DT)
        qr = osb
        xn = osb[:, :, :].rearrange("p a n -> p (a n)").rearrange("p (q d) -> p q d", q=QT)
        st = sb(c, pre + "st", [P, QT, 6]); mv = sb(c, pre + "mv", [P, QT, 2])
        std = sb(c, pre + "std", [P, QT]); rstd = sb(c, pre + "rstd", [P, QT])
        if masked:
            mraw = exw[:, 0:QT * SK // 4].bitcast(U8).rearrange("p (q n) -> p q n", q=QT)
            biasq = sb(c, pre + "biasq", [P, QT, SK], BF16); biask = sb(c, pre + "biask", [P, KT, S], BF16)
            any_ = sb(c, pre + "any", [P, QT]); anyb = aT[:, 0, :].rearrange("p (q n) -> p q n", q=QT)
            flag = sb(c, pre + "flag", [P, S])
        qdram = nc.dram_tensor(pre + "q_parts", (3, D, S), BF16, kind="Internal").ap()
        kdram = nc.dram_tensor(pre + "k_parts", (3, D, SK), BF16, kind="Internal").ap()
        names = ("weights_in", "zeroed", "constants_made", "dve_chain", "pool_chain", "std_ready", "var_ready", "xn_ready",
                 "ctx_copied", "k_split", "q_split", "k_stored", "q_stored", "k_stacked", "q_stacked", "neg_ready",
                 "neg_turned", "neg_in", "scores_full", "exp_done", "pv_done", "attention_ready", "max_ready",
                 "mask_full", "mask_done")
        (w_in, zeroed, made, ch_s, pc_s, std_s, mv_s, xn_s, cb_s, ksp_s, qsp_s, kst_s, qst_s, kin_s, qin_s, nr_s,
         nt_s, nin_s, s_full, s_exp, pv_s, at_s, mx_s, mk_full, mk_s) = (sem(pre + n) for n in names)
        A = Ring([PS[:, 0, :], PS[:, 1, :]], sem(pre + "act_full"), sem(pre + "act_free"), N_ACT)
        V = Ring([PS[:, 2, :], PS[:, 3, :]], sem(pre + "dve_full"), sem(pre + "dve_free"), N_DVE)
        O = Ring([PS[:, 1, :], PS[:, 0, :]], pv_s, sem(pre + "products_free"), G)
        scores = [PS[:, 4:6, :], PS[:, 6:8, :]]
        loads = [(wq[:], t[Wt + "q"].rearrange("(k p) n -> p k n", p=P)),
                 (wk[:], t[Wt + "k"].rearrange("(k p) n -> p k n", p=P)),
                 (wv[:], t[Wt + "v"].rearrange("(k p) n -> p k n", p=P))]
        loads += [(wo[32 * j:32 * j + HD, :, :], t[Wt + "o"].rearrange("(g j d) n -> j d g n", j=4, d=HD)[j]) for j in range(4)]
        if biased:
            loads += [(bq[:], t["L1_xattn_bq_cols"]), (bk[:], t["L1_xattn_bk_cols"]),
                      (bv[:], t["L1_xattn_bv"].rearrange("(a n) -> a n", a=1)),
                      (bo[:], t["L1_xattn_bo"].rearrange("(a n) -> a n", a=1))]
        if masked:
            loads += [(mraw[:], t["mask_SxS2_bk0"].rearrange("(k p) n -> p k n", p=P))]
        N_CH = 2 * QT - 1 + 1 + 1 + 4 * G + (2 if masked else 1) * G
        with nc.Block() as block:
            @block.sync
            def _(sp):
                sp.wait_ge(zeroed, 2)
                for dst, src in loads:
                    sp.dma_start(dst, src).then_inc(w_in, 16)
                with sp.Fori(0, B) as b:
                    V.wait_turns(sp, b)
                    sp.wait_ge(ksp_s, 3 * b + 3)
                    for i in range(3):
                        sp.dma_start(kdram[i].rearrange("(m p) n -> p m n", p=P), ks[:, i, :, :]).then_inc(kst_s, 16)
                    sp.wait_ge(kst_s, 48 * b + 48)
                    for r, (_, i) in enumerate(TERMS):
                        sp.dma_start(kst[HD * r:HD * (r + 1), :, :],
                                     kdram[i].rearrange("(h d) n -> d h n", d=HD)).then_inc(kin_s, 16)
                    sp.wait_ge(qsp_s, 3 * b + 3)
                    for i in range(3):
                        sp.dma_start(qdram[i].rearrange("(m p) n -> p m n", p=P), qs[:, i, :, :]).then_inc(qst_s, 16)
                    sp.wait_ge(qst_s, 48 * b + 48)
                    for r, (i, _) in enumerate(TERMS):
                        sp.dma_start(qst[HD * r:HD * (r + 1), :, :],
                                     qdram[i].rearrange("(h d) n -> d h n", d=HD)).then_inc(qin_s, 16)
                    for g in range(G):
                        sp.wait_ge(nt_s, b * G + g + 1)
                        for i in range(3):
                            sp.dma_start(qst[ROWS + i:ROWS + i + 1, 4 * g:4 * g + 4, :],
                                         nT[4 * i:4 * i + 4, :]).then_inc(nin_s, 16)

            @block.gpsimd
            def _(pool):
                A.start(pool)
                V.start(pool)
                O.start(pool)
                pool.memset(wo[:], 0.0).then_inc(zeroed, 1)
                pool.memset(v[:], 0.0).then_inc(zeroed, 1)
                pool.wait_ge(zeroed, 2)
                pool.memset(kst[ROWS:P, :, :], 1.0).then_inc(made, 1)
                pool.wait_ge(made, 1)
                pool.memset(v[:, :, :, :, HD:HD + 1], 1.0).then_inc(made, 1)
                sv = sel[:].rearrange("p (j c) -> p j c", c=CW)
                pool.affine_select(out=sv, in_=ones[:].rearrange("p (j c) -> p j c", c=CW), compare_op=ALU.is_equal,
                                   fill=0.0, base=-HD, pattern=[[-CW, 4], [0, CW]], channel_multiplier=1).then_inc(made, 1)
                with pool.Fori(0, B) as b:
                    ch = Chain(pool, pc_s, b)
                    V.wait_turns(pool, b)
                    for f in range(DT):
                        pool.tensor_copy(cb[:, f, :], ctxT[:, f, ds(b * SK, SK)]).then_inc(cb_s, 1)
                    A.wait_done(pool, b, 3)
                    split_wait(pool, K["passed"])
                    pool.tensor_copy(ks[:, 0, :, :], kf[:]).then_inc(ksp_s, 1)
                    pool.wait_ge(ksp_s, 3 * b + 1)
                    ch.mark(pool.tensor_tensor(kr[:], kf[:], ks[:, 0, :, :], ALU.subtract))
                    ch.wait()
                    split_wait(pool, K["passed"])
                    pool.tensor_copy(ks[:, 1, :, :], kr[:]).then_inc(ksp_s, 1)
                    pool.wait_ge(ksp_s, 3 * b + 2)
                    pool.tensor_tensor(ks[:, 2, :, :], kr[:], ks[:, 1, :, :], ALU.subtract).then_inc(ksp_s, 1)

            @block.tensor
            def _(pe):
                pe.wait_ge(w_in, 16 * len(loads))
                pe.wait_ge(made, 3)
                if masked:
                    for kt in range(KT):
                        pe.wait_ge(mk_s, 2 if kt < 4 else kt - 1)
                        bank = PS[:, kt % 4, :].bitcast(BF16)
                        for q in range(QT):
                            mm = pe.transpose(bank[:, q * P:(q + 1) * P], biasq[:, q, kt * P:(kt + 1) * P], identb[:])
                        mm.then_inc(mk_full, 1)
                    pe.wait_ge(mk_s, 2 + KT)
                    pe.wait_ge(mk_s, 2 + KT + 1)
                    for q in range(QT):
                        mm = pe.matmul(PS[:, 4, q * P:(q + 1) * P], anyb[:, q, :], ident[:], start=True, stop=True,
                                       skip_group_check=True)
                    mm.then_inc(mk_full, 1)
                with pe.Fori(0, B) as b:
                    V.wait_turns(pe, b)
                    pe.wait_ge(cb_s, b * DT + DT)
                    for m in range(DT):
                        for n in range(2):
                            i = 2 * m + n
                            A.wait_free(pe, b, i)
                            for k in range(DT):
                                mm = pe.matmul(A.bank(i), wk[:, k, m * P:(m + 1) * P], cb[:, k, n * 512:(n + 1) * 512],
                                               start=(k == 0), stop=(k == DT - 1))
                            mm.then_inc(A.full, 1)
                    for i in range(4):
                        V.wait_free(pe, b, i)
                        for u in range(2):
                            o = V.bank(i)[:, u * D:(u + 1) * D]
                            for k in range(DT):
                                mm = pe.matmul(o, cb[:, k, (2 * i + u) * P:(2 * i + u + 1) * P], wv[:, k, :],
                                               start=(k == 0), stop=(k == DT - 1 and not biased), skip_group_check=True)
                            if biased:
                                mm = pe.matmul(o, ones[0:1, :], bv[:], start=False, stop=True, skip_group_check=True)
                        mm.then_inc(V.full, 1)
                    pe.wait_ge(xn_s, b * QT + QT)
                    for f, (R, i) in enumerate(((A, 4), (V, V_XT))):
                        R.wait_free(pe, b, i)
                        for k in range(QT):
                            mm = pe.transpose(R.bank(i)[:, k * P:(k + 1) * P], xn[:, k, f * P:(f + 1) * P], ident[:])
                        mm.then_inc(R.full, 1)
                    A.wait_done(pe, b, 4)
                    V.wait_done(pe, b, V_XT)
                    for m in range(DT):
                        A.wait_free(pe, b, 5 + m)
                        for k in range(DT):
                            mm = pe.matmul(A.bank(5 + m), wq[:, k, m * P:(m + 1) * P], xT[:, k, :],
                                           start=(k == 0), stop=(k == DT - 1))
                        mm.then_inc(A.full, 1)

                    def fill_max(g, i):
                        h, q, n = 4 * g + i // (2 * QT), i // 2 % QT, i % 2
                        at = vat["max", g, i]
                        V.wait_free(pe, b, at)
                        pe.matmul(V.bank(at), qst[0:ROWS, h, q * P:(q + 1) * P], kst[0:ROWS, h, n * 512:(n + 1) * 512],
                                  start=True, stop=True).then_inc(V.full, 1)

                    def fill_neg(g):
                        at = vat["neg", g]
                        V.wait_free(pe, b, at)
                        pe.wait_ge(nr_s, b * G + g + 1)
                        o = V.bank(at).bitcast(BF16)
                        for q in range(QT):
                            mm = pe.transpose(o[0:12, q * P:(q + 1) * P], nsp[:, q, :, :].rearrange("p i j -> p (i j)"), identb[:])
                        mm.then_inc(V.full, 1)

                    def fill_sum(g):
                        at = vat["sum", g]
                        V.wait_free(pe, b, at)
                        O.wait_done(pe, b, g)
                        pe.matmul(V.bank(at), sel[:], osb[:, g % 2, :], start=True, stop=True).then_inc(V.full, 1)

                    def scores_of(g, n):
                        u, j = n // 4, n % 4
                        h, at = 4 * g + j, g * UNITS + n
                        if at >= 2:
                            pe.wait_ge(s_exp, b * G * UNITS + at - 1)
                        for kk in range(2):
                            kt = 2 * u + kk
                            mm = pe.matmul(scores[at % 2][:, kk, :], kst[0:ROWS + 3, h, kt * P:(kt + 1) * P],
                                           qst[0:ROWS + 3, h, :], start=True, stop=not masked)
                            if masked:
                                mm = pe.matmul(scores[at % 2][:, kk, :], identb[:], biask[:, kt, :], start=False, stop=True)
                        mm.then_inc(s_full, 1)

                    def products(g, u):
                        if u == 0:
                            O.wait_free(pe, b, g)
                        pe.wait_ge(s_exp, b * G * UNITS + g * UNITS + 4 * u + 4)
                        for kk in range(2):
                            for j in range(4):
                                kt = 2 * u + kk
                                mm = pe.matmul(O.bank(g)[32 * j:32 * j + CW, :], v[:, kt, g, j, :],
                                               ex[:, (4 * u + j) % NE, kk * 512:(kk + 1) * 512],
                                               start=(kt == 0), stop=(kt == KT - 1), skip_group_check=True)
                        mm.then_inc(pv_s, 1)

                    A.wait_done(pe, b, 6)
                    pe.wait_ge(kin_s, 16 * 6 * (b + 1))
                    pe.wait_ge(qin_s, 16 * 6 * (b + 1))
                    for i in range(N_MAX):
                        fill_max(0, i)
                    fill_neg(0)
                    for g in range(G):
                        pe.wait_ge(nin_s, 48 * (b * G + g + 1))
                        for n in range(UNITS):
                            scores_of(g, n)
                            if g >= 1 and n == 3:
                                fill_sum(g - 1)
                            if g + 1 < G:
                                for i in range(3 * n, min(3 * n + 3, N_MAX)):
                                    fill_max(g + 1, i)
                                if n == 12:
                                    fill_neg(g + 1)
                            if n % 4 == 3 and n >= 7:
                                products(g, n // 4 - 1)
                        products(g, 3)
                    fill_sum(G - 1)
                    pe.wait_ge(at_s, b * G + G)
                    for q in range(QT):
                        at = vat["y", q]
                        V.wait_free(pe, b, at)
                        for g in range(G):
                            mm = pe.matmul(V.bank(at)[:, 0:D], aT[:, g, q * P:(q + 1) * P], wo[:, g, :],
                                           start=(g == 0), stop=(g == G - 1 and not biased))
                        if biased:
                            mm = pe.matmul(V.bank(at)[:, 0:D], ones[0:1, :], bo[:], start=False, stop=True)
                        mm.then_inc(V.full, 1)

            @block.scalar
            def _(act):
                act.wait_ge(w_in, 16 * len(loads))
                with act.Fori(0, B) as b:
                    V.wait_turns(act, b)
                    act.wait_ge(mv_s, b + 1)
                    act.activation(std[:], mv[:, :, 1], ACT.Sqrt, bias=eps[:]).then_inc(std_s, 1)
                    for m in range(DT):
                        for n in range(2):
                            A.wait_full(act, b, 2 * m + n)
                            act.activation(kf[:, m, n * 512:(n + 1) * 512], A.bank(2 * m + n), ACT.Identity,
                                           bias=bk[:, m:m + 1] if biased else 0.0).then_inc(A.free, 1)
                    A.wait_full(act, b, 4)
                    act.copy(xT[:, 0, :], A.bank(4)).then_inc(A.free, 1)
                    for m in range(DT):
                        A.wait_full(act, b, 5 + m)
                        act.activation(qf[:, m, :], A.bank(5 + m), ACT.Identity,
                                       bias=bq[:, m:m + 1] if biased else 0.0).then_inc(A.free, 1)

                    def take(g):
                        act.wait_ge(pv_s, 4 * (b * G + g + 1))
                        act.copy(osb[:, g % 2, :], O.bank(g)).then_inc(O.free, 1)

                    for g in range(G):
                        for n in range(UNITS):
                            at = g * UNITS + n
                            act.wait_ge(s_full, b * G * UNITS + at + 1)
                            if at >= NE:
                                act.wait_ge(pv_s, b * 4 * G + (at - NE) // 4 + 1)
                            act.activation(ex[:, n % NE, :], scores[at % 2], ACT.Exp, scale=scale).then_inc(s_exp, 1)
                            if g >= 1 and n == 1:
                                if g >= 3:
                                    act.wait_ge(at_s, b * G + g - 2)
                                take(g - 1)
                    take(G - 1)

            @block.vector
            def _(dve):
                if masked:
                    dve.wait_ge(w_in, 16 * len(loads))
                    dve.tensor_scalar(biasq[:], mraw[:], BIG, -BIG, ALU.mult, ALU.add).then_inc(mk_s, 1)
                    dve.tensor_reduce(any_[:], mraw[:], AX.X, ALU.max).then_inc(mk_s, 1)
                    for kt in range(KT):
                        dve.wait_ge(mk_full, kt + 1)
                        dve.tensor_copy(biask[:, kt, :], PS[:, kt % 4, :].bitcast(BF16)[:, 0:S]).then_inc(mk_s, 1)
                    dve.wait_ge(mk_s, 2 + KT)
                    dve.tensor_copy(anyb[:], any_[:, :, None].broadcast_to([P, QT, P])).then_inc(mk_s, 1)
                    dve.wait_ge(mk_full, KT + 1)
                    dve.tensor_copy(flag[:], PS[:, 4, :]).then_inc(mk_s, 1)
                    dve.wait_ge(mk_s, 2 + KT + 2)
                with dve.Fori(0, B) as b:
                    ch = Chain(dve, ch_s, b * N_CH)
                    V.wait_turns(dve, b)
                    split_wait(dve, K["passed"])
                    src = lambda k: X[:, ds(b * QT + k, 1), :]
                    for k in range(QT):
                        ch.mark(dve.bn_stats(st[:, k, :], src(k)))
                    ch.wait()
                    split_wait(dve, K["passed"])
                    for k in range(QT):
                        ins = dve.bn_aggr(mv[:, k, :], st[:, k, :])
                        if k < QT - 1:
                            ch.mark(ins)
                    ins.then_inc(mv_s, 1)
                    dve.wait_ge(mv_s, b + 1)
                    dve.wait_ge(std_s, b + 1)
                    ln_apply(dve, ch, src, mv, std, rstd, xn, xn_s)
                    for at, job in enumerate(vjobs):
                        if job[0] == "max" and job[2] == 0 and job[1] == 0:
                            A.wait_done(dve, b, 6)
                            dve.tensor_copy(qs[:, 0, :, :], qf[:]).then_inc(qsp_s, 1)
                            dve.wait_ge(qsp_s, 3 * b + 1)
                            ch.mark(dve.tensor_tensor(qr[:], qf[:], qs[:, 0, :, :], ALU.subtract))
                            ch.wait()
                            dve.tensor_copy(qs[:, 1, :, :], qr[:]).then_inc(qsp_s, 1)
                            dve.wait_ge(qsp_s, 3 * b + 2)
                            dve.tensor_tensor(qs[:, 2, :, :], qr[:], qs[:, 1, :, :], ALU.subtract).then_inc(qsp_s, 1)
                        if job[0] == "neg":
                            g = job[1]
                            V.wait_done(dve, b, at - 1)
                            ch.mark(dve.tensor_reduce(nm[:], mx[:], AX.X, ALU.max, negate=True))
                            ch.wait()
                            ch.mark(dve.tensor_copy(nsp[:, :, 0, :], nm[:]))
                            ch.wait()
                            ch.mark(dve.tensor_tensor(nr[:], nm[:], nsp[:, :, 0, :], ALU.subtract))
                            ch.wait()
                            ch.mark(dve.tensor_copy(nsp[:, :, 1, :], nr[:]))
                            ch.wait()
                            dve.tensor_tensor(nsp[:, :, 2, :], nr[:], nsp[:, :, 1, :], ALU.subtract).then_inc(nr_s, 1)
                        V.wait_full(dve, b, at)
                        o = V.bank(at)
                        if job[0] == "v":
                            for u in range(2):
                                ins = dve.tensor_copy(v[:, 2 * job[1] + u, :, :, 0:HD],
                                                      o[:, u * D:(u + 1) * D].rearrange("p (g j d) -> p g j d", g=G, j=4))
                            ins.then_inc(V.free, 1)
                        elif job[0] == "xT":
                            dve.tensor_copy(xT[:, 1, :], o).then_inc(V.free, 1)
                        elif job[0] == "max":
                            i = job[2]
                            j, q, n = i // (2 * QT), i // 2 % QT, i % 2
                            if masked:
                                split_wait(dve, K["passed"])
                                dve.tensor_tensor_reduce(o, o, biasq[:, q, n * 512:(n + 1) * 512], 1.0, -3e38,
                                                         ALU.add, ALU.max, mx[:, q, j, n:n + 1]).then_inc(V.free, 1)
                            else:
                                dve.reduce_max(mx[:, q, j, n:n + 1], o, AX.X).then_inc(V.free, 1)
                        elif job[0] == "neg":
                            if job[1]:
                                dve.wait_ge(nin_s, 48 * (b * G + job[1]))
                            dve.tensor_copy(nT[:], o.bitcast(BF16)[0:12, 0:S]).then_inc(nt_s, 1)
                            dve.wait_ge(nt_s, b * G + job[1] + 1)
                            dve.sem_inc(V.free, 1)
                        elif job[0] == "sum":
                            g = job[1]
                            if g:
                                dve.wait_ge(at_s, b * G + g)
                            ch.mark(dve.reciprocal(rc[:], o))
                            ch.wait()
                            dve.sem_inc(V.free, 1)
                            if masked:
                                ch.mark(dve.tensor_tensor(rc[:], rc[:], flag[:], ALU.mult))
                                ch.wait()
                            dve.tensor_tensor(aT[:, g, :], osb[:, g % 2, :], rc[:], ALU.mult).then_inc(at_s, 1)
                        else:
                            x = X[:, ds(b * QT + job[1], 1), :]
                            dve.tensor_tensor(x, x, o[:, None, 0:D], ALU.add).then_inc(V.free, 1)
                    assert ch.n == N_CH, ch.n


def experts(K, name, act_fn, by_expert):
    nc, t, sb, sem = (K[n] for n in ("nc", "t", "sb", "sem"))
    pre = name + "f_"
    names = {"L1": ("L1_ffn_router_w", "L1_ffn_w1", "L1_ffn_b1", "L1_ffn_w2", "L1_ffn_b2"),
             "L2": ("L2_ffn_gate_w", "L2_ffn_fc1s", "L2_ffn_b1s", "L2_ffn_fc2s", "L2_ffn_b2s"),
             "L3": ("L3_ffn_router_w", "L3_ffn_expert_w1", "L3_ffn_expert_b1", "L3_ffn_expert_w2", "L3_ffn_expert_b2")}[name]
    NB = NT if by_expert else 2 * NT + E
    table = nc.dram_tensor(pre + "table", (NT * P + P, D), F32, kind="Internal").ap()
    total = nc.dram_tensor(pre + "total", (NT * P + P, D), F32, kind="Internal").ap()
    with ExitStack() as c:
        M = {"pre": pre, "NB": NB, "by_expert": by_expert, "table": table, "total": total, "act_fn": act_fn,
             "t_r": t[names[0]], "t_w1": t[names[1]], "t_b1": t[names[2] + "_cols"], "t_w2": t[names[3]], "t_b2": t[names[4]]}
        M["w1"] = sb(c, pre + "w1", [P, E, DT, F]); M["w2"] = sb(c, pre + "w2", [P, E, FT, D])
        M["b1"] = sb(c, pre + "b1", [P, E, FT]); M["b2"] = sb(c, pre + "b2", [1, E, D])
        M["w_in"] = sem(pre + "weights_in")
        M["lnw"] = sb(c, pre + "lnw", [P, DT]); M["lnb"] = sb(c, pre + "lnb", [P, DT])
        M["index"] = sb(c, pre + "index", [P, NB], I32)
        M["slot_gate"] = sb(c, pre + "slot_gate", [P, NB])
        M["block_expert"] = sb(c, pre + "block_expert", [P, NB], I32)
        with ExitStack() as c2:
            gate = sb(c2, pre + "gate", [P, NT, E]); chosen = sb(c2, pre + "chosen", [P, NT, E])
            route(K, M, gate, chosen)
            if by_expert:
                choose_tokens(K, pre, gate, chosen)
            list_slots(K, M, gate, chosen)
        run_blocks(K, M)


def route(K, M, gate, chosen):
    nc, t, sb, sem, PS, X = (K[n] for n in ("nc", "t", "sb", "sem", "PS", "X"))
    ident, eps, ones = K["ident"], K["eps"], K["ones"]
    pre, by_expert, table, total = M["pre"], M["by_expert"], M["table"], M["total"]
    with ExitStack() as c:
        rw = sb(c, pre + "rw", [P, DT, E])
        xn = sb(c, pre + "xn", [P, QT, D]); xT = sb(c, pre + "xT", [P, DT, S])
        st = sb(c, pre + "st", [P, QT, 6]); mv = sb(c, pre + "mv", [P, QT, 2])
        std = sb(c, pre + "std", [P, QT]); rstd = sb(c, pre + "rstd", [P, QT])
        lg = sb(c, pre + "lg", [P, QT, E]); lm = sb(c, pre + "lm", [P, QT]); le = sb(c, pre + "le", [P, QT, E])
        ls = sb(c, pre + "ls", [P, QT]); zero = sb(c, pre + "zero", [P, D])
        if by_expert:
            st2 = sb(c, pre + "st2", [P, QT, 6]); mv2 = sb(c, pre + "mv2", [P, QT, 2])
            std2 = sb(c, pre + "std2", [P, QT]); rstd2 = sb(c, pre + "rstd2", [P, QT]); xn2 = sb(c, pre + "xn2", [P, QT, D])
        else:
            pb = sb(c, pre + "pb", [P, QT, E]); rank = sb(c, pre + "rank", [P, QT, E])
            gt = sb(c, pre + "gt", [P, QT, E, E]); eq = sb(c, pre + "eq", [P, QT, E, E]); first = sb(c, pre + "first", [P, QT, E, E])
        w_in, made, ch_s, std_s, mv_s, xn_s, lg_s, le_s, tab_s, end_s, st2_s, xn2_s, tot_s, zr_s = (sem(pre + n) for n in (
            "router_in", "order_made", "dve_chain", "std_ready", "var_ready", "xn_ready", "logits_shifted", "exp_ready",
            "table_stored", "gates_ready", "std2_ready", "xn2_ready", "total_stored", "zeros_made"))
        A = Ring([PS[:, 0, :], PS[:, 1, :]], sem(pre + "r_act_full"), sem(pre + "r_act_free"), 1)
        V = Ring([PS[:, 2, :], PS[:, 3, :], PS[:, 4, :]], sem(pre + "r_dve_full"), sem(pre + "r_dve_free"), 2)
        rows, rows_s = (xn2, xn2_s) if by_expert else (xn, xn_s)
        with nc.Block() as block:
            @block.sync
            def _(sp):
                sp.dma_start(rw[:], M["t_r"].rearrange("(k p) n -> p k n", p=P)).then_inc(w_in, 16)
                if by_expert:
                    sp.dma_start(M["lnw"][:], t["L2_ffn_ln_w_cols"]).then_inc(w_in, 16)
                    sp.dma_start(M["lnb"][:], t["L2_ffn_ln_b_cols"]).then_inc(w_in, 16)
                sp.dma_start(M["b1"][:], M["t_b1"].rearrange("e p k -> p e k")).then_inc(M["w_in"], 16)
                sp.dma_start(M["b2"][:], M["t_b2"].rearrange("(a e) n -> a e n", a=1)).then_inc(M["w_in"], 16)
                for e in range(E):
                    sp.dma_start(M["w1"][:, e, :, :], M["t_w1"][e].rearrange("(k p) n -> p k n", p=P)).then_inc(M["w_in"], 16)
                    sp.dma_start(M["w2"][:, e, :, :], M["t_w2"][e].rearrange("(k p) n -> p k n", p=P)).then_inc(M["w_in"], 16)
                sp.wait_ge(zr_s, 1)
                sp.dma_start(table[NT * P:NT * P + P, :], zero[:]).then_inc(tot_s, 16)
                sp.dma_start(total[NT * P:NT * P + P, :], zero[:]).then_inc(tot_s, 16)
                with sp.Fori(0, B) as b:
                    sp.wait_ge(rows_s, b * QT + QT)
                    sp.dma_start(table[ds(b * S, S), :].rearrange("(k p) d -> p k d", p=P), rows[:]).then_inc(tab_s, 16)
                sp.wait_ge(end_s, B + 1)
                sp.dma_start(total[0:NT * P, :].rearrange("(k p) d -> p k d", p=P), X[:]).then_inc(tot_s, 16)
                sp.wait_ge(tot_s, 48)
                sp.wait_ge(tab_s, 16 * (B + 1))

            @block.gpsimd
            def _(pool):
                A.start(pool)
                V.start(pool)
                pool.sem_inc(end_s, 1)
                pool.sem_inc(tab_s, 16)
                pool.memset(zero[:], 0.0).then_inc(zr_s, 1)
                if not by_expert:
                    pool.memset(eq[:], 1.0).then_inc(made, 1)
                    pool.wait_ge(made, 1)
                    pool.affine_select(out=first[:], in_=eq[:], compare_op=ALU.is_gt, fill=0.0, base=0,
                                       pattern=[[0, QT], [1, E], [-1, E]], channel_multiplier=0).then_inc(made, 1)

            @block.tensor
            def _(pe):
                pe.wait_ge(w_in, 48 if by_expert else 16)
                with pe.Fori(0, B) as b:
                    pe.wait_ge(xn_s, b * QT + QT)
                    for f, R in enumerate((A, V)):
                        for k in range(QT):
                            mm = pe.transpose(R.bank(0)[:, k * P:(k + 1) * P], xn[:, k, f * P:(f + 1) * P], ident[:])
                        mm.then_inc(R.full, 1)
                    A.wait_done(pe, b, 0)
                    V.wait_done(pe, b, 0)
                    for q in range(QT):
                        for k in range(DT):
                            mm = pe.matmul(V.bank(1)[:, q * E:(q + 1) * E], xT[:, k, q * P:(q + 1) * P], rw[:, k, :],
                                           start=(k == 0), stop=(k == DT - 1), skip_group_check=True)
                    mm.then_inc(V.full, 1)

            @block.scalar
            def _(act):
                with act.Fori(0, B) as b:
                    act.wait_ge(end_s, b + 1)
                    act.wait_ge(mv_s, b + 1)
                    act.activation(std[:], mv[:, :, 1], ACT.Sqrt, bias=eps[:]).then_inc(std_s, 1)
                    A.wait_full(act, b, 0)
                    act.copy(xT[:, 0, :], A.bank(0)).then_inc(A.free, 1)
                    if by_expert:
                        act.wait_ge(st2_s, 2 * b + 1)
                        act.activation(std2[:], mv2[:, :, 1], ACT.Sqrt, bias=eps[:]).then_inc(st2_s, 1)
                    act.wait_ge(lg_s, b + 1)
                    act.activation(le[:], lg[:], ACT.Exp).then_inc(le_s, 1)

            @block.vector
            def _(dve):
                if not by_expert:
                    dve.wait_ge(made, 2)
                N_CH = 2 * QT - 1 + 1 + 1 + 2 + (2 * QT - 1 + 1 + QT if by_expert else 11)
                with dve.Fori(0, B) as b:
                    ch = Chain(dve, ch_s, b * N_CH)
                    dve.wait_ge(end_s, b + 1)
                    dve.wait_ge(tab_s, 16 * b + 16)
                    split_wait(dve, K["passed"])
                    src = lambda k: X[:, ds(b * QT + k, 1), :]
                    for k in range(QT):
                        ch.mark(dve.bn_stats(st[:, k, :], src(k)))
                    ch.wait()
                    split_wait(dve, K["passed"])
                    for k in range(QT):
                        ins = dve.bn_aggr(mv[:, k, :], st[:, k, :])
                        if k < QT - 1:
                            ch.mark(ins)
                    ins.then_inc(mv_s, 1)
                    dve.wait_ge(mv_s, b + 1)
                    dve.wait_ge(std_s, b + 1)
                    ln_apply(dve, ch, src, mv, std, rstd, xn, xn_s)
                    if by_expert:
                        dve.wait_ge(xn_s, b * QT + QT)
                        split_wait(dve, K["passed"])
                        for k in range(QT):
                            ch.mark(dve.bn_stats(st2[:, k, :], xn[:, k, :]))
                        ch.wait()
                        split_wait(dve, K["passed"])
                        for k in range(QT):
                            ins = dve.bn_aggr(mv2[:, k, :], st2[:, k, :])
                            if k < QT - 1:
                                ch.mark(ins)
                        ins.then_inc(st2_s, 1)
                        dve.wait_ge(st2_s, 2 * b + 2)
                        ch.mark(dve.reciprocal(rstd2[:], std2[:]))
                        ch.wait()
                        for k in range(QT):
                            dve.tensor_scalar(xn2[:, k, :], xn[:, k, :], mv2[:, k, 0:1], rstd2[:, k:k + 1],
                                              ALU.subtract, ALU.mult).then_inc(xn2_s, 1)
                        for k in range(QT):
                            ch.mark(dve.tensor_tensor(src(k), src(k), xn[:, k:k + 1, :], ALU.add))
                    V.wait_full(dve, b, 0)
                    dve.tensor_copy(xT[:, 1, :], V.bank(0)).then_inc(V.free, 1)
                    V.wait_full(dve, b, 1)
                    o = V.bank(1)[:, 0:QT * E].rearrange("p (q e) -> p q e", q=QT)
                    ch.mark(dve.tensor_reduce(lm[:], o, AX.X, ALU.max))
                    ch.wait()
                    dve.tensor_tensor(lg[:], o, lm[:, :, None].broadcast_to([P, QT, E]), ALU.subtract).then_inc(lg_s, 1)
                    dve.wait_ge(lg_s, b + 1)
                    dve.sem_inc(V.free, 1)
                    dve.wait_ge(le_s, b + 1)
                    ch.mark(dve.tensor_reduce(ls[:], le[:], AX.X, ALU.add))
                    ch.wait()
                    ch.mark(dve.reciprocal(ls[:], ls[:]))
                    ch.wait()
                    lb = ls[:, :, None].broadcast_to([P, QT, E])
                    if by_expert:
                        dve.tensor_tensor(gate[:, ds(b * QT, QT), :], le[:], lb, ALU.mult).then_inc(end_s, 1)
                    else:
                        ch.mark(dve.tensor_tensor(pb[:], le[:], lb, ALU.mult))
                        ch.wait()
                        mine = pb[:, :, :, None].broadcast_to([P, QT, E, E])
                        other = pb[:, :, None, :].broadcast_to([P, QT, E, E])
                        ch.mark(dve.tensor_tensor(gt[:], other, mine, ALU.is_gt))
                        ch.mark(dve.tensor_tensor(eq[:], other, mine, ALU.is_equal))
                        ch.wait()
                        ch.mark(dve.tensor_tensor(eq[:], eq[:], first[:], ALU.mult))
                        ch.wait()
                        ch.mark(dve.tensor_tensor(gt[:], gt[:], eq[:], ALU.add))
                        ch.wait()
                        ch.mark(dve.tensor_reduce(rank[:], gt[:], AX.X, ALU.add))
                        ch.wait()
                        ch.mark(dve.tensor_scalar(chosen[:, ds(b * QT, QT), :], rank[:], 1.5, None, ALU.is_lt))
                        ch.mark(dve.scalar_tensor_tensor(out=pb[:], in0=rank[:], scalar=1.5, in1=pb[:], op0=ALU.is_lt, op1=ALU.mult))
                        ch.wait()
                        ch.mark(dve.tensor_reduce(lm[:], pb[:], AX.X, ALU.add))
                        ch.wait()
                        ch.mark(dve.tensor_scalar(lm[:], lm[:], 1e-9, None, ALU.add))
                        ch.wait()
                        ch.mark(dve.reciprocal(ls[:], lm[:]))
                        ch.wait()
                        dve.tensor_tensor(gate[:, ds(b * QT, QT), :], pb[:], lb, ALU.mult).then_inc(end_s, 1)
                    assert ch.n == N_CH, (ch.n, N_CH)


def list_slots(K, M, gate, chosen):
    nc, sb, sem, PS, ones = (K[n] for n in ("nc", "sb", "sem", "PS", "ones"))
    pre, NB = M["pre"], M["NB"]
    NF = 6
    with ExitStack() as c:
        low = sb(c, pre + "s_low", [P, P]); tot = sb(c, pre + "s_tot", [P, NT, E]); pos = sb(c, pre + "s_pos", [P, NT, E])
        posi = sb(c, pre + "s_posi", [P, NT, E], I32); rowi = sb(c, pre + "s_rowi", [P, NT, E], I32)
        row = sb(c, pre + "s_row", [P, NT, E]); blk = sb(c, pre + "s_blk", [P, NT, E]); cnt = sb(c, pre + "s_cnt", [P, E])
        step = sb(c, pre + "s_step", [P, E, NT]); over = sb(c, pre + "s_over", [P, E, NT]); nblk = sb(c, pre + "s_nblk", [P, E])
        start = sb(c, pre + "s_start", [P, E])
        iota_i = sb(c, pre + "s_iotai", [P, P], I32); iota_r = sb(c, pre + "s_iotar", [P, P]); part_i = sb(c, pre + "s_parti", [P, 1], I32)
        part = sb(c, pre + "s_part", [P, 1]); spare = sb(c, pre + "s_spare", [P, 1])
        fields = sb(c, pre + "s_fields", [P, NT, E, NF], BF16); g1 = sb(c, pre + "s_g1", [P, NT, E])
        H = E // 2
        oh_r = sb(c, pre + "s_ohr", [P, 2, H, P], BF16); oh_b = sb(c, pre + "s_ohb", [P, 2, H, NB], BF16)
        fb = sb(c, pre + "s_fb", [P, 2, H, NB * NF], BF16)
        res = sb(c, pre + "s_res", [P, NB, NF]); tok = sb(c, pre + "s_tok", [P, NB]); tok2 = sb(c, pre + "s_tok2", [P, NB])
        be = sb(c, pre + "s_be", [P, NB, E]); bs = sb(c, pre + "s_bs", [P, NB])
        made, ch_s, full, hot_s, res_s = (sem(pre + n) for n in ("s_made", "s_chain", "s_full", "s_onehots", "s_listed"))
        with nc.Block() as block:
            @block.gpsimd
            def _(pool):
                pool.affine_select(out=low[:], in_=ones[:], compare_op=ALU.is_gt, fill=0.0, base=0,
                                   pattern=[[1, P]], channel_multiplier=-1).then_inc(made, 1)
                pool.iota(iota_i[:], [[1, P]], base=0, channel_multiplier=0).then_inc(made, 1)
                pool.iota(part_i[:], [[0, 1]], base=0, channel_multiplier=1).then_inc(made, 1)

            @block.tensor
            def _(pe):
                pe.wait_ge(made, 3)
                flat = chosen[:].rearrange("p t e -> p (t e)")
                pe.matmul(PS[:, 1, 0:NT * E], low[:], flat, start=True, stop=True).then_inc(full, 1)
                pe.matmul(PS[:, 2, 0:NT * E], ones[:], flat, start=True, stop=True).then_inc(full, 1)
                for k in range(NT):
                    for h in range(2):
                        pe.wait_ge(hot_s, 2 * k + h + 1)
                        for e in range(H):
                            mm = pe.matmul(PS[:, 3, 0:NB * NF], oh_r[:, h, e, :], fb[:, h, e, :],
                                           start=(k == 0 and h == 0 and e == 0), stop=(k == NT - 1 and h == 1 and e == H - 1))
                        mm.then_inc(res_s, 1)

            @block.vector
            def _(dve):
                ch = Chain(dve, ch_s)

                def do(ins):
                    ch.mark(ins)
                    ch.wait()

                dve.wait_ge(made, 3)
                do(dve.tensor_copy(iota_r[:], iota_i[:]))
                do(dve.tensor_copy(part[:], part_i[:]))
                do(dve.tensor_scalar(spare[:], part[:], float(NT * P), None, ALU.add))
                do(dve.tensor_scalar(step[:], iota_r[:, None, 0:NT].broadcast_to([P, E, NT]), float(P), None, ALU.mult))
                dve.wait_ge(full, 2)
                do(dve.tensor_copy(tot[:].rearrange("p t e -> p (t e)"), PS[:, 2, 0:NT * E]))
                do(dve.memset(pos[:, 0, :], 0.0))
                for k in range(1, NT):
                    do(dve.tensor_tensor(pos[:, k, :], pos[:, k - 1, :], tot[:, k - 1, :], ALU.add))
                do(dve.tensor_tensor(cnt[:], pos[:, NT - 1, :], tot[:, NT - 1, :], ALU.add))
                do(dve.tensor_tensor(pos[:], pos[:], PS[:, 1, 0:NT * E].rearrange("p (t e) -> p t e", t=NT), ALU.add))
                do(dve.tensor_tensor(over[:], cnt[:, :, None].broadcast_to([P, E, NT]), step[:], ALU.is_gt))
                do(dve.tensor_reduce(nblk[:], over[:], AX.X, ALU.add))
                do(dve.memset(start[:, 0:1], 0.0))
                for e in range(1, E):
                    do(dve.tensor_tensor(start[:, e:e + 1], start[:, e - 1:e], nblk[:, e - 1:e], ALU.add))
                do(dve.tensor_copy(posi[:], pos[:]))
                do(dve.tensor_single_scalar(rowi[:], posi[:], P - 1, ALU.bitwise_and))
                do(dve.tensor_single_scalar(posi[:], posi[:], 7, ALU.arith_shift_right))
                do(dve.tensor_copy(row[:], rowi[:]))
                do(dve.tensor_copy(blk[:], posi[:]))
                do(dve.tensor_tensor(blk[:], blk[:], start[:, None, :].broadcast_to([P, NT, E]), ALU.add))
                do(dve.tensor_scalar(g1[:], chosen[:], -1000.0, 1000.0, ALU.mult, ALU.add))
                do(dve.tensor_tensor(row[:], row[:], g1[:], ALU.add))
                do(dve.tensor_copy(fields[:, :, :, 0], iota_r[:, 0:NT, None].broadcast_to([P, NT, E])))
                do(dve.tensor_copy(fields[:, :, :, 1], part[:, :, None].broadcast_to([P, NT, E])))
                do(dve.memset(fields[:, :, :, 2], 1.0))
                do(dve.tensor_copy(fields[:, :, :, 3], gate[:]))
                do(dve.tensor_tensor(g1[:], gate[:], fields[:, :, :, 3], ALU.subtract))
                do(dve.tensor_copy(fields[:, :, :, 4], g1[:]))
                do(dve.tensor_tensor(fields[:, :, :, 5], g1[:], fields[:, :, :, 4], ALU.subtract))
                do(dve.tensor_tensor(be[:], start[:, None, :].broadcast_to([P, NB, E]),
                                     iota_r[:, 0:NB, None].broadcast_to([P, NB, E]), ALU.is_le))
                do(dve.tensor_reduce(bs[:], be[:], AX.X, ALU.add))
                do(dve.tensor_scalar(bs[:], bs[:], -1.0, None, ALU.add))
                do(dve.tensor_copy(M["block_expert"][:], bs[:]))
                for k in range(NT):
                    for h in range(2):
                        es = slice(h * H, h * H + H)
                        if k >= 1:
                            dve.wait_ge(res_s, 2 * k + h - 1)
                        ch.mark(dve.tensor_tensor(oh_r[:, h, :, :], iota_r[:, None, :].broadcast_to([P, H, P]),
                                                  row[:, k, es, None].broadcast_to([P, H, P]), ALU.is_equal))
                        do(dve.tensor_tensor(oh_b[:, h, :, :], iota_r[:, None, 0:NB].broadcast_to([P, H, NB]),
                                             blk[:, k, es, None].broadcast_to([P, H, NB]), ALU.is_equal))
                        dve.tensor_tensor(fb[:, h, :, :].rearrange("p e (b f) -> p e b f", f=NF),
                                          oh_b[:, h, :, :, None].broadcast_to([P, H, NB, NF]),
                                          fields[:, k, es, None, :].broadcast_to([P, H, NB, NF]), ALU.mult).then_inc(hot_s, 1)
                dve.wait_ge(res_s, 2 * NT)
                do(dve.tensor_copy(res[:].rearrange("p b f -> p (b f)"), PS[:, 3, 0:NB * NF]))
                do(dve.scalar_tensor_tensor(out=tok[:], in0=res[:, :, 0], scalar=float(P), in1=res[:, :, 1], op0=ALU.mult, op1=ALU.add))
                do(dve.tensor_scalar(tok2[:], res[:, :, 2], -1.0, 1.0, ALU.mult, ALU.add))
                do(dve.scalar_tensor_tensor(out=tok[:], in0=tok2[:], scalar=spare[:], in1=tok[:], op0=ALU.mult, op1=ALU.add))
                do(dve.tensor_copy(M["index"][:], tok[:]))
                do(dve.tensor_tensor(tok[:], res[:, :, 3], res[:, :, 4], ALU.add))
                do(dve.tensor_tensor(M["slot_gate"][:], tok[:], res[:, :, 5], ALU.add))


def run_blocks(K, M):
    nc, t, sb, sem, PS, X, ident, ones = (K[n] for n in ("nc", "t", "sb", "sem", "PS", "X", "ident", "ones"))
    pre, NB, table, total, by_expert = M["pre"], M["NB"], M["table"], M["total"], M["by_expert"]
    w1, w2, b1, b2, index, sg, be = (M[n] for n in ("w1", "w2", "b1", "b2", "index", "slot_gate", "block_expert"))
    w1f = w1[:, :, :, :].rearrange("p e k n -> p (e k n)")
    w2f = w2[:, :, :, :].rearrange("p e k n -> p (e k n)")
    b1f = b1[:, :, :].rearrange("p e k -> p (e k)")
    b2f = b2[:, :, :].rearrange("p e n -> p (e n)")
    with ExitStack() as c:
        AHEAD = 4
        xg = sb(c, pre + "xg", [P, AHEAD, D]); xgT = sb(c, pre + "xgT", [P, 2, DT * P])
        hb = sb(c, pre + "hb", [P, F]); hT = sb(c, pre + "hT", [P, FT, P]); yo = sb(c, pre + "yo", [P, 2, D])
        ig = sb(c, pre + "ig", [P, AHEAD], I32); isc = sb(c, pre + "isc", [P, 2], I32)
        gathered = [sem(pre + "gathered%d" % n) for n in range(AHEAD)]
        (cp_s, sc_s, x_full, x_done, h_full, h_done, t_full, t_done, y_full, y_done, back) = (sem(pre + n) for n in (
            "index_copied", "added", "rows_turned", "rows_ready", "hidden_full", "hidden_ready",
            "hidden_turned", "activated", "output_full", "output_ready", "x_back"))
        X_BANK, H_BANK, T_BANK, Y_BANK = (0, 7), 1, 3, (5, 6)
        LOOPS = (NB - 2) // 2
        with nc.Block() as block:
            @block.gpsimd
            def _(pool):
                def gather(j, buf, n):
                    pool.tensor_copy(ig[:, buf:buf + 1], index[:, ds(j, 1)]).then_inc(cp_s, 1)
                    pool.wait_ge(cp_s, n + 1)
                    split_wait(pool, K["passed"])
                    pool.indirect_dma_start(xg[:, buf, :], None, table, bass.IndirectOffsetOnAxis(ap=ig[:, buf:buf + 1], axis=0),
                                            bounds_check=NT * P + P - 1).then_inc(gathered[buf], 16)

                def add(j, par, n, first=False):
                    pool.tensor_copy(isc[:, par:par + 1], index[:, ds(j, 1)]).then_inc(cp_s, 1)
                    pool.wait_ge(cp_s, n + 1)
                    pool.wait_ge(y_done, j + 1)
                    if not first:
                        pool.wait_ge(sc_s, 16 * j)
                    split_wait(pool, K["passed"])
                    pool.indirect_dma_start(total, bass.IndirectOffsetOnAxis(ap=isc[:, par:par + 1], axis=0), yo[:, par, :], None,
                                            bounds_check=NT * P + P - 1, compute_op=ALU.add).then_inc(sc_s, 16)

                def four(i, first=False):
                    for buf in range(AHEAD):
                        j = i * AHEAD + buf
                        pool.wait_ge(x_full, j + 1)
                        split_wait(pool, K["passed"])
                        gather(j + AHEAD, buf, j * 2 + AHEAD)
                        add(j, buf % 2, j * 2 + AHEAD + 1, first and buf == 0)

                for j in range(AHEAD):
                    gather(j, j, j)
                four(0, True)
                with pool.Fori(1, NB // AHEAD - 1) as i:
                    four(i)
                for j in range(NB - AHEAD, NB):
                    add(j, j % 2, NB + j)

            @block.sync
            def _(sp):
                sp.wait_ge(sc_s, 16 * NB)
                sp.dma_start(X[:], total[0:NT * P, :].rearrange("(k p) d -> p k d", p=P)).then_inc(back, 16)
                sp.wait_ge(back, 16)

            @block.tensor
            def _(pe):
                pe.wait_ge(M["w_in"], 16 * (2 + 2 * E))

                def turn_rows(j, u, n):
                    pe.wait_ge(gathered[u], 16 * n)
                    for f in range(DT):
                        mm = pe.transpose(PS[:, X_BANK[u % 2], f * P:(f + 1) * P], xg[:, u, f * P:(f + 1) * P], ident[:])
                    mm.then_inc(x_full, 1)

                def hidden(j, par):
                    e = pe.value_load(be[0:1, ds(j, 1)], min_val=0, max_val=E - 1)
                    pe.wait_ge(x_done, j + 1)
                    for n in range(2):
                        for k in range(DT):
                            mm = pe.matmul(PS[:, H_BANK + n, :], xgT[:, par, k * P:(k + 1) * P],
                                           w1f[:, ds(e * (DT * F) + k * F + n * 512, 512)], start=(k == 0), stop=(k == DT - 1))
                    mm.then_inc(h_full, 1)

                def outward(j, par):
                    e = pe.value_load(be[0:1, ds(j, 1)], min_val=0, max_val=E - 1)
                    pe.wait_ge(t_done, j + 1)
                    o = PS[:, Y_BANK[par], 0:D]
                    pe.matmul(o, ones[0:1, :], b2f[:, ds(e * D, D)], start=True, stop=False)
                    for k in range(FT):
                        mm = pe.matmul(o, hT[:, k, :], w2f[:, ds(e * (FT * D) + k * D, D)], start=False, stop=(k == FT - 1))
                    mm.then_inc(y_full, 1)

                def turn_hidden(j):
                    pe.wait_ge(h_done, j + 1)
                    for m in range(FT):
                        mm = pe.transpose(PS[:, T_BANK + m // 4, (m % 4) * P:(m % 4 + 1) * P], hb[:, m * P:(m + 1) * P], ident[:])
                    mm.then_inc(t_full, 1)

                def step(j, u, n):
                    pe.wait_ge(x_done, j)
                    turn_rows(j + 1, (u + 1) % AHEAD, n)
                    hidden(j, u % 2)
                    outward(j - 1, 1 - u % 2)
                    turn_hidden(j)

                turn_rows(0, 0, 1)
                turn_rows(1, 1, 1)
                hidden(0, 0)
                turn_hidden(0)
                with pe.Fori(0, NB // AHEAD - 1) as i:
                    for u in range(AHEAD):
                        step(i * AHEAD + u + 1, (u + 1) % AHEAD, i + (u + 2) // AHEAD + 1)
                for j in (NB - 3, NB - 2):
                    step(j, j % AHEAD, (j + 1) // AHEAD + 1)
                hidden(NB - 1, 1)
                outward(NB - 2, 0)
                turn_hidden(NB - 1)
                outward(NB - 1, 1)

            @block.scalar
            def _(act):
                def activate(j):
                    e = act.value_load(be[0:1, ds(j, 1)], min_val=0, max_val=E - 1)
                    act.wait_ge(t_full, j + 1)
                    split_wait(act, K["passed"])
                    for m in range(FT):
                        ins = act.activation(hT[:, m, :], PS[:, T_BANK + m // 4, (m % 4) * P:(m % 4 + 1) * P], M["act_fn"],
                                             bias=b1f[:, ds(e * FT + m, 1)])
                    ins.then_inc(t_done, 1)

                activate(0)
                with act.Fori(0, LOOPS) as i:
                    activate(i * 2 + 1)
                    activate(i * 2 + 2)
                activate(NB - 1)

            @block.vector
            def _(dve):
                def rows(j, par):
                    dve.wait_ge(x_full, j + 1)
                    if by_expert:
                        for f in range(DT):
                            ins = dve.tensor_scalar(xgT[:, par, f * P:(f + 1) * P], PS[:, X_BANK[par], f * P:(f + 1) * P],
                                                    M["lnw"][:, f:f + 1], M["lnb"][:, f:f + 1], ALU.mult, ALU.add)
                    else:
                        ins = dve.tensor_copy(xgT[:, par, :], PS[:, X_BANK[par], 0:D])
                    ins.then_inc(x_done, 1)

                def hidden(j):
                    dve.wait_ge(h_full, j + 1)
                    dve.tensor_copy(hb[:].rearrange("p (b n) -> p b n", b=2), PS[:, H_BANK:H_BANK + 2, :]).then_inc(h_done, 1)

                def weigh(j, par, first=False):
                    dve.wait_ge(y_full, j + 1)
                    if not first:
                        dve.wait_ge(sc_s, 16 * j - 16)
                    split_wait(dve, K["passed"])
                    dve.tensor_scalar(yo[:, par, :], PS[:, Y_BANK[par], 0:D], sg[:, ds(j, 1)], None, ALU.mult).then_inc(y_done, 1)

                rows(0, 0)
                rows(1, 1)
                hidden(0)

                def pair(i, first=False):
                    for j, par in ((i * 2 + 1, 1), (i * 2 + 2, 0)):
                        dve.wait_ge(h_full, j)
                        rows(j + 1, 1 - par)
                        dve.wait_ge(t_full, j)
                        hidden(j)
                        weigh(j - 1, 1 - par, first)

                pair(0, True)
                with dve.Fori(1, LOOPS) as i:
                    pair(i)
                hidden(NB - 1)
                weigh(NB - 2, 0)
                weigh(NB - 1, 1)


def choose_tokens(K, pre, gate, chosen):
    nc, sb, sem, PS, ones = (K[n] for n in ("nc", "sb", "sem", "PS", "ones"))
    KEEP = NT * P // E
    with ExitStack() as c:
        thr = sb(c, pre + "thr", [P, E]); bit = sb(c, pre + "bit", [P, E], I32); cand = sb(c, pre + "cand", [P, E])
        ge = sb(c, pre + "ge", [P, NT, E]); cnt = sb(c, pre + "cnt", [P, E]); ok = sb(c, pre + "ok", [P, E])
        above = sb(c, pre + "above", [P, NT, E]); tie = sb(c, pre + "tie", [P, NT, E]); need = sb(c, pre + "need", [P, E])
        seen = sb(c, pre + "seen", [P, NT, E]); tot = sb(c, pre + "tot", [P, NT, E]); low = sb(c, pre + "low", [P, P])
        ch_s, cnt_s, sum_s, made = (sem(pre + n) for n in ("c_chain", "count_ready", "count_summed", "c_made"))
        BITS = 30
        PER = 6
        with nc.Block() as block:
            @block.gpsimd
            def _(pool):
                pool.affine_select(out=low[:], in_=ones[:], compare_op=ALU.is_gt, fill=0.0, base=0,
                                   pattern=[[1, P]], channel_multiplier=-1).then_inc(made, 1)

            @block.tensor
            def _(pe):
                with pe.Fori(0, BITS) as i:
                    pe.wait_ge(cnt_s, i + 1)
                    pe.matmul(PS[:, 0, 0:E], ones[:], cnt[:], start=True, stop=True).then_inc(sum_s, 1)
                pe.wait_ge(cnt_s, BITS + 1)
                pe.matmul(PS[:, 0, 0:E], ones[:], cnt[:], start=True, stop=True).then_inc(sum_s, 1)
                pe.wait_ge(cnt_s, BITS + 2)
                pe.wait_ge(made, 1)
                pe.matmul(PS[:, 1, 0:NT * E], low[:], tie[:].rearrange("p t e -> p (t e)"), start=True, stop=True).then_inc(sum_s, 1)
                pe.matmul(PS[:, 2, 0:NT * E], ones[:], tie[:].rearrange("p t e -> p (t e)"), start=True, stop=True).then_inc(sum_s, 1)

            @block.vector
            def _(dve):
                spread = lambda a: a[:, None, :].broadcast_to([P, NT, E])
                dve.memset(thr[:], 0.0).then_inc(ch_s, 1)
                dve.memset(bit[:], 1 << (BITS - 1)).then_inc(ch_s, 1)
                dve.wait_ge(ch_s, 2)
                with dve.Fori(0, BITS) as i:
                    ch = Chain(dve, ch_s, i * PER + 2)
                    ch.mark(dve.tensor_tensor(cand[:].bitcast(I32), thr[:].bitcast(I32), bit[:], ALU.bitwise_or))
                    ch.wait()
                    ch.mark(dve.tensor_tensor(ge[:], gate[:], spread(cand), ALU.is_ge))
                    ch.mark(dve.tensor_single_scalar(bit[:], bit[:], 1, ALU.logical_shift_right))
                    ch.wait()
                    dve.tensor_reduce(cnt[:], ge[:].rearrange("p t e -> p e t"), AX.X, ALU.add).then_inc(cnt_s, 1)
                    dve.wait_ge(sum_s, i + 1)
                    ch.mark(dve.tensor_scalar(ok[:], PS[:, 0, 0:E], KEEP - 0.5, None, ALU.is_ge))
                    ch.wait()
                    ch.mark(dve.tensor_tensor(cand[:], cand[:], ok[:], ALU.mult))
                    ch.wait()
                    ch.mark(dve.tensor_tensor(thr[:], thr[:], cand[:], ALU.max))
                    ch.wait()
                    assert ch.n == PER, ch.n
                ch = Chain(dve, ch_s, 2 + PER * BITS)
                ch.wait()
                ch.mark(dve.tensor_tensor(above[:], gate[:], spread(thr), ALU.is_gt))
                ch.mark(dve.tensor_tensor(tie[:], gate[:], spread(thr), ALU.is_equal))
                ch.wait()
                dve.tensor_reduce(cnt[:], above[:].rearrange("p t e -> p e t"), AX.X, ALU.add).then_inc(cnt_s, 2)
                dve.wait_ge(sum_s, BITS + 1)
                ch.mark(dve.tensor_scalar(need[:], PS[:, 0, 0:E], -1.0, float(KEEP), ALU.mult, ALU.add))
                dve.wait_ge(sum_s, BITS + 3)
                ch.mark(dve.tensor_copy(tot[:].rearrange("p t e -> p (t e)"), PS[:, 2, 0:NT * E]))
                ch.mark(dve.memset(seen[:, 0, :], 0.0))
                ch.wait()
                for k in range(1, NT):
                    ch.mark(dve.tensor_tensor(seen[:, k, :], seen[:, k - 1, :], tot[:, k - 1, :], ALU.add))
                    ch.wait()
                ch.mark(dve.tensor_tensor(seen[:], seen[:], PS[:, 1, 0:NT * E].rearrange("p (t e) -> p t e", t=NT), ALU.add))
                ch.wait()
                ch.mark(dve.tensor_tensor(seen[:], seen[:], spread(need), ALU.is_lt))
                ch.wait()
                ch.mark(dve.tensor_tensor(tie[:], tie[:], seen[:], ALU.mult))
                ch.wait()
                ch.mark(dve.tensor_tensor(chosen[:], above[:], tie[:], ALU.add))
                ch.wait()


def causal_attention(K):
    nc, t, sb, sem, PS, X, ctxT = (K[n] for n in ("nc", "t", "sb", "sem", "PS", "X", "ctxT"))
    ident, ones, eps = K["ident"], K["ones"], K["eps"]
    HD = 64
    M = H * HD // P
    SCALE = HD ** -0.5
    pre = "L3a_"
    ajobs = [("k", m) for m in range(M)] + [("xT",)] + [("q", m) for m in range(M)]
    vjobs = [("v", k, n) for k in range(QT) for n in range(2)] + [("xT",)]
    for h in range(H):
        ajobs += [("turn", h, q) for q in (1, 3)]
        vjobs += [("turn", h, q) for q in (0, 2)]
        if h % 2:
            vjobs += [("out", h // 2)]
    vjobs += [("y", q) for q in range(QT)]
    aat = {j: i for i, j in enumerate(ajobs)}
    vat = {j: i for i, j in enumerate(vjobs)}
    with ExitStack() as c:
        wq = sb(c, pre + "wq", [P, DT, H * HD]); wk = sb(c, pre + "wk", [P, DT, H * HD]); wv = sb(c, pre + "wv", [P, DT, H * HD])
        wo = sb(c, pre + "wo", [P, M, D])
        cb = sb(c, pre + "cb", [P, DT, S])
        xn = sb(c, pre + "xn", [P, QT, D]); xT = sb(c, pre + "xT", [P, DT, S])
        qT = sb(c, pre + "qT", [P, M, S]); kT = sb(c, pre + "kT", [P, M, S]); v = sb(c, pre + "v", [P, QT, H * HD])
        keep = sb(c, pre + "keep", [P, S]); padi = sb(c, pre + "padi", [1, S], I32); padf = sb(c, pre + "padf", [1, S])
        bias = sb(c, pre + "bias", [P, QT, S], BF16); seen = sb(c, pre + "seen", [P, QT]); vis = sb(c, pre + "vis", [P, QT, S], BF16)
        causal = sb(c, pre + "causal", [P, QT, S], BF16)
        sm = sb(c, pre + "sm", [P, 4, S]); pT = sb(c, pre + "pT", [P, 2, QT, S])
        nmx = sb(c, pre + "nmx", [P, 4]); mx = sb(c, pre + "mx", [P, 4]); su = sb(c, pre + "su", [P, 4]); rs = sb(c, pre + "rs", [P, 4])
        aT = sb(c, pre + "aT", [P, M, S])
        st = sb(c, pre + "st", [P, QT, 6]); mv = sb(c, pre + "mv", [P, QT, 2])
        std = sb(c, pre + "std", [P, QT]); rstd = sb(c, pre + "rstd", [P, QT])
        (w_in, made, ch_s, std_s, mv_s, xn_s, cb_s, pad_s, padf_s, keep_s, bias_s, s_full, mx_s, s_free, exp_s, pn_s) = (
            sem(pre + n) for n in ("weights_in", "constants_made", "dve_chain", "std_ready", "var_ready", "xn_ready",
                                   "ctx_copied", "pad_in", "pad_ready", "keep_full", "bias_ready", "scores_full",
                                   "max_ready", "scores_read", "exp_done", "probs_scaled"))
        A = Ring([PS[:, 0, :], PS[:, 1, :]], sem(pre + "act_full"), sem(pre + "act_free"), len(ajobs))
        V = Ring([PS[:, 2, :], PS[:, 3, :]], sem(pre + "dve_full"), sem(pre + "dve_free"), len(vjobs))
        scores = [PS[:, 4 + i, :] for i in range(3)]
        keepbank = PS[:, 7, :]
        with nc.Block() as block:
            @block.sync
            def _(sp):
                for dst, src in ((wq, t["L3_xattn_Wq"]), (wk, t["L3_xattn_Wk"]), (wv, t["L3_xattn_Wv"]), (wo, t["L3_xattn_Wo"])):
                    sp.dma_start(dst[:], src.rearrange("(k p) n -> p k n", p=P)).then_inc(w_in, 16)
                with sp.Fori(0, B) as b:
                    V.wait_turns(sp, b)
                    sp.dma_start(padi[:], t["mask_BxS2_if1"][ds(b, 1), 0:S]).then_inc(pad_s, 16)

            @block.gpsimd
            def _(pool):
                A.start(pool)
                V.start(pool)
                pool.memset(vis[:], 1.0).then_inc(made, 1)
                pool.wait_ge(made, 1)
                pool.affine_select(out=causal[:], in_=vis[:], compare_op=ALU.is_ge, fill=0.0, base=0,
                                   pattern=[[P, QT], [-1, S]], channel_multiplier=1).then_inc(made, 1)
                with pool.Fori(0, B) as b:
                    V.wait_turns(pool, b)
                    split_wait(pool, K["passed"])
                    pool.tensor_copy(cb[:], ctxT[:, :, ds(b * SK, S)]).then_inc(cb_s, 1)

            @block.tensor
            def _(pe):
                pe.wait_ge(w_in, 64)
                with pe.Fori(0, B) as b:
                    V.wait_turns(pe, b)
                    pe.wait_ge(cb_s, b + 1)
                    for m in range(M):
                        at = aat["k", m]
                        A.wait_free(pe, b, at)
                        for k in range(DT):
                            mm = pe.matmul(A.bank(at), wk[:, k, m * P:(m + 1) * P], cb[:, k, :], start=(k == 0), stop=(k == DT - 1))
                        mm.then_inc(A.full, 1)
                    pe.wait_ge(padf_s, b + 1)
                    pe.matmul(keepbank, ones[0:1, :], padf[:], start=True, stop=True).then_inc(keep_s, 1)
                    for kt in range(QT):
                        for n in range(2):
                            at = vat["v", kt, n]
                            V.wait_free(pe, b, at)
                            for k in range(DT):
                                mm = pe.matmul(V.bank(at), cb[:, k, kt * P:(kt + 1) * P], wv[:, k, n * 512:(n + 1) * 512],
                                               start=(k == 0), stop=(k == DT - 1))
                            mm.then_inc(V.full, 1)
                    pe.wait_ge(xn_s, b * QT + QT)
                    for f, (R, i) in enumerate(((A, aat["xT",]), (V, vat["xT",]))):
                        R.wait_free(pe, b, i)
                        for k in range(QT):
                            mm = pe.transpose(R.bank(i)[:, k * P:(k + 1) * P], xn[:, k, f * P:(f + 1) * P], ident[:])
                        mm.then_inc(R.full, 1)
                    A.wait_done(pe, b, aat["xT",])
                    V.wait_done(pe, b, vat["xT",])
                    for m in range(M):
                        at = aat["q", m]
                        A.wait_free(pe, b, at)
                        for k in range(DT):
                            mm = pe.matmul(A.bank(at), wq[:, k, m * P:(m + 1) * P], xT[:, k, :], start=(k == 0), stop=(k == DT - 1))
                        mm.then_inc(A.full, 1)
                    A.wait_done(pe, b, aat["q", M - 1])

                    def score(h, q):
                        at = h * QT + q
                        if at >= 3:
                            pe.wait_ge(s_free, b * H * QT + at - 2)
                        p0, n = HD * (h % 2), (q + 1) * P
                        pe.matmul(scores[at % 3][:, 0:n], qT[p0:p0 + HD, h // 2, q * P:(q + 1) * P], kT[p0:p0 + HD, h // 2, 0:n],
                                  start=True, stop=True).then_inc(s_full, 1)

                    def turn(h, q):
                        R, at = (A, aat["turn", h, q]) if q % 2 else (V, vat["turn", h, q])
                        R.wait_free(pe, b, at)
                        pe.wait_ge(pn_s, b * H * QT + h * QT + q + 1)
                        for k in range(q + 1):
                            mm = pe.transpose(R.bank(at)[:, k * P:(k + 1) * P], sm[:, q, k * P:(k + 1) * P], ident[:])
                        mm.then_inc(R.full, 1)

                    def product(h):
                        at = vat["out", h // 2]
                        if h % 2 == 0:
                            V.wait_free(pe, b, at)
                        A.wait_done(pe, b, aat["turn", h, 3])
                        V.wait_done(pe, b, vat["turn", h, 2])
                        p0 = HD * (h % 2)
                        for k in range(QT):
                            mm = pe.matmul(V.bank(at)[p0:p0 + HD, k * P:S], v[:, k, h * HD:(h + 1) * HD],
                                           pT[:, h % 2, k, k * P:S], start=(k == 0), stop=(k == QT - 1), skip_group_check=True)
                        if h % 2:
                            mm.then_inc(V.full, 1)

                    for h in range(H + 1):
                        for q in range(QT):
                            if h < H:
                                score(h, q)
                            if h >= 1:
                                turn(h - 1, q)
                        if h >= 2 and h % 2 == 0:
                            product(h - 2)
                            product(h - 1)
                    for q in range(QT):
                        at = vat["y", q]
                        V.wait_free(pe, b, at)
                        V.wait_done(pe, b, vat["out", M - 1])
                        for m in range(M):
                            mm = pe.matmul(V.bank(at)[:, 0:D], aT[:, m, q * P:(q + 1) * P], wo[:, m, :],
                                           start=(m == 0), stop=(m == M - 1))
                        mm.then_inc(V.full, 1)

            @block.scalar
            def _(act):
                with act.Fori(0, B) as b:
                    V.wait_turns(act, b)
                    act.wait_ge(mv_s, b + 1)
                    act.activation(std[:], mv[:, :, 1], ACT.Sqrt, bias=eps[:]).then_inc(std_s, 1)

                    def empty(job, dst, src=lambda o: o):
                        A.wait_full(act, b, aat[job])
                        act.copy(dst, src(A.bank(aat[job]))).then_inc(A.free, 1)

                    for m in range(M):
                        empty(("k", m), kT[:, m, :])
                    empty(("xT",), xT[:, 0, :])
                    for m in range(M):
                        empty(("q", m), qT[:, m, :])
                    for h in range(H + 1):
                        for q in range(QT):
                            if h < H:
                                n, at = (q + 1) * P, h * QT + q
                                act.wait_ge(mx_s, b * H * QT + at + 1)
                                act.activation(sm[:, q, 0:n], sm[:, q, 0:n], ACT.Exp, bias=nmx[:, q:q + 1], scale=SCALE,
                                               accum_out=su[:, q:q + 1]).then_inc(exp_s, 1)
                            if h >= 1 and q % 2:
                                if h >= 3:
                                    V.wait_done(act, b, vat["out", (h - 3) // 2])
                                empty(("turn", h - 1, q), pT[:, (h - 1) % 2, 0:q + 1, q * P:(q + 1) * P],
                                      lambda o: o[:, 0:(q + 1) * P].rearrange("p (k n) -> p k n", n=P))

            @block.vector
            def _(dve):
                dve.wait_ge(made, 2)
                N_CH = 2 * QT - 1 + 1 + 3 + H * QT * 4
                with dve.Fori(0, B) as b:
                    ch = Chain(dve, ch_s, b * N_CH)
                    V.wait_turns(dve, b)
                    split_wait(dve, K["passed"])
                    src = lambda k: X[:, ds(b * QT + k, 1), :]
                    for k in range(QT):
                        ch.mark(dve.bn_stats(st[:, k, :], src(k)))
                    ch.wait()
                    split_wait(dve, K["passed"])
                    for k in range(QT):
                        ins = dve.bn_aggr(mv[:, k, :], st[:, k, :])
                        if k < QT - 1:
                            ch.mark(ins)
                    ins.then_inc(mv_s, 1)
                    dve.wait_ge(mv_s, b + 1)
                    dve.wait_ge(std_s, b + 1)
                    ln_apply(dve, ch, src, mv, std, rstd, xn, xn_s)
                    dve.wait_ge(pad_s, 16 * b + 16)
                    dve.tensor_scalar(padf[:], padi[:], 0.0, None, ALU.not_equal).then_inc(padf_s, 1)
                    dve.wait_ge(keep_s, b + 1)
                    ch.mark(dve.tensor_copy(keep[:], keepbank))
                    ch.wait()
                    ch.mark(dve.tensor_tensor(vis[:], causal[:], keep[:, None, :].broadcast_to([P, QT, S]), ALU.mult))
                    ch.wait()
                    ch.mark(dve.tensor_reduce(seen[:], vis[:], AX.X, ALU.max))
                    dve.tensor_scalar(bias[:], vis[:], BIG, -BIG, ALU.mult, ALU.add).then_inc(bias_s, 1)

                    def empty(job, dst, src=lambda o: o):
                        V.wait_full(dve, b, vat[job])
                        dve.tensor_copy(dst, src(V.bank(vat[job]))).then_inc(V.free, 1)

                    for k in range(QT):
                        for n in range(2):
                            empty(("v", k, n), v[:, k, n * 512:(n + 1) * 512])
                    empty(("xT",), xT[:, 1, :])
                    dve.wait_ge(bias_s, b + 1)

                    def largest(h, q):
                        n, at = (q + 1) * P, h * QT + q
                        dve.wait_ge(s_full, b * H * QT + at + 1)
                        if h >= 1:
                            (A if q % 2 else V).wait_full(dve, b, (aat if q % 2 else vat)["turn", h - 1, q])
                        split_wait(dve, K["passed"])
                        dve.tensor_tensor_reduce(sm[:, q, 0:n], scores[at % 3][:, 0:n], bias[:, q, 0:n], 1.0, -3e38,
                                                 ALU.add, ALU.max, mx[:, q:q + 1]).then_inc(s_free, 1)
                        dve.wait_ge(s_free, b * H * QT + at + 1)
                        dve.tensor_scalar(nmx[:, q:q + 1], mx[:, q:q + 1], -SCALE, None, ALU.mult).then_inc(mx_s, 1)

                    def scale(h, q):
                        n, at = (q + 1) * P, h * QT + q
                        dve.wait_ge(exp_s, b * H * QT + at + 1)
                        ch.mark(dve.tensor_tensor(rs[:, q:q + 1], su[:, q:q + 1], seen[:, q:q + 1], ALU.mult))
                        ch.wait()
                        ch.mark(dve.reciprocal(rs[:, q:q + 1], rs[:, q:q + 1]))
                        ch.wait()
                        ch.mark(dve.tensor_tensor(rs[:, q:q + 1], rs[:, q:q + 1], seen[:, q:q + 1], ALU.mult))
                        ch.wait()
                        ch.mark(dve.tensor_scalar(sm[:, q, 0:n], sm[:, q, 0:n], rs[:, q:q + 1], None, ALU.mult))
                        ch.wait()
                        dve.sem_inc(pn_s, 1)

                    for h in range(H + 1):
                        for q in range(QT):
                            if h < H:
                                largest(h, q)
                            if h >= 1 and q % 2 == 0:
                                if h >= 3:
                                    V.wait_done(dve, b, vat["out", (h - 3) // 2])
                                empty(("turn", h - 1, q), pT[:, (h - 1) % 2, 0:q + 1, q * P:(q + 1) * P],
                                      lambda o: o[:, 0:(q + 1) * P].rearrange("p (k n) -> p k n", n=P))
                            if h < H:
                                if q >= 1:
                                    scale(h, q - 1)
                        if h < H:
                            scale(h, QT - 1)
                        if h >= 2 and h % 2 == 0:
                            empty(("out", h // 2 - 1), aT[:, h // 2 - 1, :])
                    for q in range(QT):
                        V.wait_full(dve, b, vat["y", q])
                        x = X[:, ds(b * QT + q, 1), :]
                        dve.tensor_tensor(x, x, V.bank(vat["y", q])[:, None, 0:D], ALU.add).then_inc(V.free, 1)
                    assert ch.n == N_CH, ch.n


_OUTS = [((4, 512, 256), 'float32')]
_SWAPPED = ("L1_xattn_Wq", "L1_xattn_Wk", "L1_xattn_Wv", "L1_xattn_Wo", "L2_xattn_Wq", "L2_xattn_Wk",
            "L2_xattn_Wv", "L2_xattn_Wo", "L1_ffn_router_w", "L1_ffn_w1", "L1_ffn_w2", "L2_ffn_gate_w",
            "L2_ffn_fc1s", "L2_ffn_fc2s", "L3_ffn_router_w", "L3_ffn_expert_w1", "L3_ffn_expert_w2")
_COLUMNS = ("L0_xattn_b_kv", "L0_xattn_b_q", "L0_xattn_b1", "L0_ffn_cn_b1", "L0_ffn_cn_b2", "L0_ffn_gc_b1",
            "L1_xattn_bq", "L1_xattn_bk", "L1_ffn_b1", "L2_ffn_ln_w", "L2_ffn_ln_b", "L2_ffn_b1s", "L3_ffn_expert_b1")


def kernel(**inputs):
    import numpy as _np
    import concourse.bacc as _bacc
    from concourse import mybir as _mybir
    from concourse.bass_utils import run_bass_kernel_spmd as _run

    nc = _bacc.Bacc("TRN2", target_bir_lowering=False, num_devices=1)
    arrays, args = {}, {}
    for name in inputs:
        a = _np.asarray(inputs[name])
        if name in _SWAPPED:
            a = _np.swapaxes(a, -1, -2)
        a = _np.ascontiguousarray(a)
        laid = {name: a}
        if name in _COLUMNS:
            laid[name + "_cols"] = _np.ascontiguousarray(_np.swapaxes(a.reshape(*a.shape[:-1], -1, 128), -1, -2))
        for key, a in laid.items():
            arrays[f"in_{key}_dram"] = a
            args[key] = nc.dram_tensor(f"in_{key}_dram", a.shape, _mybir.dt.from_np(a.dtype), kind="ExternalInput").ap()
    outs = []
    for i, (shape, dtype) in enumerate(_OUTS):
        dt = _mybir.dt.from_np(_np.dtype(dtype))
        outs.append(nc.dram_tensor(f"out_{i}_dram", shape, dt, kind="ExternalOutput").ap())
    program(nc, args, outs[0], STAGES)
    r = _run(nc, [arrays], core_ids=[0])
    return r.results[0]["out_0_dram"]


STAGES = range(8)
```

```python
from contextlib import ExitStack

import concourse.bass as bass
from concourse import mybir

F32 = mybir.dt.float32
BF16 = mybir.dt.bfloat16
I32 = mybir.dt.int32
U8 = mybir.dt.uint8
ACT = mybir.ActivationFunctionType
ALU = mybir.AluOpType
AX = mybir.AxisListType
ds = bass.ds

P = 128
B = 4
S = 512
SK = 1024
D = 256
DT = D // P
QT = S // P
KT = SK // P
NT = B * QT
F = 1024
FT = F // P
E = 8
H = 16
LN_EPS = 1e-5
BIG = 2.0 ** 30


class Chain:

    def __init__(self, eng, sem, base=0):
        self.eng, self.sem, self.base, self.n = eng, sem, base, 0

    def mark(self, ins):
        ins.then_inc(self.sem, 1)
        self.n += 1
        return self.n

    def wait(self, k=None):
        self.eng.wait_ge(self.sem, self.base + (self.n if k is None else k))


class Ring:

    def __init__(self, banks, full, free, per):
        self.banks, self.full, self.free, self.per = banks, full, free, per

    def start(self, eng):
        eng.sem_inc(self.free, 1)

    def bank(self, n):
        return self.banks[n % len(self.banks)]

    def wait_turns(self, eng, b):
        eng.wait_ge(self.free, b * self.per + 1)

    def wait_free(self, pe, b, n):
        if n >= len(self.banks):
            pe.wait_ge(self.free, b * self.per + n - len(self.banks) + 2)

    def wait_full(self, eng, b, n):
        eng.wait_ge(self.full, b * self.per + n + 1)

    def wait_done(self, eng, b, n):
        eng.wait_ge(self.free, b * self.per + n + 2)


def split_wait(eng, sem):
    eng.sem_inc(sem, 1)


def program(nc, t, out, stages):
    ctx = ExitStack()
    with ctx:
        def sb(c, name, shape, dt=F32):
            return c.enter_context(nc.sbuf_tensor(name, shape, dt))

        taken = []

        def sem(name):
            taken.append(nc.alloc_semaphore(name))
            return taken[-1]

        def end_layer():
            nc.clear_and_free_semaphores(taken)
            taken.clear()
            nc.all_engine_barrier()

        K = {"nc": nc, "t": t, "sb": sb, "sem": sem}
        K["PS"] = ctx.enter_context(nc.psum_tensor("PS", [P, 8, 512], F32))
        K["X"] = sb(ctx, "X", [P, NT, D])
        K["ctxT"] = sb(ctx, "ctxT", [P, DT, B * SK])
        K["ident"] = sb(ctx, "ident", [P, P])
        K["identb"] = sb(ctx, "identb", [P, P], BF16)
        K["ones"] = sb(ctx, "ones", [P, P])
        K["eps"] = sb(ctx, "eps", [P, 1])
        K["passed"] = nc.alloc_semaphore("waits_passed")
        load_stage(K)
        layers = (lambda: single_head_attention(K),
                  lambda: coupled_ffn(K),
                  lambda: head_attention(K, "L1", 1.0 / 16.0, True, False),
                  lambda: experts(K, "L1", ACT.Relu, False),
                  lambda: head_attention(K, "L2", 0.25, False, True),
                  lambda: experts(K, "L2", ACT.Gelu_apprx_tanh, True),
                  lambda: causal_attention(K),
                  lambda: experts(K, "L3", ACT.Gelu, False))
        for i in stages:
            layers[i]()
            end_layer()
        store_stage(K, out)


def load_stage(K):
    nc, t, sb, sem, PS = K["nc"], K["t"], K["sb"], K["sem"], K["PS"]
    X, ctxT, ident, identb, ones, eps = (K[n] for n in ("X", "ctxT", "ident", "identb", "ones", "eps"))
    with ExitStack() as c:
        raw = sb(c, "ctx_raw", [P, B * KT, D])
        x_in, ctx_in, made, idm, turned, moved, movedv = (sem(n) for n in (
            "x_in", "ctx_in", "ident_zero", "ident_made", "ctx_turned", "ctx_moved_act", "ctx_moved_dve"))
        with nc.Block() as block:
            @block.sync
            def _(sp):
                for b in range(B):
                    sp.dma_start(raw[:, KT * b:KT * (b + 1), :],
                                 t["ctx_1024"][b].rearrange("(k p) d -> p k d", p=P)).then_inc(ctx_in, 16)
                sp.dma_start(X[:], t["x"].rearrange("b (k p) d -> p (b k) d", p=P)).then_inc(x_in, 16)
                sp.wait_ge(x_in, 16)

            @block.gpsimd
            def _(pool):
                pool.memset(ones[:], 1.0).then_inc(made, 1)
                pool.memset(eps[:], LN_EPS).then_inc(made, 1)
                pool.wait_ge(made, 2)
                pool.affine_select(out=ident[:], in_=ones[:], compare_op=ALU.is_equal, fill=0.0, base=0,
                                   pattern=[[1, P]], channel_multiplier=-1).then_inc(idm, 1)
                pool.wait_ge(idm, 1)
                pool.tensor_copy(identb[:], ident[:]).then_inc(idm, 1)
                pool.wait_ge(idm, 2)

            def half(n):
                return n // DT, n % DT

            @block.tensor
            def _(pe):
                pe.wait_ge(idm, 1)
                for n in range(B * KT // 4 * DT):
                    g, f = half(n)
                    pe.wait_ge(ctx_in, 16 * B)
                    if n >= 8:
                        pe.wait_ge((moved, movedv)[n % 2], (n - 8) // 2 + 1)
                    for k in range(4):
                        mm = pe.transpose(PS[:, n % 8, k * P:(k + 1) * P], raw[:, 4 * g + k, f * P:(f + 1) * P], ident[:])
                    mm.then_inc(turned, 1)

            def move(eng, mine, done, op):
                for n in range(mine, B * KT // 4 * DT, 2):
                    g, f = half(n)
                    eng.wait_ge(turned, n + 1)
                    op(ctxT[:, f, 512 * g:512 * (g + 1)], PS[:, n % 8, :]).then_inc(done, 1)
                eng.wait_ge(done, B * KT // 4 * DT // 2)

            @block.scalar
            def _(act):
                move(act, 0, moved, act.copy)

            @block.vector
            def _(dve):
                move(dve, 1, movedv, dve.tensor_copy)


def store_stage(K, out):
    nc, X = K["nc"], K["X"]
    stored = K["sem"]("stored")
    with nc.Block() as block:
        @block.sync
        def _(sp):
            sp.dma_start(out.rearrange("b (k p) d -> p (b k) d", p=P), X[:]).then_inc(stored, 16)
            sp.wait_ge(stored, 16)


def ln_statistics(dve, ch, src, st, mv):
    for k in range(QT):
        ch.mark(dve.bn_stats(st[:, k, :], src(k)))
    ch.wait()
    for k in range(QT):
        ch.mark(dve.bn_aggr(mv[:, k, :], st[:, k, :]))
    ch.wait()


def ln_apply(dve, ch, src, mv, std, rstd, xn, done):
    ch.mark(dve.reciprocal(rstd[:], std[:]))
    ch.wait()
    for k in range(QT):
        dve.tensor_scalar(xn[:, k, :], src(k), mv[:, k, 0:1], rstd[:, k:k + 1], ALU.subtract, ALU.mult).then_inc(done, 1)


def single_head_attention(K):
    nc, t, sb, sem, PS, X, ctxT = (K[n] for n in ("nc", "t", "sb", "sem", "PS", "X", "ctxT"))
    ident, ones, eps = K["ident"], K["ones"], K["eps"]
    N_ACT = 4 + 1 + 2 + FT
    N_DVE = 4 + 1 + 2 * QT + DT + QT
    XT_A, Q_A, H_A = 4, 5, 7
    XT_D, T_D, O_D, Y_D = 4, 5, 5 + 2 * QT, 5 + 2 * QT + DT
    N_CH = 2 * QT - 1 + 1 + QT
    with ExitStack() as c:
        wkv = sb(c, "a0_wkv", [P, DT, 2 * D]); wq = sb(c, "a0_wq", [P, DT, D])
        w1 = sb(c, "a0_w1", [P, DT, F]); w2 = sb(c, "a0_w2", [P, FT, D])
        bk = sb(c, "a0_bk", [P, DT]); bq = sb(c, "a0_bq", [P, DT]); b1 = sb(c, "a0_b1", [P, FT])
        bv = sb(c, "a0_bv", [1, D]); b2 = sb(c, "a0_b2", [1, D])
        cb = sb(c, "a0_ctxb", [P, DT, SK])
        xn = sb(c, "a0_xn", [P, QT, D]); xT = sb(c, "a0_xT", [P, DT, S])
        qT = sb(c, "a0_qT", [P, DT, S]); kT = sb(c, "a0_kT", [P, DT, SK]); v = sb(c, "a0_v", [P, KT, D])
        pr = sb(c, "a0_pr", [P, 2, SK]); pT = sb(c, "a0_pT", [P, KT, S])
        oT = sb(c, "a0_oT", [P, DT, S]); hT = sb(c, "a0_hT", [P, FT, S])
        st = sb(c, "a0_st", [P, QT, 6]); mv = sb(c, "a0_mv", [P, QT, 2])
        std = sb(c, "a0_std", [P, QT]); rstd = sb(c, "a0_rstd", [P, QT])
        nmax = sb(c, "a0_nmax", [P, QT]); psum_ = sb(c, "a0_sum", [P, QT]); rsum = sb(c, "a0_rsum", [P, QT])
        w_in, ch_s, std_s, mv_s, xn_s, cb_s = (sem("a0_" + n) for n in (
            "weights_in", "dve_chain", "std_ready", "var_ready", "xn_ready", "ctx_copied"))
        s_full, s_max, s_exp, p_norm = (sem("a0_" + n) for n in ("scores_full", "max_ready", "exp_done", "probs_scaled"))
        A = Ring([PS[:, 0, :], PS[:, 1, :]], sem("a0_act_full"), sem("a0_act_free"), N_ACT)
        V = Ring([PS[:, 2, :], PS[:, 3, :]], sem("a0_dve_full"), sem("a0_dve_free"), N_DVE)
        scores = [PS[:, 4:6, :], PS[:, 6:8, :]]
        N_W = 16 * 9
        with nc.Block() as block:
            @block.sync
            def _(sp):
                for dst, src in (
                    (wkv[:], t["L0_xattn_W_kv"].rearrange("(k p) n -> p k n", p=P)),
                    (wq[:], t["L0_xattn_W_q"].rearrange("(k p) n -> p k n", p=P)),
                    (bk[:], t["L0_xattn_b_kv_cols"][:, 0:DT]),
                    (bq[:], t["L0_xattn_b_q_cols"]),
                    (b1[:], t["L0_xattn_b1_cols"]),
                    (bv[:], t["L0_xattn_b_kv"][D:2 * D].rearrange("(a n) -> a n", a=1)),
                    (b2[:], t["L0_xattn_b2"].rearrange("(a n) -> a n", a=1)),
                    (w1[:], t["L0_xattn_W1"].rearrange("(k p) n -> p k n", p=P)),
                    (w2[:], t["L0_xattn_W2"].rearrange("(k p) n -> p k n", p=P)),
                ):
                    sp.dma_start(dst, src).then_inc(w_in, 16)

            @block.gpsimd
            def _(pool):
                A.start(pool)
                V.start(pool)
                for f in range(DT):
                    pool.tensor_copy(cb[:, f, :], ctxT[:, f, 0:SK]).then_inc(cb_s, 1)
                with pool.Fori(0, B - 1) as b:
                    A.wait_done(pool, b, 3)
                    V.wait_done(pool, b, 3)
                    split_wait(pool, K["passed"])
                    for f in range(DT):
                        pool.tensor_copy(cb[:, f, :], ctxT[:, f, ds(b * SK + SK, SK)]).then_inc(cb_s, 1)

            @block.tensor
            def _(pe):
                pe.wait_ge(w_in, N_W)
                with pe.Fori(0, B) as b:
                    pe.wait_ge(cb_s, b * DT + DT)
                    for m in range(DT):
                        for n in range(2):
                            i = 2 * m + n
                            A.wait_free(pe, b, i)
                            for k in range(DT):
                                mm = pe.matmul(A.bank(i), wkv[:, k, m * P:(m + 1) * P], cb[:, k, n * 512:(n + 1) * 512],
                                               start=(k == 0), stop=(k == DT - 1))
                            mm.then_inc(A.full, 1)
                    V.wait_turns(pe, b)
                    for i in range(4):
                        V.wait_free(pe, b, i)
                        for u in range(2):
                            o = V.bank(i)[:, u * D:(u + 1) * D]
                            pe.matmul(o, ones[0:1, :], bv[:], start=True, stop=False, skip_group_check=True)
                            for k in range(DT):
                                mm = pe.matmul(o, cb[:, k, (2 * i + u) * P:(2 * i + u + 1) * P], wkv[:, k, D:2 * D],
                                               start=False, stop=(k == DT - 1), skip_group_check=True)
                        mm.then_inc(V.full, 1)
                    pe.wait_ge(xn_s, b * QT + QT)
                    for f, (R, i) in enumerate(((A, XT_A), (V, XT_D))):
                        R.wait_free(pe, b, i)
                        for k in range(QT):
                            mm = pe.transpose(R.bank(i)[:, k * P:(k + 1) * P], xn[:, k, f * P:(f + 1) * P], ident[:])
                        mm.then_inc(R.full, 1)
                    A.wait_done(pe, b, XT_A)
                    V.wait_done(pe, b, XT_D)
                    for m in range(DT):
                        A.wait_free(pe, b, Q_A + m)
                        for k in range(DT):
                            mm = pe.matmul(A.bank(Q_A + m), wq[:, k, m * P:(m + 1) * P], xT[:, k, :],
                                           start=(k == 0), stop=(k == DT - 1))
                        mm.then_inc(A.full, 1)
                    A.wait_done(pe, b, Q_A + 1)

                    def turn(q):
                        pe.wait_ge(p_norm, b * QT + q + 1)
                        for u in range(2):
                            i = T_D + 2 * q + u
                            V.wait_free(pe, b, i)
                            for k in range(4):
                                mm = pe.transpose(V.bank(i)[:, k * P:(k + 1) * P],
                                                  pr[:, q % 2, (4 * u + k) * P:(4 * u + k + 1) * P], ident[:])
                            mm.then_inc(V.full, 1)

                    for q in range(QT):
                        if q >= 2:
                            pe.wait_ge(s_exp, b * QT + q - 1)
                        for n in range(2):
                            for k in range(DT):
                                mm = pe.matmul(scores[q % 2][:, n, :], qT[:, k, q * P:(q + 1) * P],
                                               kT[:, k, n * 512:(n + 1) * 512], start=(k == 0), stop=(k == DT - 1))
                        mm.then_inc(s_full, 1)
                        if q >= 1:
                            turn(q - 1)
                    turn(QT - 1)
                    V.wait_done(pe, b, T_D + 2 * QT - 1)
                    for m in range(DT):
                        i = O_D + m
                        V.wait_free(pe, b, i)
                        for k in range(KT):
                            mm = pe.matmul(V.bank(i), v[:, k, m * P:(m + 1) * P], pT[:, k, :],
                                           start=(k == 0), stop=(k == KT - 1))
                        mm.then_inc(V.full, 1)
                    V.wait_done(pe, b, O_D + 1)
                    for m in range(FT):
                        i = H_A + m
                        A.wait_free(pe, b, i)
                        for k in range(DT):
                            mm = pe.matmul(A.bank(i), w1[:, k, m * P:(m + 1) * P], oT[:, k, :],
                                           start=(k == 0), stop=(k == DT - 1))
                        mm.then_inc(A.full, 1)
                    A.wait_done(pe, b, H_A + FT - 1)
                    for q in range(QT):
                        i = Y_D + q
                        V.wait_free(pe, b, i)
                        o = V.bank(i)[:, 0:D]
                        pe.matmul(o, ones[0:1, :], b2[:], start=True, stop=False)
                        for k in range(FT):
                            mm = pe.matmul(o, hT[:, k, q * P:(q + 1) * P], w2[:, k, :], start=False, stop=(k == FT - 1))
                        mm.then_inc(V.full, 1)

            @block.scalar
            def _(act):
                act.wait_ge(w_in, N_W)
                with act.Fori(0, B) as b:
                    for m in range(DT):
                        for n in range(2):
                            A.wait_full(act, b, 2 * m + n)
                            act.activation(kT[:, m, n * 512:(n + 1) * 512], A.bank(2 * m + n), ACT.Identity,
                                           bias=bk[:, m:m + 1]).then_inc(A.free, 1)
                            if m == 0 and n == 1:
                                act.wait_ge(mv_s, b + 1)
                                act.activation(std[:], mv[:, :, 1], ACT.Sqrt, bias=eps[:]).then_inc(std_s, 1)
                    A.wait_full(act, b, XT_A)
                    act.copy(xT[:, 0, :], A.bank(XT_A)).then_inc(A.free, 1)
                    for m in range(DT):
                        A.wait_full(act, b, Q_A + m)
                        act.activation(qT[:, m, :], A.bank(Q_A + m), ACT.Identity, bias=bq[:, m:m + 1]).then_inc(A.free, 1)
                    for q in range(QT):
                        act.wait_ge(s_max, b * QT + q + 1)
                        if q >= 2:
                            V.wait_done(act, b, T_D + 2 * (q - 2) + 1)
                        act.activation(pr[:, q % 2, :], scores[q % 2], ACT.Exp, bias=nmax[:, q:q + 1],
                                       accum_out=psum_[:, q:q + 1]).then_inc(s_exp, 1)
                    for m in range(FT):
                        A.wait_full(act, b, H_A + m)
                        act.activation(hT[:, m, :], A.bank(H_A + m), ACT.Gelu, bias=b1[:, m:m + 1]).then_inc(A.free, 1)

            @block.vector
            def _(dve):
                with dve.Fori(0, B) as b:
                    ch = Chain(dve, ch_s, b * N_CH)
                    V.wait_turns(dve, b)
                    split_wait(dve, K["passed"])
                    src = lambda k: X[:, ds(b * QT + k, 1), :]
                    for k in range(QT):
                        ch.mark(dve.bn_stats(st[:, k, :], src(k)))
                    ch.wait()
                    split_wait(dve, K["passed"])
                    for k in range(QT):
                        ins = dve.bn_aggr(mv[:, k, :], st[:, k, :])
                        if k < QT - 1:
                            ch.mark(ins)
                    ins.then_inc(mv_s, 1)
                    dve.wait_ge(mv_s, b + 1)
                    dve.wait_ge(std_s, b + 1)
                    ln_apply(dve, ch, src, mv, std, rstd, xn, xn_s)
                    for i in range(4):
                        V.wait_full(dve, b, i)
                        dve.tensor_copy(v[:, 2 * i:2 * i + 2, :], V.bank(i).rearrange("p (u d) -> p u d", u=2)).then_inc(V.free, 1)
                    V.wait_full(dve, b, XT_D)
                    dve.tensor_copy(xT[:, 1, :], V.bank(XT_D)).then_inc(V.free, 1)

                    def max_of(q):
                        dve.wait_ge(s_full, b * QT + q + 1)
                        dve.tensor_reduce(nmax[:, q:q + 1], scores[q % 2], AX.XY, ALU.max, negate=True).then_inc(s_max, 1)

                    def scale(q):
                        dve.wait_ge(s_exp, b * QT + q + 1)
                        ch.mark(dve.reciprocal(rsum[:, q:q + 1], psum_[:, q:q + 1]))
                        ch.wait()
                        dve.tensor_scalar(pr[:, q % 2, :], pr[:, q % 2, :], rsum[:, q:q + 1], None,
                                          ALU.mult).then_inc(p_norm, 1)

                    def turned(q):
                        for u in range(2):
                            i = T_D + 2 * q + u
                            V.wait_full(dve, b, i)
                            dve.tensor_copy(pT[:, 4 * u:4 * u + 4, q * P:(q + 1) * P],
                                            V.bank(i).rearrange("p (k n) -> p k n", k=4)).then_inc(V.free, 1)

                    for q in range(QT):
                        max_of(q)
                        if q >= 1:
                            scale(q - 1)
                            turned(q - 1)
                    scale(QT - 1)
                    turned(QT - 1)
                    for m in range(DT):
                        V.wait_full(dve, b, O_D + m)
                        dve.tensor_copy(oT[:, m, :], V.bank(O_D + m)).then_inc(V.free, 1)
                    for q in range(QT):
                        V.wait_full(dve, b, Y_D + q)
                        x = X[:, ds(b * QT + q, 1), :]
                        dve.tensor_tensor(x, x, V.bank(Y_D + q)[:, None, 0:D], ALU.add).then_inc(V.free, 1)
                    assert ch.n == N_CH, ch.n


def coupled_ffn(K):
    nc, t, sb, sem, PS, X = (K[n] for n in ("nc", "t", "sb", "sem", "PS", "X"))
    ident, ones, eps = K["ident"], K["ones"], K["eps"]
    TURNS = 3
    H3 = 64
    N_ACT = 1 + 3 + TURNS * 5
    N_DVE = 1 + QT
    N_CH = 2 * QT - 1 + 1 + 1 + 2 + TURNS * 3
    with ExitStack() as c:
        w1 = sb(c, "f0_w1", [P, DT, D]); w2 = sb(c, "f0_w2", [P, DT, P]); w3 = sb(c, "f0_w3", [P, H3])
        w4 = sb(c, "f0_w4", [H3, 1]); w4b = sb(c, "f0_w4b", [H3, P])
        g1w = sb(c, "f0_g1w", [P, DT, P]); g2w = sb(c, "f0_g2w", [P, H3]); g3w = sb(c, "f0_g3w", [H3, 1])
        b1 = sb(c, "f0_b1", [P, DT]); b2 = sb(c, "f0_b2", [P, 1]); b3 = sb(c, "f0_b3", [H3, 1])
        gb1 = sb(c, "f0_gb1", [P, 1]); gb2 = sb(c, "f0_gb2", [H3, 1])
        row = sb(c, "f0_row", [1, 3]); sc = sb(c, "f0_sc", [P, 3]); slope = sb(c, "f0_slope", [P, 1])
        sign = sb(c, "f0_sign", [P, 2])
        xn = sb(c, "f0_xn", [P, QT, D]); y = sb(c, "f0_y", [P, DT, S])
        mean = sb(c, "f0_mean", [P, DT]); g1 = sb(c, "f0_g1", [P, 1]); g2 = sb(c, "f0_g2", [H3, 1])
        g2b = sb(c, "f0_g2b", [H3, P]); gf = sb(c, "f0_gf", [P, 1]); off = sb(c, "f0_off", [P, 2])
        h1 = sb(c, "f0_h1", [P, DT, S]); h2 = sb(c, "f0_h2", [P, S]); h3 = sb(c, "f0_h3", [H3, S])
        tf = sb(c, "f0_tf", [P, S]); cp = sb(c, "f0_cp", [P, S]); tw = sb(c, "f0_tw", [P, DT, S])
        st = sb(c, "f0_st", [P, QT, 6]); mv = sb(c, "f0_mv", [P, QT, 2])
        std = sb(c, "f0_std", [P, QT]); rstd = sb(c, "f0_rstd", [P, QT])
        w_in, made, ch_s, std_s, mv_s, xn_s, mean_s, g2b_s, y_s, sc_full, sc_s = (sem("f0_" + n) for n in (
            "weights_in", "constants_made", "dve_chain", "std_ready", "var_ready", "xn_ready", "mean_ready",
            "g2_spread", "y_updated", "scalars_full", "scalars_ready"))
        A = Ring([PS[:, i, :] for i in range(4)], sem("f0_act_full"), sem("f0_act_free"), N_ACT)
        V = Ring([PS[:, i, :] for i in range(4, 7)], sem("f0_dve_full"), sem("f0_dve_free"), N_DVE)
        loads = [(w1[:], t["L0_ffn_cn_w1"].rearrange("(k p) n -> p k n", p=P)),
                 (w2[:], t["L0_ffn_cn_w2"].rearrange("(k p) n -> p k n", p=P)),
                 (w3[:], t["L0_ffn_cn_w3"]), (w4[:], t["L0_ffn_cn_w4"]),
                 (g1w[:], t["L0_ffn_gc_w1"].rearrange("(k p) n -> p k n", p=P)),
                 (g2w[:], t["L0_ffn_gc_w2"]), (g3w[:], t["L0_ffn_gc_w3"]),
                 (b1[:], t["L0_ffn_cn_b1_cols"]), (b2[:], t["L0_ffn_cn_b2_cols"]),
                 (b3[:], t["L0_ffn_cn_b3"].rearrange("(p a) -> p a", a=1)),
                 (gb1[:], t["L0_ffn_gc_b1_cols"]), (gb2[:], t["L0_ffn_gc_b2"].rearrange("(p a) -> p a", a=1)),
                 (row[:, 0:1], t["L0_ffn_cn_b4"].rearrange("(a n) -> a n", a=1)),
                 (row[:, 1:2], t["L0_ffn_gc_b3"].rearrange("(a n) -> a n", a=1)),
                 (row[:, 2:3], t["L0_ffn_adaptive_range"].rearrange("(a n) -> a n", a=1))]
        with nc.Block() as block:
            @block.sync
            def _(sp):
                for dst, src in loads:
                    sp.dma_start(dst, src).then_inc(w_in, 16)

            @block.gpsimd
            def _(pool):
                A.start(pool)
                V.start(pool)
                pool.memset(sign[0:64, 0:1], 1.0).then_inc(made, 1)
                pool.memset(sign[64:128, 0:1], -1.0).then_inc(made, 1)
                pool.memset(sign[0:64, 1:2], -1.0).then_inc(made, 1)
                pool.memset(sign[64:128, 1:2], 1.0).then_inc(made, 1)

            @block.tensor
            def _(pe):
                pe.wait_ge(w_in, 16 * len(loads))
                pe.matmul(PS[:, 7, 0:3], ones[0:1, :], row[:], start=True, stop=True).then_inc(sc_full, 1)
                pe.wait_ge(sc_s, 3)
                with pe.Fori(0, B) as b:
                    pe.wait_ge(xn_s, b * QT + QT)
                    for f, R in enumerate((A, V)):
                        for k in range(QT):
                            mm = pe.transpose(R.bank(0)[:, k * P:(k + 1) * P], xn[:, k, f * P:(f + 1) * P], ident[:])
                        mm.then_inc(R.full, 1)
                    i = 1
                    pe.wait_ge(mean_s, b + 1)
                    for k in range(DT):
                        mm = pe.matmul(A.bank(i)[:, 0:1], g1w[:, k, :], mean[:, k:k + 1], start=(k == 0), stop=(k == DT - 1))
                    mm.then_inc(A.full, 1)
                    A.wait_done(pe, b, i)
                    i += 1
                    pe.matmul(A.bank(i)[0:H3, 0:1], g2w[:], g1[:], start=True, stop=True).then_inc(A.full, 1)
                    i += 1
                    pe.wait_ge(g2b_s, b + 1)
                    pe.matmul(A.bank(i)[:, 0:1], g2b[:], g3w[:], start=True, stop=True).then_inc(A.full, 1)
                    i += 1
                    for r in range(TURNS):
                        if r:
                            pe.wait_ge(y_s, b * TURNS * DT + DT * r)
                        for m in range(DT):
                            A.wait_free(pe, b, i)
                            for k in range(DT):
                                mm = pe.matmul(A.bank(i), w1[:, k, m * P:(m + 1) * P], y[:, k, :],
                                               start=(k == 0), stop=(k == DT - 1))
                            mm.then_inc(A.full, 1)
                            i += 1
                        A.wait_done(pe, b, i - 1)
                        for k in range(DT):
                            mm = pe.matmul(A.bank(i), w2[:, k, :], h1[:, k, :], start=(k == 0), stop=(k == DT - 1))
                        mm.then_inc(A.full, 1)
                        A.wait_done(pe, b, i)
                        i += 1
                        pe.matmul(A.bank(i)[0:H3, :], w3[:], h2[:], start=True, stop=True).then_inc(A.full, 1)
                        A.wait_done(pe, b, i)
                        i += 1
                        pe.matmul(A.bank(i), w4b[:], h3[:], start=True, stop=True).then_inc(A.full, 1)
                        i += 1
                    assert i == N_ACT
                    pe.wait_ge(y_s, b * TURNS * DT + DT * TURNS)
                    for q in range(QT):
                        V.wait_free(pe, b, 1 + q)
                        for f in range(DT):
                            mm = pe.transpose(V.bank(1 + q)[:, f * P:(f + 1) * P], y[:, f, q * P:(q + 1) * P], ident[:])
                        mm.then_inc(V.full, 1)

            @block.scalar
            def _(act):
                act.wait_ge(w_in, 16 * len(loads))
                act.wait_ge(sc_s, 3)
                with act.Fori(0, B) as b:
                    V.wait_turns(act, b)
                    act.wait_ge(mv_s, b + 1)
                    act.activation(std[:], mv[:, :, 1], ACT.Sqrt, bias=eps[:]).then_inc(std_s, 1)
                    i = 0

                    def job(dst, src, func, bias):
                        nonlocal i
                        A.wait_full(act, b, i)
                        if bias is None:
                            act.copy(dst, src(A.bank(i))).then_inc(A.free, 1)
                        else:
                            act.activation(dst, src(A.bank(i)), func, bias=bias).then_inc(A.free, 1)
                        i += 1

                    job(y[:, 0, :], lambda o: o, None, None)
                    job(g1[:], lambda o: o[:, 0:1], ACT.Gelu, gb1[:])
                    job(g2[:], lambda o: o[0:H3, 0:1], ACT.Gelu, gb2[:])
                    job(gf[:], lambda o: o[:, 0:1], ACT.Sigmoid, sc[:, 1:2])
                    for r in range(TURNS):
                        job(h1[:, 0, :], lambda o: o, ACT.Gelu, b1[:, 0:1])
                        job(h1[:, 1, :], lambda o: o, ACT.Gelu, b1[:, 1:2])
                        job(h2[:], lambda o: o, ACT.Gelu, b2[:])
                        job(h3[:], lambda o: o[0:H3, :], ACT.Gelu, b3[:])
                        job(tf[:], lambda o: o, ACT.Sigmoid, sc[:, 0:1])

            @block.vector
            def _(dve):
                dve.wait_ge(w_in, 16 * len(loads))
                dve.wait_ge(made, 4)
                dve.tensor_copy(w4b[:], w4[:].broadcast_to([H3, P])).then_inc(sc_s, 1)
                dve.wait_ge(sc_full, 1)
                dve.tensor_copy(sc[:], PS[:, 7, 0:3]).then_inc(sc_s, 1)
                dve.wait_ge(sc_s, 2)
                dve.tensor_scalar(slope[:], sc[:, 2:3], 0.6, None, ALU.mult).then_inc(sc_s, 1)
                dve.wait_ge(sc_s, 3)
                with dve.Fori(0, B) as b:
                    ch = Chain(dve, ch_s, b * N_CH)
                    V.wait_turns(dve, b)
                    split_wait(dve, K["passed"])
                    src = lambda k: X[:, ds(b * QT + k, 1), :]
                    for k in range(QT):
                        ch.mark(dve.bn_stats(st[:, k, :], src(k)))
                    ch.wait()
                    split_wait(dve, K["passed"])
                    for k in range(QT):
                        ins = dve.bn_aggr(mv[:, k, :], st[:, k, :])
                        if k < QT - 1:
                            ch.mark(ins)
                    ins.then_inc(mv_s, 1)
                    dve.wait_ge(mv_s, b + 1)
                    dve.wait_ge(std_s, b + 1)
                    ln_apply(dve, ch, src, mv, std, rstd, xn, xn_s)
                    V.wait_full(dve, b, 0)
                    dve.tensor_copy(y[:, 1, :], V.bank(0)).then_inc(V.free, 1)
                    A.wait_done(dve, b, 0)
                    V.wait_done(dve, b, 0)
                    ch.mark(dve.tensor_reduce(mean[:, 0:2], y[:], AX.X, ALU.add))
                    ch.wait()
                    dve.tensor_scalar(mean[:], mean[:], 1.0 / S, None, ALU.mult).then_inc(mean_s, 1)
                    A.wait_done(dve, b, 2)
                    dve.tensor_copy(g2b[:], g2[:].broadcast_to([H3, P])).then_inc(g2b_s, 1)
                    A.wait_done(dve, b, 3)
                    ch.mark(dve.tensor_scalar(off[:, 0:1], gf[:], 1.4, -1.0, ALU.mult, ALU.add))
                    ch.wait()
                    ch.mark(dve.tensor_scalar(off[:, 1:2], off[:, 0:1], sc[:, 2:3], 0.1, ALU.mult, ALU.add))
                    ch.wait()
                    for r in range(TURNS):
                        A.wait_done(dve, b, 3 + 5 * (r + 1))
                        ch.mark(dve.tensor_scalar(cp[:], tf[:], slope[:], off[:, 1:2], ALU.mult, ALU.add))
                        ch.wait()
                        for f in range(DT):
                            ch.mark(dve.scalar_tensor_tensor(out=tw[:, f, :], in0=y[:, 1 - f, :], scalar=sign[:, f:f + 1],
                                                             in1=cp[:], op0=ALU.mult, op1=ALU.mult))
                        ch.wait()
                        for f in range(DT):
                            dve.tensor_tensor(y[:, f, :], y[:, f, :], tw[:, f, :], ALU.add).then_inc(y_s, 1)
                        dve.wait_ge(y_s, b * TURNS * DT + DT * (r + 1))
                    for q in range(QT):
                        V.wait_full(dve, b, 1 + q)
                        x = X[:, ds(b * QT + q, 1), :]
                        dve.tensor_tensor(x, x, V.bank(1 + q)[:, None, 0:D], ALU.add).then_inc(V.free, 1)
                    assert ch.n == N_CH, ch.n


class Flow:

    def __init__(self, banks, full, free):
        self.banks, self.full, self.free = banks, full, free

    def start(self, eng):
        eng.sem_inc(self.free, len(self.banks))

    def bank(self, n):
        return self.banks[n % len(self.banks)]

    def wait_free(self, pe, base, n):
        pe.wait_ge(self.free, base + n + 1)

    def wait_full(self, eng, base, n):
        eng.wait_ge(self.full, base + n + 1)

    def wait_done(self, eng, base, n):
        eng.wait_ge(self.free, base + n + 1 + len(self.banks))


HEAD_TERMS = ((0, 0), (1, 0), (0, 1), (2, 0), (0, 2), (1, 1))


def head_projections(K, name, biased, qdram, kdram):
    nc, t, sb, sem, PS, X, ctxT = (K[n] for n in ("nc", "t", "sb", "sem", "PS", "X", "ctxT"))
    ident, eps = K["ident"], K["eps"]
    Wt = "%s_xattn_W" % name
    pre = name + "p_"
    with ExitStack() as c:
        wq = sb(c, pre + "wq", [P, DT, D]); wk = sb(c, pre + "wk", [P, DT, D])
        bq = sb(c, pre + "bq", [P, DT]); bk = sb(c, pre + "bk", [P, DT])
        cb = sb(c, pre + "cb", [P, 2, DT, SK])
        xn = sb(c, pre + "xn", [P, 2, QT, D]); xT = sb(c, pre + "xT", [P, 2, DT, S])
        kf = sb(c, pre + "kf", [P, 2, DT, SK]); kr = sb(c, pre + "kr", [P, DT, SK]); ks = sb(c, pre + "ks", [P, 2, 3, DT, SK], BF16)
        qf = sb(c, pre + "qf", [P, 2, DT, S]); qr = sb(c, pre + "qr", [P, DT, S]); qs = sb(c, pre + "qs", [P, 2, 3, DT, S], BF16)
        st = sb(c, pre + "st", [P, NT, 6]); mv = sb(c, pre + "mv", [P, NT, 2])
        std = sb(c, pre + "std", [P, NT]); rstd = sb(c, pre + "rstd", [P, NT])
        mvb = sb(c, pre + "mvb", [P, 2, QT, 2]); rsb = sb(c, pre + "rsb", [P, 2, QT])
        w_in, ch_s, mv_s, std_s, xn_s, cb_s, ksp_s, qsp_s, st_s, stored = (sem(pre + n) for n in (
            "weights_in", "dve_chain", "var_ready", "std_ready", "xn_ready", "ctx_copied", "k_split", "q_split",
            "parts_out", "batches_stored"))
        N_A = 4 + 2 + 2
        A = Flow([PS[:, n, :] for n in range(8)], sem(pre + "act_full"), sem(pre + "act_free"))
        loads = [(wq[:], t[Wt + "q"].rearrange("(k p) n -> p k n", p=P)),
                 (wk[:], t[Wt + "k"].rearrange("(k p) n -> p k n", p=P))]
        if biased:
            loads += [(bq[:], t["L1_xattn_bq_cols"]), (bk[:], t["L1_xattn_bk_cols"])]
        with nc.Block() as block:
            @block.sync
            def _(sp):
                for dst, src in loads:
                    sp.dma_start(dst, src).then_inc(w_in, 16)
                with sp.Fori(0, B // 2) as i:
                    for par in range(2):
                        b = i * 2 + par
                        sp.wait_ge(ksp_s, b + 1)
                        sp.dma_start(kdram[ds(b * 3 * D, 3 * D), :].rearrange("(j p) n -> p j n", p=P),
                                     ks[:, par, :, :, :].rearrange("p i k n -> p (i k) n")).then_inc(st_s, 16)
                        sp.wait_ge(qsp_s, b + 1)
                        sp.dma_start(qdram[ds(b * 3 * D, 3 * D), :].rearrange("(j p) n -> p j n", p=P),
                                     qs[:, par, :, :, :].rearrange("p i k n -> p (i k) n")).then_inc(st_s, 16)
                        sp.wait_ge(st_s, 32 * b + 32)
                        sp.sem_inc(stored, 1)

            @block.gpsimd
            def _(pool):
                A.start(pool)
                pool.sem_inc(stored, 2)
                for b in range(B):
                    if b >= 2:
                        A.wait_done(pool, (b - 2) * N_A, 3)
                    pool.tensor_copy(cb[:, b % 2, :, :], ctxT[:, :, b * SK:(b + 1) * SK]).then_inc(cb_s, 1)

            @block.tensor
            def _(pe):
                pe.wait_ge(w_in, 16 * len(loads))
                with pe.Fori(0, B // 2) as i:
                    for par in range(2):
                        b = i * 2 + par
                        pe.wait_ge(cb_s, b + 1)
                        for n in range(4):
                            A.wait_free(pe, b * N_A, n)
                            m, h = n // 2, n % 2
                            for k in range(DT):
                                mm = pe.matmul(A.bank(n), wk[:, k, m * P:(m + 1) * P], cb[:, par, k, h * 512:(h + 1) * 512],
                                               start=(k == 0), stop=(k == DT - 1))
                            mm.then_inc(A.full, 1)
                        pe.wait_ge(xn_s, b + 1)
                        for f in range(DT):
                            A.wait_free(pe, b * N_A, 4 + f)
                            for k in range(QT):
                                mm = pe.transpose(A.bank(4 + f)[:, k * P:(k + 1) * P], xn[:, par, k, f * P:(f + 1) * P], ident[:])
                            mm.then_inc(A.full, 1)
                        A.wait_done(pe, b * N_A, 5)
                        for m in range(DT):
                            A.wait_free(pe, b * N_A, 6 + m)
                            for k in range(DT):
                                mm = pe.matmul(A.bank(6 + m), wq[:, k, m * P:(m + 1) * P], xT[:, par, k, :],
                                               start=(k == 0), stop=(k == DT - 1))
                            mm.then_inc(A.full, 1)

            @block.scalar
            def _(act):
                act.wait_ge(w_in, 16 * len(loads))
                act.wait_ge(mv_s, 1)
                act.activation(std[:], mv[:, :, 1], ACT.Sqrt, bias=eps[:]).then_inc(std_s, 1)
                with act.Fori(0, B // 2) as i:
                    for par in range(2):
                        b = i * 2 + par
                        act.wait_ge(stored, b + 1)
                        for n in range(4):
                            m, h = n // 2, n % 2
                            A.wait_full(act, b * N_A, n)
                            bias = bk[:, m:m + 1] if biased else 0.0
                            act.activation(kf[:, par, m, h * 512:(h + 1) * 512], A.bank(n), ACT.Identity, bias=bias)
                            act.activation(ks[:, par, 0, m, h * 512:(h + 1) * 512], A.bank(n), ACT.Identity, bias=bias).then_inc(A.free, 1)
                        for f in range(DT):
                            A.wait_full(act, b * N_A, 4 + f)
                            act.copy(xT[:, par, f, :], A.bank(4 + f)).then_inc(A.free, 1)
                        for m in range(DT):
                            A.wait_full(act, b * N_A, 6 + m)
                            bias = bq[:, m:m + 1] if biased else 0.0
                            act.activation(qf[:, par, m, :], A.bank(6 + m), ACT.Identity, bias=bias)
                            act.activation(qs[:, par, 0, m, :], A.bank(6 + m), ACT.Identity, bias=bias).then_inc(A.free, 1)

            @block.vector
            def _(dve):
                ch = Chain(dve, ch_s)
                for k in range(NT):
                    ch.mark(dve.bn_stats(st[:, k, :], X[:, k, :]))
                ch.wait()
                for k in range(NT):
                    ins = dve.bn_aggr(mv[:, k, :], st[:, k, :])
                    if k < NT - 1:
                        ch.mark(ins)
                ins.then_inc(mv_s, 1)
                dve.wait_ge(mv_s, 1)
                dve.wait_ge(std_s, 1)
                ch.mark(dve.reciprocal(rstd[:], std[:]))
                ch.wait()
                ch0 = ch.n
                with dve.Fori(0, B // 2) as i:
                    ch = Chain(dve, ch_s, i * 12 + ch0)
                    for par in range(2):
                        b = i * 2 + par
                        dve.wait_ge(stored, b + 1)
                        split_wait(dve, K["passed"])
                        ch.mark(dve.tensor_copy(mvb[:, par, :, :], mv[:, ds(b * QT, QT), :]))
                        ch.mark(dve.tensor_copy(rsb[:, par, :], rstd[:, ds(b * QT, QT)]))
                        ch.wait()
                        for k in range(QT):
                            ins = dve.tensor_scalar(xn[:, par, k:k + 1, :], X[:, ds(b * QT + k, 1), :], mvb[:, par, k, 0:1],
                                                    rsb[:, par, k:k + 1], ALU.subtract, ALU.mult)
                        ins.then_inc(xn_s, 1)
                        A.wait_done(dve, b * N_A, 3)
                        ch.mark(dve.tensor_tensor(kr[:], kf[:, par, :, :], ks[:, par, 0, :, :], ALU.subtract))
                        ch.wait()
                        ch.mark(dve.tensor_copy(ks[:, par, 1, :, :], kr[:]))
                        ch.wait()
                        dve.tensor_tensor(ks[:, par, 2, :, :], kr[:], ks[:, par, 1, :, :], ALU.subtract).then_inc(ksp_s, 1)
                        dve.wait_ge(ksp_s, b + 1)
                        A.wait_done(dve, b * N_A, 7)
                        ch.mark(dve.tensor_tensor(qr[:], qf[:, par, :, :], qs[:, par, 0, :, :], ALU.subtract))
                        ch.wait()
                        ch.mark(dve.tensor_copy(qs[:, par, 1, :, :], qr[:]))
                        ch.wait()
                        dve.tensor_tensor(qs[:, par, 2, :, :], qr[:], qs[:, par, 1, :, :], ALU.subtract).then_inc(qsp_s, 1)
                        dve.wait_ge(qsp_s, b + 1)
                    assert ch.n == 12, ch.n


def head_attention(K, name, scale, biased, masked):
    nc, t, sb, sem, PS, X, ctxT = (K[n] for n in ("nc", "t", "sb", "sem", "PS", "X", "ctxT"))
    ident, identb, ones = K["ident"], K["identb"], K["ones"]
    HD = D // H
    G = H // 4
    TERMS = HEAD_TERMS
    ROWS = HD * len(TERMS)
    CW = 32
    N_MAX = 4 * QT * 2
    UNITS = 4 * 4
    NE = 8

    def slot_jobs(g, before, after, outputs, values=True):
        jobs = [[] for _ in range(UNITS)]
        if before:
            jobs[6] += [("sum", g - 1)]
            jobs[7] += [("share", g - 1)]
        for q in range(QT if outputs else 0):
            jobs[9 + q] += [("y", q)]
        if after:
            for n in range(UNITS):
                jobs[n] += [("max", g + 1, i) for i in range(3 * n, min(3 * n + 3, N_MAX))]
            jobs[11] += [("neg", g + 1)]
        if values:
            jobs[12] += [("v", g)]
        return jobs

    def v_part(g):
        return (g + 2) // G, 1 if g % G < 2 else 0, g % 2

    first = [[[("v", -2), ("v", -1)] + [("max", 0, i) for i in range(N_MAX)] + [("neg", 0)]], slot_jobs(0, False, True, False)]
    middle = [slot_jobs(g, True, True, g == G) for g in range(1, G + 1)]
    last = [slot_jobs(g, True, g < G - 1, False, g == 1) for g in range(1, G)]
    last += [[[("sum", G - 1), ("share", G - 1)] + [("y", q) for q in range(QT)]]]
    NV = 3
    for turn in (first, middle):
        turn[-1][-1] += [("skip", i) for i in range(-sum(len(unit) for slot in turn for unit in slot) % NV)]

    def places(turn):
        flat = [(s, n, j) for s, slot in enumerate(turn) for n, unit in enumerate(slot) for j in unit]
        return {(s, n, j): at for at, (s, n, j) in enumerate(flat)}, len(flat)

    Wt = "%s_xattn_W" % name
    pre = name + "a_"
    qdram = nc.dram_tensor(pre + "q_parts", (B * 3 * D, S), BF16, kind="Internal").ap()
    kdram = nc.dram_tensor(pre + "k_parts", (B * 3 * D, SK), BF16, kind="Internal").ap()
    head_projections(K, name, biased, qdram, kdram)
    with ExitStack() as c:
        wv = sb(c, pre + "wv", [P, DT, D])
        wo = sb(c, pre + "wo", [P, G, D]); sel = sb(c, pre + "sel", [P, 4]); rcw = sb(c, pre + "rcw", [P, QT, P])
        bv = sb(c, pre + "bv", [1, D]); bo = sb(c, pre + "bo", [1, D])
        cb = sb(c, pre + "cb", [P, DT, SK])
        ex = sb(c, pre + "ex", [P, NE, SK])
        exw = ex[:, :, :].rearrange("p e n -> p (e n)")
        kst = sb(c, pre + "kst", [P, H, SK], BF16); qst = sb(c, pre + "qst", [P, H, S], BF16)
        v = sb(c, pre + "v", [P, G, KT, 4, CW]); bvb = sb(c, pre + "bvb", [P, D])
        mx = sb(c, pre + "mx", [P, QT, 4, 2]); nm = sb(c, pre + "nm", [P, QT, 4]); nr = sb(c, pre + "nr", [P, QT, 4])
        nsp = sb(c, pre + "nsp", [P, QT, 3, 4], BF16); nT = sb(c, pre + "nT", [12, S], BF16)
        osb = sb(c, pre + "osb", [P, 2, S]); aT = sb(c, pre + "aT", [P, G, S]); rc = sb(c, pre + "rc", [P, QT, 4])
        if masked:
            mraw = exw[:, 0:QT * SK // 4].bitcast(U8).rearrange("p (q n) -> p q n", q=QT)
            biasq = sb(c, pre + "biasq", [P, QT, SK], BF16); biask = sb(c, pre + "biask", [P, KT, S], BF16)
            any_ = sb(c, pre + "any", [P, QT])
        names = ("weights_in", "zeroed", "constants_made", "dve_chain", "ctx_copied", "neg_ready",
                 "neg_turned", "neg_in", "scores_full", "exp_done", "pv_done", "attention_ready", "mask_full", "mask_done",
                 "v_bias_full", "v_bias_ready", "wo_in")
        (w_in, zeroed, made, ch_s, cb_s, nr_s, nt_s, nin_s, s_full, s_exp, pv_s, at_s, mk_full, mk_s,
         bvf_s, bvb_s, wo_s) = (sem(pre + n) for n in names)
        stacked = [sem(pre + "stacked%d" % g) for g in range(G)]
        V = Flow([PS[:, 1 + i, :] for i in range(NV)], sem(pre + "dve_full"), sem(pre + "dve_free"))
        o_free = sem(pre + "products_taken")
        O = PS[:, 0, :]
        scores = [PS[:, 4:6, :], PS[:, 6:8, :]]
        AHEAD = 3
        loads = [(wv[:], t[Wt + "v"].rearrange("(k p) n -> p k n", p=P))]
        wo_loads = [(wo[32 * j:32 * j + HD, :, :], t[Wt + "o"].rearrange("(g j d) n -> j d g n", j=4, d=HD)[j]) for j in range(4)]
        if biased:
            loads += [(bv[:], t["L1_xattn_bv"].rearrange("(a n) -> a n", a=1)),
                      (bo[:], t["L1_xattn_bo"].rearrange("(a n) -> a n", a=1))]
        if masked:
            loads += [(mraw[:], t["mask_SxS2_bk0"].rearrange("(k p) n -> p k n", p=P))]
        pos, counts = zip(*(places(turn) for turn in (first, middle, last)))
        base_of = (lambda b: 0, lambda b: b * counts[1] + counts[0], lambda b: (B - 1) * counts[1] + counts[0])
        V_CB = pos[1][0, 12, ("v", 1)]
        with nc.Block() as block:
            @block.sync
            def _(sp):
                def stack(b, g):
                    for r, (i, j) in enumerate(TERMS):
                        sp.dma_start(kst[HD * r:HD * (r + 1), 4 * g:4 * g + 4, :],
                                     kdram[ds(b * 3 * D + j * D + g * 4 * HD, 4 * HD), :].rearrange("(h d) n -> d h n", d=HD)
                                     ).then_inc(stacked[g], 16)
                        sp.dma_start(qst[HD * r:HD * (r + 1), 4 * g:4 * g + 4, :],
                                     qdram[ds(b * 3 * D + i * D + g * 4 * HD, 4 * HD), :].rearrange("(h d) n -> d h n", d=HD)
                                     ).then_inc(stacked[g], 16)

                def negated(s, g):
                    sp.wait_ge(nt_s, s + 1)
                    for i in range(3):
                        sp.dma_start(qst[ROWS + i:ROWS + i + 1, 4 * g:4 * g + 4, :], nT[4 * i:4 * i + 4, :]).then_inc(nin_s, 16)

                for dst, src in loads:
                    sp.dma_start(dst, src).then_inc(w_in, 16)
                stack(0, 0)
                sp.wait_ge(zeroed, 2)
                for dst, src in wo_loads:
                    sp.dma_start(dst, src).then_inc(wo_s, 16)
                for g in range(1, G):
                    stack(0, g)
                negated(0, 0)
                negated(1, 1)
                with sp.Fori(0, B - 1) as b:
                    for g in range(G):
                        if g:
                            negated(b * G + g + 1, (g + 1) % G)
                        sp.wait_ge(s_full, b * (G * UNITS) + (g + 1) * UNITS)
                        stack(b + 1, g)
                    negated(b * G + G + 1, 1)
                for g in range(2, G):
                    negated((B - 1) * G + g, g)

            @block.gpsimd
            def _(pool):
                V.start(pool)
                pool.sem_inc(o_free, 1)
                pool.sem_inc(at_s, AHEAD)
                pool.memset(wo[:], 0.0).then_inc(zeroed, 1)
                pool.memset(v[:], 0.0).then_inc(zeroed, 1)
                pool.wait_ge(zeroed, 2)
                pool.memset(v[:, :, :, :, HD:HD + 1], 1.0).then_inc(made, 1)
                pool.affine_select(out=sel[:], in_=ones[:, 0:4], compare_op=ALU.is_equal,
                                   fill=0.0, base=-HD, pattern=[[-CW, 4]], channel_multiplier=1).then_inc(made, 1)
                pool.wait_ge(made, 2)
                pool.memset(kst[ROWS:P, :, :], 1.0).then_inc(made, 1)
                pool.wait_ge(made, 3)
                with pool.Fori(0, B - 1) as b:
                    V.wait_done(pool, base_of[1](b), V_CB)
                    split_wait(pool, K["passed"])
                    pool.tensor_copy(cb[:], ctxT[:, :, ds(b * SK + SK, SK)]).then_inc(cb_s, 1)

            @block.tensor
            def _(pe):
                pe.wait_ge(w_in, 16 * len(loads))
                if masked:
                    for kt in range(KT):
                        pe.wait_ge(mk_s, 2 if kt < 4 else kt - 1)
                        bank = PS[:, kt % 4, :].bitcast(BF16)
                        for q in range(QT):
                            mm = pe.transpose(bank[:, q * P:(q + 1) * P], biasq[:, q, kt * P:(kt + 1) * P], identb[:])
                        mm.then_inc(mk_full, 1)
                    pe.wait_ge(mk_s, 2 + KT)

                def fill(b, base, place, s, n, job):
                    at = place[s, n, job]
                    o = V.bank(at)
                    V.wait_free(pe, base, at)
                    if job[0] == "max":
                        g, i = job[1], job[2]
                        h, q, n = 4 * (g % G) + i // (2 * QT), i // 2 % QT, i % 2
                        if i == 0:
                            pe.wait_ge(stacked[g % G], (b + g // G) * 192 + 192)
                        pe.matmul(o, qst[0:ROWS, h, q * P:(q + 1) * P], kst[0:ROWS, h, n * 512:(n + 1) * 512],
                                  start=True, stop=True).then_inc(V.full, 1)
                    elif job[0] == "neg":
                        pe.wait_ge(nr_s, b * G + job[1] + 1)
                        o = o.bitcast(BF16)
                        for q in range(QT):
                            mm = pe.transpose(o[0:12, q * P:(q + 1) * P], nsp[:, q, :, :].rearrange("p i j -> p (i j)"), identb[:])
                        mm.then_inc(V.full, 1)
                    elif job[0] == "v":
                        ahead, pair, half = v_part(job[1])
                        pe.wait_ge(cb_s, b + ahead + 1)
                        for kk in range(KT // 2):
                            kt = half * (KT // 2) + kk
                            for k in range(DT):
                                mm = pe.matmul(o[:, kk * P:(kk + 1) * P], cb[:, k, kt * P:(kt + 1) * P], wv[:, k, pair * P:(pair + 1) * P],
                                               start=(k == 0), stop=(k == DT - 1), skip_group_check=True)
                        mm.then_inc(V.full, 1)
                    elif job[0] == "sum":
                        g = job[1]
                        pe.wait_ge(o_free, b * G + g + 2)
                        for q in range(QT):
                            mm = pe.matmul(o[:, 4 * q:4 * q + 4], osb[:, g % 2, q * P:(q + 1) * P], sel[:],
                                           start=True, stop=True, skip_group_check=True)
                        mm.then_inc(V.full, 1)
                    elif job[0] == "share":
                        V.wait_done(pe, base, place[s, n - 1 if n else 0, ("sum", job[1])])
                        for q in range(QT):
                            mm = pe.matmul(o[:, q * P:(q + 1) * P], rcw[:, q, :], ident[:], start=True, stop=True,
                                           skip_group_check=True)
                        mm.then_inc(V.full, 1)
                    elif job[0] == "skip":
                        V.wait_full(pe, base, at - 1)
                        pe.sem_inc(V.full, 1)
                    else:
                        q = job[1]
                        pe.wait_ge(at_s, b * G + G + AHEAD)
                        for g in range(G):
                            mm = pe.matmul(o[:, 0:D], aT[:, g, q * P:(q + 1) * P], wo[:, g, :],
                                           start=(g == 0), stop=(g == G - 1 and not biased))
                        if biased:
                            mm = pe.matmul(o[:, 0:D], ones[0:1, :], bo[:], start=False, stop=True)
                        mm.then_inc(V.full, 1)

                def scores_of(b, g, n):
                    u, j = n // 4, n % 4
                    h, at = 4 * (g % G) + j, b * (G * UNITS) + (g * UNITS + n)
                    if g or n >= 2:
                        pe.wait_ge(s_exp, at - 1)
                    for kk in range(2):
                        kt = 2 * u + kk
                        mm = pe.matmul(scores[n % 2][:, kk, :], kst[0:ROWS + 3, h, kt * P:(kt + 1) * P],
                                       qst[0:ROWS + 3, h, :], start=True, stop=not masked)
                        if masked:
                            mm = pe.matmul(scores[n % 2][:, kk, :], identb[:], biask[:, kt, :], start=False, stop=True)
                    mm.then_inc(s_full, 1)

                def products(b, g, n):
                    if n % 2 == 0:
                        return
                    u, kk = n // 4, n % 4 // 2
                    if n == 1:
                        pe.wait_ge(o_free, b * G + g + 1)
                    if n % 4 == 1:
                        pe.wait_ge(s_exp, b * (G * UNITS) + (g * UNITS + 4 * u + 4))
                    kt = 2 * u + kk
                    for j in range(4):
                        mm = pe.matmul(O[32 * j:32 * j + CW, :], v[:, g % G, kt, j, :],
                                       ex[:, (4 * u + j) % NE, kk * 512:(kk + 1) * 512],
                                       start=(kt == 0), stop=(kt == KT - 1), skip_group_check=True)
                    if n % 4 == 3:
                        mm.then_inc(pv_s, 1)

                def slot(b, g, base, place, s, jobs):
                    pe.wait_ge(nin_s, b * (G * 48) + (g + 1) * 48)
                    for n in range(UNITS):
                        scores_of(b, g, n)
                        for j in jobs[n][:2]:
                            fill(b, base, place, s, n, j)
                        if n >= 4:
                            products(b, g, n - 4)
                        elif g:
                            products(b, g - 1, UNITS - 4 + n)
                        for j in jobs[n][2:]:
                            fill(b, base, place, s, n, j)

                if biased:
                    pe.matmul(O[:, 0:D], ones[0:1, :], bv[:], start=True, stop=True).then_inc(bvf_s, 1)
                for j in first[0][0]:
                    fill(0, 0, pos[0], 0, 0, j)
                pe.wait_ge(made, 3)
                pe.wait_ge(wo_s, 16 * len(wo_loads))
                slot(0, 0, 0, pos[0], 1, first[1])
                with pe.Fori(0, B - 1) as b:
                    for s in range(G):
                        slot(b, s + 1, base_of[1](b), pos[1], s, middle[s])
                for s in range(G - 1):
                    slot(B - 1, s + 1, base_of[2](0), pos[2], s, last[s])
                for n in range(UNITS - 4, UNITS):
                    products(B - 1, G - 1, n)
                for j in last[G - 1][0]:
                    fill(B - 1, base_of[2](0), pos[2], G - 1, 0, j)

            @block.scalar
            def _(act):
                def take(b, g):
                    act.wait_ge(pv_s, b * (4 * G) + (g + 1) * 4)
                    act.wait_ge(at_s, b * G + g - 1 + AHEAD)
                    act.copy(osb[:, g % 2, :], O).then_inc(o_free, 1)

                def slot(b, g):
                    for n in range(UNITS):
                        act.wait_ge(s_full, b * (G * UNITS) + (g * UNITS + n + 1))
                        if g or n >= NE:
                            act.wait_ge(pv_s, b * (4 * G) + (4 * g + n // 4 - 1))
                        act.activation(ex[:, n % NE, :], scores[n % 2], ACT.Exp, scale=scale).then_inc(s_exp, 1)
                        if g and n == 4:
                            take(b, g - 1)

                act.copy(cb[:], ctxT[:, :, 0:SK]).then_inc(cb_s, 1)
                if masked:
                    act.wait_ge(mk_s, 2)
                slot(0, 0)
                with act.Fori(0, B - 1) as b:
                    for s in range(G):
                        slot(b, s + 1)
                for s in range(G - 1):
                    slot(B - 1, s + 1)
                take(B - 1, G - 1)

            @block.vector
            def _(dve):
                if masked:
                    dve.wait_ge(w_in, 16 * len(loads))
                    dve.tensor_scalar(biasq[:], mraw[:], BIG, -BIG, ALU.mult, ALU.add).then_inc(mk_s, 1)
                    dve.tensor_reduce(any_[:], mraw[:], AX.X, ALU.max).then_inc(mk_s, 1)
                    for kt in range(KT):
                        dve.wait_ge(mk_full, kt + 1)
                        dve.tensor_copy(biask[:, kt, :], PS[:, kt % 4, :].bitcast(BF16)[:, 0:S]).then_inc(mk_s, 1)
                    dve.wait_ge(mk_s, 2 + KT)
                if biased:
                    dve.wait_ge(bvf_s, 1)
                    dve.tensor_copy(bvb[:], O[:, 0:D]).then_inc(bvb_s, 1)
                    dve.wait_ge(bvb_s, 1)
                dve.wait_ge(made, 1)

                def empty(ch, b, base, at, job):
                    if job[0] == "neg":
                        V.wait_done(dve, base, at - 1)
                        ch.mark(dve.tensor_reduce(nm[:], mx[:], AX.X, ALU.max, negate=True))
                        ch.wait()
                        ch.mark(dve.tensor_copy(nsp[:, :, 0, :], nm[:]))
                        ch.wait()
                        ch.mark(dve.tensor_tensor(nr[:], nm[:], nsp[:, :, 0, :], ALU.subtract))
                        ch.wait()
                        ch.mark(dve.tensor_copy(nsp[:, :, 1, :], nr[:]))
                        ch.wait()
                        dve.tensor_tensor(nsp[:, :, 2, :], nr[:], nsp[:, :, 1, :], ALU.subtract).then_inc(nr_s, 1)
                    V.wait_full(dve, base, at)
                    o = V.bank(at)
                    if job[0] == "v":
                        g = job[1]
                        _, pair, half = v_part(g)
                        if g in (2, G):
                            dve.wait_ge(pv_s, b * (4 * G) + 4 * g)
                        for u in range(2):
                            dst = v[:, 2 * pair + u, half * (KT // 2):(half + 1) * (KT // 2), :, 0:HD]
                            src = o.rearrange("p (t u j d) -> p u t j d", t=KT // 2, u=2, j=4)[:, u]
                            if biased:
                                bias = bvb[:, (2 * pair + u) * 4 * HD:(2 * pair + u + 1) * 4 * HD].rearrange("p (j d) -> p j d", j=4)
                                ins = dve.tensor_tensor(dst, src, bias[:, None, :, :].broadcast_to([P, KT // 2, 4, HD]), ALU.add)
                            else:
                                ins = dve.tensor_copy(dst, src)
                        ins.then_inc(V.free, 1)
                    elif job[0] == "max":
                        i = job[2]
                        j, q, n = i // (2 * QT), i // 2 % QT, i % 2
                        if masked:
                            split_wait(dve, K["passed"])
                            dve.tensor_tensor_reduce(o, o, biasq[:, q, n * 512:(n + 1) * 512], 1.0, -3e38,
                                                     ALU.add, ALU.max, mx[:, q, j, n:n + 1]).then_inc(V.free, 1)
                        else:
                            dve.reduce_max(mx[:, q, j, n:n + 1], o, AX.X).then_inc(V.free, 1)
                    elif job[0] == "neg":
                        g = job[1]
                        if g:
                            dve.wait_ge(nin_s, b * (G * 48) + g * 48)
                        dve.tensor_copy(nT[:], o.bitcast(BF16)[0:12, 0:S]).then_inc(nt_s, 1)
                        dve.wait_ge(nt_s, b * G + g + 1)
                        dve.sem_inc(V.free, 1)
                    elif job[0] == "sum":
                        o = o[:, 0:4 * QT].rearrange("p (q j) -> p q j", q=QT)
                        ch.mark(dve.reciprocal(rc[:], o))
                        ch.wait()
                        if masked:
                            ch.mark(dve.tensor_tensor(rc[:], rc[:], any_[:, :, None].broadcast_to([P, QT, 4]), ALU.mult))
                            ch.wait()
                        dve.tensor_copy(rcw[:].rearrange("p q (j c) -> p q j c", j=4),
                                        rc[:, :, :, None].broadcast_to([P, QT, 4, CW])).then_inc(V.free, 1)
                    elif job[0] == "share":
                        g = job[1]
                        dve.tensor_tensor(aT[:, g, :], osb[:, g % 2, :], o, ALU.mult).then_inc(at_s, 1)
                        dve.wait_ge(at_s, b * G + g + 1 + AHEAD)
                        dve.sem_inc(V.free, 1)
                    elif job[0] == "skip":
                        V.wait_done(dve, base, at - 1)
                        dve.sem_inc(V.free, 1)
                    else:
                        x = X[:, ds(b * QT + job[1], 1), :]
                        dve.tensor_tensor(x, x, o[:, None, 0:D], ALU.add).then_inc(V.free, 1)

                def turn(b, which, place, ch):
                    for (s, n, j), at in place.items():
                        empty(ch, b, base_of[which](b), at, j)

                PER_SUM = 2 if masked else 1
                chains = [sum(4 if j[0] == "neg" else PER_SUM if j[0] == "sum" else 0 for _, _, j in p) for p in pos]
                turn(0, 0, pos[0], Chain(dve, ch_s, 0))
                with dve.Fori(0, B - 1) as b:
                    ch = Chain(dve, ch_s, b * chains[1] + chains[0])
                    turn(b, 1, pos[1], ch)
                    assert ch.n == chains[1], (ch.n, chains)
                turn(B - 1, 2, pos[2], Chain(dve, ch_s, (B - 1) * chains[1] + chains[0]))


def experts(K, name, act_fn, by_expert):
    nc, t, sb, sem = (K[n] for n in ("nc", "t", "sb", "sem"))
    pre = name + "f_"
    names = {"L1": ("L1_ffn_router_w", "L1_ffn_w1", "L1_ffn_b1", "L1_ffn_w2", "L1_ffn_b2"),
             "L2": ("L2_ffn_gate_w", "L2_ffn_fc1s", "L2_ffn_b1s", "L2_ffn_fc2s", "L2_ffn_b2s"),
             "L3": ("L3_ffn_router_w", "L3_ffn_expert_w1", "L3_ffn_expert_b1", "L3_ffn_expert_w2", "L3_ffn_expert_b2")}[name]
    NB = NT if by_expert else 2 * NT + E
    table = nc.dram_tensor(pre + "table", (NT * P + P, D), F32, kind="Internal").ap()
    total = nc.dram_tensor(pre + "total", (NT * P + P, D), F32, kind="Internal").ap()
    with ExitStack() as c:
        M = {"pre": pre, "NB": NB, "by_expert": by_expert, "table": table, "total": total, "act_fn": act_fn,
             "t_r": t[names[0]], "t_w1": t[names[1]], "t_b1": t[names[2] + "_cols"], "t_w2": t[names[3]], "t_b2": t[names[4]]}
        M["w1"] = sb(c, pre + "w1", [P, E, DT, F]); M["w2"] = sb(c, pre + "w2", [P, E, FT, D])
        M["b1"] = sb(c, pre + "b1", [P, E, FT]); M["b2"] = sb(c, pre + "b2", [1, E, D])
        M["w_in"] = sem(pre + "weights_in")
        M["lnw"] = sb(c, pre + "lnw", [P, DT]); M["lnb"] = sb(c, pre + "lnb", [P, DT])
        M["index"] = sb(c, pre + "index", [P, NB], I32)
        M["slot_gate"] = sb(c, pre + "slot_gate", [P, NB])
        M["block_expert"] = sb(c, pre + "block_expert", [P, NB], I32)
        with ExitStack() as c2:
            gate = sb(c2, pre + "gate", [P, NT, E]); chosen = sb(c2, pre + "chosen", [P, NT, E])
            if not by_expert:
                M["top"] = sb(c2, pre + "top", [P, NT, E])
            route(K, M, gate, chosen)
            if by_expert:
                choose_tokens(K, pre, gate, chosen)
            list_slots(K, M, gate, chosen)
        run_blocks(K, M)


def route(K, M, gate, chosen):
    nc, t, sb, sem, PS, X = (K[n] for n in ("nc", "t", "sb", "sem", "PS", "X"))
    ident, eps = K["ident"], K["eps"]
    pre, by_expert, table, total = M["pre"], M["by_expert"], M["table"], M["total"]
    logits = PS[:, 4, 0:NT * E].rearrange("p (t e) -> p t e", t=NT)
    with ExitStack() as c:
        rw = sb(c, pre + "rw", [P, DT, E])
        xn = sb(c, pre + "xn", [P, 2, QT, D]); xT = sb(c, pre + "xT", [P, DT, S])
        st = sb(c, pre + "st", [P, NT, 6]); mv = sb(c, pre + "mv", [P, NT, 2])
        std = sb(c, pre + "std", [P, NT]); rstd = sb(c, pre + "rstd", [P, NT]); zero = sb(c, pre + "zero", [P, D])
        if by_expert:
            st2 = sb(c, pre + "st2", [P, NT, 6]); mv2 = sb(c, pre + "mv2", [P, NT, 2])
            std2 = sb(c, pre + "std2", [P, NT]); rstd2 = sb(c, pre + "rstd2", [P, NT]); xn2 = sb(c, pre + "xn2", [P, 1, QT, D])
        rows, NR = (xn2, 1) if by_expert else (xn, 2)
        w_in, ch_s, std_s, mv_s, xn_s, rows_s, lgt_s, mv2_s, std2_s, tot_s, zr_s, x_s = (sem(pre + n) for n in (
            "router_in", "dve_chain", "std_ready", "var_ready", "xn_ready", "table_rows_ready", "logits_made", "var2_ready",
            "std2_ready", "total_stored", "zeros_made", "x_ready"))
        tab_s = [sem(pre + "table_stored%d" % n) for n in range(2)]

        def wait_stored(eng, b):
            eng.wait_ge(tab_s[b % 2], 16 * (b // 2 + 1))

        A = Flow([PS[:, 0, :], PS[:, 1, :]], sem(pre + "r_act_full"), sem(pre + "r_act_free"))
        V = Flow([PS[:, 2, :], PS[:, 3, :]], sem(pre + "r_dve_full"), sem(pre + "r_dve_free"))
        with nc.Block() as block:
            @block.sync
            def _(sp):
                sp.dma_start(rw[:], M["t_r"].rearrange("(k p) n -> p k n", p=P)).then_inc(w_in, 16)
                if by_expert:
                    sp.dma_start(M["lnw"][:], t["L2_ffn_ln_w_cols"]).then_inc(w_in, 16)
                    sp.dma_start(M["lnb"][:], t["L2_ffn_ln_b_cols"]).then_inc(w_in, 16)
                sp.dma_start(M["b1"][:], M["t_b1"].rearrange("e p k -> p e k")).then_inc(M["w_in"], 16)
                sp.dma_start(M["b2"][:], M["t_b2"].rearrange("(a e) n -> a e n", a=1)).then_inc(M["w_in"], 16)
                sp.wait_ge(zr_s, 1)
                sp.dma_start(table[NT * P:NT * P + P, :], zero[:]).then_inc(tot_s, 16)
                sp.dma_start(total[NT * P:NT * P + P, :], zero[:]).then_inc(tot_s, 16)
                for b in range(B):
                    sp.wait_ge(rows_s, b + 1)
                    sp.dma_start(table[b * S:(b + 1) * S, :].rearrange("(k p) d -> p k d", p=P), rows[:, b % NR, :, :]).then_inc(tab_s[b % 2], 16)
                if by_expert:
                    sp.wait_ge(x_s, B)
                sp.dma_start(total[0:NT * P, :].rearrange("(k p) d -> p k d", p=P), X[:]).then_inc(tot_s, 16)
                for e in range(E):
                    sp.dma_start(M["w1"][:, e, :, :], M["t_w1"][e].rearrange("(k p) n -> p k n", p=P)).then_inc(M["w_in"], 16)
                    sp.dma_start(M["w2"][:, e, :, :], M["t_w2"][e].rearrange("(k p) n -> p k n", p=P)).then_inc(M["w_in"], 16)
                sp.wait_ge(tot_s, 48)
                wait_stored(sp, B - 2)
                wait_stored(sp, B - 1)

            @block.gpsimd
            def _(pool):
                A.start(pool)
                V.start(pool)
                pool.memset(zero[:], 0.0).then_inc(zr_s, 1)

            @block.tensor
            def _(pe):
                pe.wait_ge(w_in, 48 if by_expert else 16)

                def turn(b):
                    pe.wait_ge(xn_s, b + 1)
                    for f, R in enumerate((A, V)):
                        R.wait_free(pe, 0, b)
                        for k in range(QT):
                            mm = pe.transpose(R.bank(b)[:, k * P:(k + 1) * P], xn[:, b % 2, k, f * P:(f + 1) * P], ident[:])
                        mm.then_inc(R.full, 1)

                turn(0)
                for b in range(B):
                    if b + 1 < B:
                        turn(b + 1)
                    A.wait_done(pe, 0, b)
                    V.wait_done(pe, 0, b)
                    for q in range(QT):
                        for k in range(DT):
                            mm = pe.matmul(logits[:, b * QT + q, :], xT[:, k, q * P:(q + 1) * P], rw[:, k, :],
                                           start=(k == 0), stop=(k == DT - 1), skip_group_check=True)
                    mm.then_inc(lgt_s, 1)

            @block.scalar
            def _(act):
                act.wait_ge(mv_s, 1)
                act.activation(std[:], mv[:, :, 1], ACT.Sqrt, bias=eps[:]).then_inc(std_s, 1)
                for b in range(B):
                    if by_expert:
                        act.wait_ge(mv2_s, b + 1)
                        bs = slice(b * QT, b * QT + QT)
                        act.activation(std2[:, bs], mv2[:, bs, 1], ACT.Sqrt, bias=eps[:]).then_inc(std2_s, 1)
                    A.wait_full(act, 0, b)
                    if b:
                        act.wait_ge(lgt_s, b)
                    act.copy(xT[:, 0, :], A.bank(b)).then_inc(A.free, 1)

            @block.vector
            def _(dve):
                ch = Chain(dve, ch_s)
                for k in range(NT):
                    ch.mark(dve.bn_stats(st[:, k, :], X[:, k, :]))
                ch.wait()
                for k in range(NT):
                    ins = dve.bn_aggr(mv[:, k, :], st[:, k, :])
                    if k < NT - 1:
                        ch.mark(ins)
                ins.then_inc(mv_s, 1)
                dve.wait_ge(mv_s, 1)
                dve.wait_ge(std_s, 1)
                ch.mark(dve.reciprocal(rstd[:], std[:]))
                ch.wait()

                def normalise(b):
                    if b >= 2:
                        V.wait_full(dve, 0, b - 2)
                        if not by_expert:
                            wait_stored(dve, b - 2)
                    for k in range(QT):
                        n = b * QT + k
                        ins = dve.tensor_scalar(xn[:, b % 2, k, :], X[:, n, :], mv[:, n, 0:1], rstd[:, n:n + 1],
                                                ALU.subtract, ALU.mult)
                        if k < QT - 1:
                            ch.mark(ins)
                    ins.then_inc(xn_s, 1)
                    dve.wait_ge(xn_s, b + 1)
                    if not by_expert:
                        dve.sem_inc(rows_s, 1)

                def second(b):
                    for k in range(QT):
                        ch.mark(dve.bn_stats(st2[:, b * QT + k, :], xn[:, b % 2, k, :]))
                    ch.wait()
                    for k in range(QT):
                        ins = dve.bn_aggr(mv2[:, b * QT + k, :], st2[:, b * QT + k, :])
                        if k < QT - 1:
                            ch.mark(ins)
                    ins.then_inc(mv2_s, 1)

                def table_rows(b):
                    bs = slice(b * QT, b * QT + QT)
                    dve.wait_ge(std2_s, b + 1)
                    dve.wait_ge(mv2_s, b + 1)
                    ch.mark(dve.reciprocal(rstd2[:, bs], std2[:, bs]))
                    ch.wait()
                    if b:
                        wait_stored(dve, b - 1)
                    for k in range(QT):
                        n = b * QT + k
                        ins = dve.tensor_scalar(xn2[:, 0, k, :], xn[:, b % 2, k, :], mv2[:, n, 0:1], rstd2[:, n:n + 1],
                                                ALU.subtract, ALU.mult)
                        if k < QT - 1:
                            ch.mark(ins)
                    ins.then_inc(rows_s, 1)
                    dve.tensor_tensor(X[:, bs, :], X[:, bs, :], xn[:, b % 2, :, :], ALU.add).then_inc(x_s, 1)
                    dve.wait_ge(x_s, b + 1)

                for b in range(B):
                    normalise(b)
                    if by_expert:
                        second(b)
                    V.wait_full(dve, 0, b)
                    if b:
                        dve.wait_ge(lgt_s, b)
                    dve.tensor_copy(xT[:, 1, :], V.bank(b)).then_inc(V.free, 1)
                    if by_expert:
                        table_rows(b)
                dve.wait_ge(lgt_s, B)
    with ExitStack() as c:
        lg = sb(c, pre + "lg", [P, NT, E]); lm = sb(c, pre + "lm", [P, NT]); ls = sb(c, pre + "ls", [P, NT])
        ch_s, lg_s, le_s, made = (sem(pre + n) for n in ("g_chain", "logits_shifted", "exp_ready", "order_made"))
        if not by_expert:
            rank = sb(c, pre + "rank", [P, NT, E])
            gt = sb(c, pre + "gt", [P, NT, E, E]); eq = sb(c, pre + "eq", [P, NT, E, E]); first = sb(c, pre + "first", [P, E, E])
            one = sb(c, pre + "one", [P, E, E])
        spread = lambda a: a[:, :, None].broadcast_to([P, NT, E])
        with nc.Block() as block:
            @block.gpsimd
            def _(pool):
                if not by_expert:
                    pool.memset(one[:], 1.0).then_inc(made, 1)
                    pool.wait_ge(made, 1)
                    pool.affine_select(out=first[:], in_=one[:], compare_op=ALU.is_gt, fill=0.0, base=0,
                                       pattern=[[1, E], [-1, E]], channel_multiplier=0).then_inc(made, 1)

            @block.scalar
            def _(act):
                act.wait_ge(lg_s, 1)
                act.activation(lg[:], lg[:], ACT.Exp).then_inc(le_s, 1)

            @block.vector
            def _(dve):
                ch = Chain(dve, ch_s)

                def do(ins):
                    ch.mark(ins)
                    ch.wait()

                do(dve.tensor_reduce(lm[:], logits, AX.X, ALU.max))
                dve.tensor_tensor(lg[:], logits, spread(lm), ALU.subtract).then_inc(lg_s, 1)
                dve.wait_ge(le_s, 1)
                do(dve.tensor_reduce(ls[:], lg[:], AX.X, ALU.add))
                do(dve.reciprocal(ls[:], ls[:]))
                if by_expert:
                    do(dve.tensor_tensor(gate[:], lg[:], spread(ls), ALU.mult))
                else:
                    do(dve.tensor_tensor(lg[:], lg[:], spread(ls), ALU.mult))
                    mine = lg[:, :, :, None].broadcast_to([P, NT, E, E])
                    other = lg[:, :, None, :].broadcast_to([P, NT, E, E])
                    ch.mark(dve.tensor_tensor(gt[:], other, mine, ALU.is_gt))
                    do(dve.tensor_tensor(eq[:], other, mine, ALU.is_equal))
                    dve.wait_ge(made, 2)
                    do(dve.tensor_tensor(eq[:], eq[:], first[:, None, :, :].broadcast_to([P, NT, E, E]), ALU.mult))
                    do(dve.tensor_tensor(gt[:], gt[:], eq[:], ALU.add))
                    do(dve.tensor_reduce(rank[:], gt[:], AX.X, ALU.add))
                    do(dve.tensor_scalar(chosen[:], rank[:], 1.5, None, ALU.is_lt))
                    do(dve.tensor_scalar(M["top"][:], rank[:], 0.5, None, ALU.is_lt))
                    do(dve.tensor_tensor(lg[:], lg[:], chosen[:], ALU.mult))
                    do(dve.tensor_reduce(lm[:], lg[:], AX.X, ALU.add))
                    do(dve.tensor_scalar(lm[:], lm[:], 1e-9, None, ALU.add))
                    do(dve.reciprocal(ls[:], lm[:]))
                    do(dve.tensor_tensor(gate[:], lg[:], spread(ls), ALU.mult))


def list_slots(K, M, gate, chosen):
    nc, sb, sem, PS, ones = (K[n] for n in ("nc", "sb", "sem", "PS", "ones"))
    pre, NB = M["pre"], M["NB"]
    NF = 6
    by_expert = M["by_expert"]
    A, H = (E, E // 2) if by_expert else (2, 2)
    parts = [(k, a) for k in range(NT) for a in range(0, A, H)]
    with ExitStack() as c:
        low = sb(c, pre + "s_low", [P, P]); tot = sb(c, pre + "s_tot", [P, NT, E]); pos = sb(c, pre + "s_pos", [P, NT, E])
        posi = sb(c, pre + "s_posi", [P, NT, E], I32); rowi = sb(c, pre + "s_rowi", [P, NT, E], I32)
        row = sb(c, pre + "s_row", [P, NT, E]); blk = sb(c, pre + "s_blk", [P, NT, E]); cnt = sb(c, pre + "s_cnt", [P, E])
        step = sb(c, pre + "s_step", [P, E, NT]); over = sb(c, pre + "s_over", [P, E, NT]); nblk = sb(c, pre + "s_nblk", [P, E])
        start = sb(c, pre + "s_start", [P, E])
        iota_i = sb(c, pre + "s_iotai", [P, P], I32); iota_r = sb(c, pre + "s_iotar", [P, P]); part_i = sb(c, pre + "s_parti", [P, 1], I32)
        part = sb(c, pre + "s_part", [P, 1]); spare = sb(c, pre + "s_spare", [P, 1])
        fields = sb(c, pre + "s_fields", [P, NT, A, NF], BF16); g1 = sb(c, pre + "s_g1", [P, NT, E])
        g2 = sb(c, pre + "s_g2", [P, NT])
        ga = sb(c, pre + "s_ga", [P, NT, A]) if A < E else gate
        rowb = sb(c, pre + "s_rowb", [P, NT, A], BF16); blkb = sb(c, pre + "s_blkb", [P, NT, A], BF16); iota_b = sb(c, pre + "s_iotab", [P, P], BF16)
        oh_r = sb(c, pre + "s_ohr", [P, 2, H, P], BF16); oh_b = sb(c, pre + "s_ohb", [P, 2, H, NB], BF16)
        fb = sb(c, pre + "s_fb", [P, 2, H, NB * NF], BF16)
        res = sb(c, pre + "s_res", [P, NB, NF]); tok = sb(c, pre + "s_tok", [P, NB]); tok2 = sb(c, pre + "s_tok2", [P, NB])
        be = sb(c, pre + "s_be", [P, NB, E]); bs = sb(c, pre + "s_bs", [P, NB])
        made, ch_s, full, hot_s, res_s = (sem(pre + n) for n in ("s_made", "s_chain", "s_full", "s_onehots", "s_listed"))
        with nc.Block() as block:
            @block.gpsimd
            def _(pool):
                pool.affine_select(out=low[:], in_=ones[:], compare_op=ALU.is_gt, fill=0.0, base=0,
                                   pattern=[[1, P]], channel_multiplier=-1).then_inc(made, 1)
                pool.iota(iota_i[:], [[1, P]], base=0, channel_multiplier=0).then_inc(made, 1)
                pool.iota(part_i[:], [[0, 1]], base=0, channel_multiplier=1).then_inc(made, 1)

            @block.tensor
            def _(pe):
                pe.wait_ge(made, 3)
                flat = chosen[:].rearrange("p t e -> p (t e)")
                pe.matmul(PS[:, 1, 0:NT * E], low[:], flat, start=True, stop=True).then_inc(full, 1)
                pe.matmul(PS[:, 2, 0:NT * E], ones[:], flat, start=True, stop=True).then_inc(full, 1)
                for n in range(len(parts)):
                    pe.wait_ge(hot_s, n + 1)
                    for e in range(H):
                        mm = pe.matmul(PS[:, 3, 0:NB * NF], oh_r[:, n % 2, e, :], fb[:, n % 2, e, :],
                                       start=(n == 0 and e == 0), stop=(n == len(parts) - 1 and e == H - 1))
                    mm.then_inc(res_s, 1)

            @block.vector
            def _(dve):
                ch = Chain(dve, ch_s)

                def do(ins):
                    ch.mark(ins)
                    ch.wait()

                dve.wait_ge(made, 3)
                do(dve.tensor_copy(iota_r[:], iota_i[:]))
                do(dve.tensor_copy(part[:], part_i[:]))
                do(dve.tensor_scalar(spare[:], part[:], float(NT * P), None, ALU.add))
                do(dve.tensor_scalar(step[:], iota_r[:, None, 0:NT].broadcast_to([P, E, NT]), float(P), None, ALU.mult))
                dve.wait_ge(full, 2)
                do(dve.tensor_copy(tot[:].rearrange("p t e -> p (t e)"), PS[:, 2, 0:NT * E]))
                do(dve.memset(pos[:, 0, :], 0.0))
                for k in range(1, NT):
                    do(dve.tensor_tensor(pos[:, k, :], pos[:, k - 1, :], tot[:, k - 1, :], ALU.add))
                do(dve.tensor_tensor(cnt[:], pos[:, NT - 1, :], tot[:, NT - 1, :], ALU.add))
                do(dve.tensor_tensor(pos[:], pos[:], PS[:, 1, 0:NT * E].rearrange("p (t e) -> p t e", t=NT), ALU.add))
                do(dve.tensor_tensor(over[:], cnt[:, :, None].broadcast_to([P, E, NT]), step[:], ALU.is_gt))
                do(dve.tensor_reduce(nblk[:], over[:], AX.X, ALU.add))
                do(dve.memset(start[:, 0:1], 0.0))
                for e in range(1, E):
                    do(dve.tensor_tensor(start[:, e:e + 1], start[:, e - 1:e], nblk[:, e - 1:e], ALU.add))
                do(dve.tensor_copy(posi[:], pos[:]))
                do(dve.tensor_single_scalar(rowi[:], posi[:], P - 1, ALU.bitwise_and))
                do(dve.tensor_single_scalar(posi[:], posi[:], 7, ALU.arith_shift_right))
                do(dve.tensor_copy(row[:], rowi[:]))
                do(dve.tensor_copy(blk[:], posi[:]))
                do(dve.tensor_tensor(blk[:], blk[:], start[:, None, :].broadcast_to([P, NT, E]), ALU.add))
                if A == E:
                    do(dve.tensor_scalar(g1[:], chosen[:], -1000.0, 1000.0, ALU.mult, ALU.add))
                    do(dve.tensor_tensor(rowb[:], row[:], g1[:], ALU.add))
                    ch.mark(dve.tensor_copy(blkb[:], blk[:]))
                else:
                    top = M["top"]
                    do(dve.tensor_tensor(chosen[:], chosen[:], top[:], ALU.subtract))
                    for a, which in enumerate((top, chosen)):
                        for src, dst in ((row, rowb), (blk, blkb), (gate, ga)):
                            do(dve.tensor_tensor(g1[:], src[:], which[:], ALU.mult))
                            do(dve.tensor_reduce(g2[:], g1[:], AX.X, ALU.add))
                            do(dve.tensor_copy(dst[:, :, a], g2[:]))
                do(dve.tensor_copy(iota_b[:], iota_r[:]))
                rest = g1[:, :, 0:A]
                do(dve.tensor_copy(fields[:, :, :, 0], iota_r[:, 0:NT, None].broadcast_to([P, NT, A])))
                do(dve.tensor_copy(fields[:, :, :, 1], part[:, :, None].broadcast_to([P, NT, A])))
                do(dve.memset(fields[:, :, :, 2], 1.0))
                do(dve.tensor_copy(fields[:, :, :, 3], ga[:]))
                do(dve.tensor_tensor(rest, ga[:], fields[:, :, :, 3], ALU.subtract))
                do(dve.tensor_copy(fields[:, :, :, 4], rest))
                do(dve.tensor_tensor(fields[:, :, :, 5], rest, fields[:, :, :, 4], ALU.subtract))
                do(dve.tensor_tensor(be[:], start[:, None, :].broadcast_to([P, NB, E]),
                                     iota_r[:, 0:NB, None].broadcast_to([P, NB, E]), ALU.is_le))
                do(dve.tensor_reduce(bs[:], be[:], AX.X, ALU.add))
                do(dve.tensor_scalar(bs[:], bs[:], -1.0, None, ALU.add))
                do(dve.tensor_copy(M["block_expert"][:], bs[:]))
                for n, (k, a) in enumerate(parts):
                    h, es = n % 2, slice(a, a + H)
                    if n >= 2:
                        dve.wait_ge(res_s, n - 1)
                    ch.mark(dve.tensor_tensor(oh_r[:, h, :, :], iota_b[:, None, :].broadcast_to([P, H, P]),
                                              rowb[:, k, es, None].broadcast_to([P, H, P]), ALU.is_equal))
                    do(dve.tensor_tensor(oh_b[:, h, :, :], iota_b[:, None, 0:NB].broadcast_to([P, H, NB]),
                                         blkb[:, k, es, None].broadcast_to([P, H, NB]), ALU.is_equal))
                    dve.tensor_tensor(fb[:, h, :, :].rearrange("p e (b f) -> p e b f", f=NF),
                                      oh_b[:, h, :, :, None].broadcast_to([P, H, NB, NF]),
                                      fields[:, k, es, None, :].broadcast_to([P, H, NB, NF]), ALU.mult).then_inc(hot_s, 1)
                dve.wait_ge(res_s, len(parts))
                do(dve.tensor_copy(res[:].rearrange("p b f -> p (b f)"), PS[:, 3, 0:NB * NF]))
                do(dve.scalar_tensor_tensor(out=tok[:], in0=res[:, :, 0], scalar=float(P), in1=res[:, :, 1], op0=ALU.mult, op1=ALU.add))
                do(dve.tensor_scalar(tok2[:], res[:, :, 2], -1.0, 1.0, ALU.mult, ALU.add))
                do(dve.scalar_tensor_tensor(out=tok[:], in0=tok2[:], scalar=spare[:], in1=tok[:], op0=ALU.mult, op1=ALU.add))
                do(dve.tensor_copy(M["index"][:], tok[:]))
                do(dve.tensor_tensor(tok[:], res[:, :, 3], res[:, :, 4], ALU.add))
                do(dve.tensor_tensor(M["slot_gate"][:], tok[:], res[:, :, 5], ALU.add))


def run_blocks(K, M):
    nc, t, sb, sem, PS, X, ident, ones = (K[n] for n in ("nc", "t", "sb", "sem", "PS", "X", "ident", "ones"))
    pre, NB, table, total, by_expert = M["pre"], M["NB"], M["table"], M["total"], M["by_expert"]
    w1, w2, b1, b2, index, sg, be = (M[n] for n in ("w1", "w2", "b1", "b2", "index", "slot_gate", "block_expert"))
    w1f = w1[:, :, :, :].rearrange("p e k n -> p (e k n)")
    w2f = w2[:, :, :, :].rearrange("p e k n -> p (e k n)")
    b1f = b1[:, :, :].rearrange("p e k -> p (e k)")
    b2f = b2[:, :, :].rearrange("p e n -> p (e n)")
    with ExitStack() as c:
        AHEAD = 4
        xg = sb(c, pre + "xg", [P, AHEAD, D]); xgT = sb(c, pre + "xgT", [P, 2, DT * P])
        hb = sb(c, pre + "hb", [P, F]); hT = sb(c, pre + "hT", [P, FT, P]); yo = sb(c, pre + "yo", [P, 2, D])
        ig = sb(c, pre + "ig", [P, AHEAD], I32); isc = sb(c, pre + "isc", [P, 2], I32)
        gathered = [sem(pre + "gathered%d" % n) for n in range(AHEAD)]
        (cp_s, sc_s, x_full, x_done, h_full, h_done, t_full, t_done, y_full, y_done, back) = (sem(pre + n) for n in (
            "index_copied", "added", "rows_turned", "rows_ready", "hidden_full", "hidden_ready",
            "hidden_turned", "activated", "output_full", "output_ready", "x_back"))
        X_BANK, H_BANK, T_BANK, Y_BANK = (0, 7), 1, 3, (5, 6)
        LOOPS = (NB - 2) // 2
        with nc.Block() as block:
            @block.gpsimd
            def _(pool):
                def gather(j, buf, n):
                    pool.tensor_copy(ig[:, buf:buf + 1], index[:, ds(j, 1)]).then_inc(cp_s, 1)
                    pool.wait_ge(cp_s, n + 1)
                    split_wait(pool, K["passed"])
                    pool.indirect_dma_start(xg[:, buf, :], None, table, bass.IndirectOffsetOnAxis(ap=ig[:, buf:buf + 1], axis=0),
                                            bounds_check=NT * P + P - 1).then_inc(gathered[buf], 16)

                def add(j, par, n, first=False):
                    pool.tensor_copy(isc[:, par:par + 1], index[:, ds(j, 1)]).then_inc(cp_s, 1)
                    pool.wait_ge(cp_s, n + 1)
                    pool.wait_ge(y_done, j + 1)
                    if not first:
                        pool.wait_ge(sc_s, 16 * j)
                    split_wait(pool, K["passed"])
                    pool.indirect_dma_start(total, bass.IndirectOffsetOnAxis(ap=isc[:, par:par + 1], axis=0), yo[:, par, :], None,
                                            bounds_check=NT * P + P - 1, compute_op=ALU.add).then_inc(sc_s, 16)

                def four(i, first=False):
                    for buf in range(AHEAD):
                        j = i * AHEAD + buf
                        pool.wait_ge(x_full, j + 1)
                        split_wait(pool, K["passed"])
                        gather(j + AHEAD, buf, j * 2 + AHEAD)
                        add(j, buf % 2, j * 2 + AHEAD + 1, first and buf == 0)

                for j in range(AHEAD):
                    gather(j, j, j)
                four(0, True)
                with pool.Fori(1, NB // AHEAD - 1) as i:
                    four(i)
                for j in range(NB - AHEAD, NB):
                    add(j, j % 2, NB + j)

            @block.sync
            def _(sp):
                sp.wait_ge(sc_s, 16 * NB)
                sp.dma_start(X[:], total[0:NT * P, :].rearrange("(k p) d -> p k d", p=P)).then_inc(back, 16)
                sp.wait_ge(back, 16)

            @block.tensor
            def _(pe):
                pe.wait_ge(M["w_in"], 16 * (2 + 2 * E))

                def turn_rows(j, u, n):
                    pe.wait_ge(gathered[u], 16 * n)
                    for f in range(DT):
                        mm = pe.transpose(PS[:, X_BANK[u % 2], f * P:(f + 1) * P], xg[:, u, f * P:(f + 1) * P], ident[:])
                    mm.then_inc(x_full, 1)

                def hidden(j, par):
                    e = pe.value_load(be[0:1, ds(j, 1)], min_val=0, max_val=E - 1)
                    pe.wait_ge(x_done, j + 1)
                    for n in range(2):
                        for k in range(DT):
                            mm = pe.matmul(PS[:, H_BANK + n, :], xgT[:, par, k * P:(k + 1) * P],
                                           w1f[:, ds(e * (DT * F) + k * F + n * 512, 512)], start=(k == 0), stop=(k == DT - 1))
                    mm.then_inc(h_full, 1)

                def outward(j, par):
                    e = pe.value_load(be[0:1, ds(j, 1)], min_val=0, max_val=E - 1)
                    pe.wait_ge(t_done, j + 1)
                    o = PS[:, Y_BANK[par], 0:D]
                    pe.matmul(o, ones[0:1, :], b2f[:, ds(e * D, D)], start=True, stop=False)
                    for k in range(FT):
                        mm = pe.matmul(o, hT[:, k, :], w2f[:, ds(e * (FT * D) + k * D, D)], start=False, stop=(k == FT - 1))
                    mm.then_inc(y_full, 1)

                def turn_hidden(j):
                    pe.wait_ge(h_done, j + 1)
                    for m in range(FT):
                        mm = pe.transpose(PS[:, T_BANK + m // 4, (m % 4) * P:(m % 4 + 1) * P], hb[:, m * P:(m + 1) * P], ident[:])
                    mm.then_inc(t_full, 1)

                def step(j, u, n):
                    pe.wait_ge(x_done, j)
                    turn_rows(j + 1, (u + 1) % AHEAD, n)
                    hidden(j, u % 2)
                    outward(j - 1, 1 - u % 2)
                    turn_hidden(j)

                turn_rows(0, 0, 1)
                turn_rows(1, 1, 1)
                hidden(0, 0)
                turn_hidden(0)
                with pe.Fori(0, NB // AHEAD - 1) as i:
                    for u in range(AHEAD):
                        step(i * AHEAD + u + 1, (u + 1) % AHEAD, i + (u + 2) // AHEAD + 1)
                for j in (NB - 3, NB - 2):
                    step(j, j % AHEAD, (j + 1) // AHEAD + 1)
                hidden(NB - 1, 1)
                outward(NB - 2, 0)
                turn_hidden(NB - 1)
                outward(NB - 1, 1)

            @block.scalar
            def _(act):
                def activate(j):
                    e = act.value_load(be[0:1, ds(j, 1)], min_val=0, max_val=E - 1)
                    act.wait_ge(t_full, j + 1)
                    split_wait(act, K["passed"])
                    for m in range(FT):
                        ins = act.activation(hT[:, m, :], PS[:, T_BANK + m // 4, (m % 4) * P:(m % 4 + 1) * P], M["act_fn"],
                                             bias=b1f[:, ds(e * FT + m, 1)])
                    ins.then_inc(t_done, 1)

                activate(0)
                with act.Fori(0, LOOPS) as i:
                    activate(i * 2 + 1)
                    activate(i * 2 + 2)
                activate(NB - 1)

            @block.vector
            def _(dve):
                def rows(j, par):
                    dve.wait_ge(x_full, j + 1)
                    if by_expert:
                        for f in range(DT):
                            ins = dve.tensor_scalar(xgT[:, par, f * P:(f + 1) * P], PS[:, X_BANK[par], f * P:(f + 1) * P],
                                                    M["lnw"][:, f:f + 1], M["lnb"][:, f:f + 1], ALU.mult, ALU.add)
                    else:
                        ins = dve.tensor_copy(xgT[:, par, :], PS[:, X_BANK[par], 0:D])
                    ins.then_inc(x_done, 1)

                def hidden(j):
                    dve.wait_ge(h_full, j + 1)
                    dve.tensor_copy(hb[:].rearrange("p (b n) -> p b n", b=2), PS[:, H_BANK:H_BANK + 2, :]).then_inc(h_done, 1)

                def weigh(j, par, first=False):
                    dve.wait_ge(y_full, j + 1)
                    if not first:
                        dve.wait_ge(sc_s, 16 * j - 16)
                    split_wait(dve, K["passed"])
                    dve.tensor_scalar(yo[:, par, :], PS[:, Y_BANK[par], 0:D], sg[:, ds(j, 1)], None, ALU.mult).then_inc(y_done, 1)

                rows(0, 0)
                rows(1, 1)
                hidden(0)

                def pair(i, first=False):
                    for j, par in ((i * 2 + 1, 1), (i * 2 + 2, 0)):
                        dve.wait_ge(h_full, j)
                        rows(j + 1, 1 - par)
                        dve.wait_ge(t_full, j)
                        hidden(j)
                        weigh(j - 1, 1 - par, first)

                pair(0, True)
                with dve.Fori(1, LOOPS) as i:
                    pair(i)
                hidden(NB - 1)
                weigh(NB - 2, 0)
                weigh(NB - 1, 1)


def choose_tokens(K, pre, gate, chosen):
    nc, sb, sem, PS, ones = (K[n] for n in ("nc", "sb", "sem", "PS", "ones"))
    KEEP = NT * P // E
    with ExitStack() as c:
        thr = sb(c, pre + "thr", [P, E]); bit = sb(c, pre + "bit", [P, E], I32); cand = sb(c, pre + "cand", [P, E])
        ge = sb(c, pre + "ge", [P, NT, E]); cnt = sb(c, pre + "cnt", [P, E]); ok = sb(c, pre + "ok", [P, E])
        above = sb(c, pre + "above", [P, NT, E]); tie = sb(c, pre + "tie", [P, NT, E]); need = sb(c, pre + "need", [P, E])
        seen = sb(c, pre + "seen", [P, NT, E]); tot = sb(c, pre + "tot", [P, NT, E]); low = sb(c, pre + "low", [P, P])
        ch_s, cnt_s, sum_s, made = (sem(pre + n) for n in ("c_chain", "count_ready", "count_summed", "c_made"))
        BITS = 30
        PER = 6
        with nc.Block() as block:
            @block.gpsimd
            def _(pool):
                pool.affine_select(out=low[:], in_=ones[:], compare_op=ALU.is_gt, fill=0.0, base=0,
                                   pattern=[[1, P]], channel_multiplier=-1).then_inc(made, 1)

            @block.tensor
            def _(pe):
                with pe.Fori(0, BITS) as i:
                    pe.wait_ge(cnt_s, i + 1)
                    pe.matmul(PS[:, 0, 0:E], ones[:], cnt[:], start=True, stop=True).then_inc(sum_s, 1)
                pe.wait_ge(cnt_s, BITS + 1)
                pe.matmul(PS[:, 0, 0:E], ones[:], cnt[:], start=True, stop=True).then_inc(sum_s, 1)
                pe.wait_ge(cnt_s, BITS + 2)
                pe.wait_ge(made, 1)
                pe.matmul(PS[:, 1, 0:NT * E], low[:], tie[:].rearrange("p t e -> p (t e)"), start=True, stop=True).then_inc(sum_s, 1)
                pe.matmul(PS[:, 2, 0:NT * E], ones[:], tie[:].rearrange("p t e -> p (t e)"), start=True, stop=True).then_inc(sum_s, 1)

            @block.vector
            def _(dve):
                spread = lambda a: a[:, None, :].broadcast_to([P, NT, E])
                dve.memset(thr[:], 0.0).then_inc(ch_s, 1)
                dve.memset(bit[:], 1 << (BITS - 1)).then_inc(ch_s, 1)
                dve.wait_ge(ch_s, 2)
                with dve.Fori(0, BITS) as i:
                    ch = Chain(dve, ch_s, i * PER + 2)
                    ch.mark(dve.tensor_tensor(cand[:].bitcast(I32), thr[:].bitcast(I32), bit[:], ALU.bitwise_or))
                    ch.wait()
                    ch.mark(dve.tensor_tensor(ge[:], gate[:], spread(cand), ALU.is_ge))
                    ch.mark(dve.tensor_single_scalar(bit[:], bit[:], 1, ALU.logical_shift_right))
                    ch.wait()
                    dve.tensor_reduce(cnt[:], ge[:].rearrange("p t e -> p e t"), AX.X, ALU.add).then_inc(cnt_s, 1)
                    dve.wait_ge(sum_s, i + 1)
                    ch.mark(dve.tensor_scalar(ok[:], PS[:, 0, 0:E], KEEP - 0.5, None, ALU.is_ge))
                    ch.wait()
                    ch.mark(dve.tensor_tensor(cand[:], cand[:], ok[:], ALU.mult))
                    ch.wait()
                    ch.mark(dve.tensor_tensor(thr[:], thr[:], cand[:], ALU.max))
                    ch.wait()
                    assert ch.n == PER, ch.n
                ch = Chain(dve, ch_s, 2 + PER * BITS)
                ch.wait()
                ch.mark(dve.tensor_tensor(above[:], gate[:], spread(thr), ALU.is_gt))
                ch.mark(dve.tensor_tensor(tie[:], gate[:], spread(thr), ALU.is_equal))
                ch.wait()
                dve.tensor_reduce(cnt[:], above[:].rearrange("p t e -> p e t"), AX.X, ALU.add).then_inc(cnt_s, 2)
                dve.wait_ge(sum_s, BITS + 1)
                ch.mark(dve.tensor_scalar(need[:], PS[:, 0, 0:E], -1.0, float(KEEP), ALU.mult, ALU.add))
                dve.wait_ge(sum_s, BITS + 3)
                ch.mark(dve.tensor_copy(tot[:].rearrange("p t e -> p (t e)"), PS[:, 2, 0:NT * E]))
                ch.mark(dve.memset(seen[:, 0, :], 0.0))
                ch.wait()
                for k in range(1, NT):
                    ch.mark(dve.tensor_tensor(seen[:, k, :], seen[:, k - 1, :], tot[:, k - 1, :], ALU.add))
                    ch.wait()
                ch.mark(dve.tensor_tensor(seen[:], seen[:], PS[:, 1, 0:NT * E].rearrange("p (t e) -> p t e", t=NT), ALU.add))
                ch.wait()
                ch.mark(dve.tensor_tensor(seen[:], seen[:], spread(need), ALU.is_lt))
                ch.wait()
                ch.mark(dve.tensor_tensor(tie[:], tie[:], seen[:], ALU.mult))
                ch.wait()
                ch.mark(dve.tensor_tensor(chosen[:], above[:], tie[:], ALU.add))
                ch.wait()


def causal_attention(K):
    nc, t, sb, sem, PS, X, ctxT = (K[n] for n in ("nc", "t", "sb", "sem", "PS", "X", "ctxT"))
    ident, ones, eps = K["ident"], K["ones"], K["eps"]
    HD = 64
    M = H * HD // P
    SCALE = HD ** -0.5
    pre = "L3a_"
    ajobs = [("k", m) for m in range(M)] + [("xT",)] + [("q", m) for m in range(M)]
    vjobs = [("v", k, n) for k in range(QT) for n in range(2)] + [("xT",)]
    STEPS = H + 4
    for h in range(STEPS):
        if 2 <= h < H + 2:
            ajobs += [("turn", h - 2, q) for q in (1, 3)]
            vjobs += [("turn", h - 2, q) for q in (0, 2)]
    vjobs += [("y", q) for q in range(QT)]
    aat = {j: i for i, j in enumerate(ajobs)}
    vat = {j: i for i, j in enumerate(vjobs)}
    with ExitStack() as c:
        wq = sb(c, pre + "wq", [P, DT, H * HD]); wk = sb(c, pre + "wk", [P, DT, H * HD]); wv = sb(c, pre + "wv", [P, DT, H * HD])
        wo = sb(c, pre + "wo", [P, M, D])
        xT = sb(c, pre + "xT", [P, DT, S])
        qT = sb(c, pre + "qT", [P, M, S]); kT = sb(c, pre + "kT", [P, M, S]); v = sb(c, pre + "v", [P, QT, H * HD])
        keep = sb(c, pre + "keep", [P, S]); padi = sb(c, pre + "padi", [1, S], I32); padf = sb(c, pre + "padf", [1, S])
        bias = sb(c, pre + "bias", [P, QT, S], BF16); seen = sb(c, pre + "seen", [P, QT])
        causal = sb(c, pre + "causal", [P, QT, S], BF16)
        sm = sb(c, pre + "sm", [P, 2, QT, S]); pT = sb(c, pre + "pT", [P, 3, QT, S])
        nmx = sb(c, pre + "nmx", [P, 2, 4]); mx = sb(c, pre + "mx", [P, 2, 4]); su = sb(c, pre + "su", [P, 2, 4]); rs = sb(c, pre + "rs", [P, 2, 4])
        aT = sb(c, pre + "aT", [P, M, S])
        cb = sb(c, pre + "cb", [P, DT, S])
        vis = pT[:, 1, 0:2, :].rearrange("p a n -> p (a n)").bitcast(BF16).rearrange("p (q n) -> p q n", q=QT)
        xn = pT[:, 0, 0:DT, :].rearrange("p a n -> p (a n)").rearrange("p (q d) -> p q d", q=QT)
        st = sb(c, pre + "st", [P, QT, 6]); mv = sb(c, pre + "mv", [P, QT, 2])
        std = sb(c, pre + "std", [P, QT]); rstd = sb(c, pre + "rstd", [P, QT])
        (w_in, made, ch_s, std_s, mv_s, xn_s, cb_s, pad_s, padf_s, keep_s, bias_s, s_full, mx_s, s_free, exp_s, pn_s, pa_s, inv_s) = (
            sem(pre + n) for n in ("weights_in", "constants_made", "dve_chain", "std_ready", "var_ready", "xn_ready",
                                   "ctx_copied", "pad_in", "pad_ready", "keep_full", "bias_ready", "scores_full",
                                   "max_ready", "scores_read", "exp_done", "probs_scaled_dve",
                                   "probs_scaled_act", "sums_inverted"))
        A = Ring([PS[:, 0, :], PS[:, 1, :]], sem(pre + "act_full"), sem(pre + "act_free"), len(ajobs))
        V = Ring([PS[:, 2, :], PS[:, 3, :]], sem(pre + "dve_full"), sem(pre + "dve_free"), len(vjobs))
        scores = [PS[:, 4 + i, :] for i in range(3)]
        O = Ring([PS[:, 7, :]], sem(pre + "out_full"), sem(pre + "out_free"), M)
        keepbank = PS[:, 7, :]
        with nc.Block() as block:
            @block.sync
            def _(sp):
                for dst, src in ((wq, t["L3_xattn_Wq"]), (wk, t["L3_xattn_Wk"]), (wv, t["L3_xattn_Wv"]), (wo, t["L3_xattn_Wo"])):
                    sp.dma_start(dst[:], src.rearrange("(k p) n -> p k n", p=P)).then_inc(w_in, 16)
                with sp.Fori(0, B) as b:
                    V.wait_turns(sp, b)
                    sp.dma_start(padi[:], t["mask_BxS2_if1"][ds(b, 1), 0:S]).then_inc(pad_s, 16)

            @block.gpsimd
            def _(pool):
                A.start(pool)
                V.start(pool)
                O.start(pool)
                pool.memset(vis[:], 1.0).then_inc(made, 1)
                pool.wait_ge(made, 1)
                pool.affine_select(out=causal[:], in_=vis[:], compare_op=ALU.is_ge, fill=0.0, base=0,
                                   pattern=[[P, QT], [-1, S]], channel_multiplier=1).then_inc(made, 1)
                pool.wait_ge(made, 2)
                pool.tensor_copy(cb[:], ctxT[:, :, 0:S]).then_inc(cb_s, 1)
                with pool.Fori(0, B - 1) as b:
                    A.wait_done(pool, b, aat["k", M - 1])
                    V.wait_done(pool, b, vat["v", QT - 1, 1])
                    split_wait(pool, K["passed"])
                    pool.tensor_copy(cb[:], ctxT[:, :, ds(b * SK + SK, S)]).then_inc(cb_s, 1)

            @block.tensor
            def _(pe):
                pe.wait_ge(w_in, 64)
                with pe.Fori(0, B) as b:
                    pe.wait_ge(cb_s, b + 1)
                    for m in range(M):
                        at = aat["k", m]
                        A.wait_free(pe, b, at)
                        for k in range(DT):
                            mm = pe.matmul(A.bank(at), wk[:, k, m * P:(m + 1) * P], cb[:, k, :], start=(k == 0), stop=(k == DT - 1))
                        mm.then_inc(A.full, 1)
                    V.wait_turns(pe, b)
                    pe.wait_ge(padf_s, b + 1)
                    pe.matmul(keepbank, ones[0:1, :], padf[:], start=True, stop=True).then_inc(keep_s, 1)
                    for kt in range(QT):
                        for n in range(2):
                            at = vat["v", kt, n]
                            V.wait_free(pe, b, at)
                            for k in range(DT):
                                mm = pe.matmul(V.bank(at), cb[:, k, kt * P:(kt + 1) * P], wv[:, k, n * 512:(n + 1) * 512],
                                               start=(k == 0), stop=(k == DT - 1))
                            mm.then_inc(V.full, 1)
                    pe.wait_ge(xn_s, b * QT + QT)
                    for f, (R, i) in enumerate(((A, aat["xT",]), (V, vat["xT",]))):
                        R.wait_free(pe, b, i)
                        for k in range(QT):
                            mm = pe.transpose(R.bank(i)[:, k * P:(k + 1) * P], xn[:, k, f * P:(f + 1) * P], ident[:])
                        mm.then_inc(R.full, 1)
                    A.wait_done(pe, b, aat["xT",])
                    V.wait_done(pe, b, vat["xT",])
                    for m in range(M):
                        at = aat["q", m]
                        A.wait_free(pe, b, at)
                        for k in range(DT):
                            mm = pe.matmul(A.bank(at), wq[:, k, m * P:(m + 1) * P], xT[:, k, :], start=(k == 0), stop=(k == DT - 1))
                        mm.then_inc(A.full, 1)
                    A.wait_done(pe, b, aat["q", M - 1])

                    def score(h, q):
                        at = h * QT + q
                        if at >= 3:
                            pe.wait_ge(s_free, b * H * QT + at - 2)
                        p0, n = HD * (h % 2), (q + 1) * P
                        pe.matmul(scores[at % 3][:, 0:n], qT[p0:p0 + HD, h // 2, q * P:(q + 1) * P], kT[p0:p0 + HD, h // 2, 0:n],
                                  start=True, stop=True).then_inc(s_full, 1)

                    def turn(h, q):
                        R, at = (A, aat["turn", h, q]) if q % 2 else (V, vat["turn", h, q])
                        R.wait_free(pe, b, at)
                        pe.wait_ge(pa_s if q >= 2 else pn_s, b * H * 2 + h * 2 + q % 2 + 1)
                        for k in range(q + 1):
                            mm = pe.transpose(R.bank(at)[:, k * P:(k + 1) * P], sm[:, h % 2, q, k * P:(k + 1) * P], ident[:])
                        mm.then_inc(R.full, 1)

                    def products(m):
                        O.wait_free(pe, b, m)
                        A.wait_done(pe, b, aat["turn", 2 * m + 1, 3])
                        V.wait_done(pe, b, vat["turn", 2 * m + 1, 2])
                        for k in range(QT):
                            for i in range(2):
                                h, p0 = 2 * m + i, HD * i
                                mm = pe.matmul(O.bank(m)[p0:p0 + HD, k * P:S], v[:, k, h * HD:(h + 1) * HD],
                                               pT[:, h % 3, k, k * P:S], start=(k == 0), stop=(k == QT - 1), skip_group_check=True)
                        mm.then_inc(O.full, 1)

                    for h in range(STEPS):
                        for q in range(QT):
                            if 2 <= h < H + 2:
                                turn(h - 2, q)
                            if h < H:
                                score(h, q)
                            if q == QT - 1 and h >= 4 and h % 2 == 0:
                                products(h // 2 - 2)
                    for q in range(QT):
                        at = vat["y", q]
                        V.wait_free(pe, b, at)
                        O.wait_done(pe, b, M - 1)
                        for m in range(M):
                            mm = pe.matmul(V.bank(at)[:, 0:D], aT[:, m, q * P:(q + 1) * P], wo[:, m, :],
                                           start=(m == 0), stop=(m == M - 1))
                        mm.then_inc(V.full, 1)

            @block.scalar
            def _(act):
                with act.Fori(0, B) as b:
                    def empty(job, dst, src=lambda o: o):
                        A.wait_full(act, b, aat[job])
                        act.copy(dst, src(A.bank(aat[job]))).then_inc(A.free, 1)

                    for m in range(M):
                        empty(("k", m), kT[:, m, :])
                        if m == 2:
                            act.wait_ge(mv_s, b + 1)
                            act.activation(std[:], mv[:, :, 1], ACT.Sqrt, bias=eps[:]).then_inc(std_s, 1)
                    empty(("xT",), xT[:, 0, :])
                    for m in range(M):
                        empty(("q", m), qT[:, m, :])
                    for h in range(STEPS):
                        for q in range(QT):
                            if h < H:
                                n, at = (q + 1) * P, h * QT + q
                                act.wait_ge(mx_s, b * H * QT + at + 1)
                                act.activation(sm[:, h % 2, q, 0:n], sm[:, h % 2, q, 0:n], ACT.Exp, bias=nmx[:, h % 2, q:q + 1],
                                               scale=SCALE, accum_out=su[:, h % 2, q:q + 1]).then_inc(exp_s, 1)
                            if 2 <= h < H + 2 and q % 2:
                                if h >= 5:
                                    O.wait_full(act, b, (h - 5) // 2)
                                empty(("turn", h - 2, q), pT[:, (h - 2) % 3, 0:q + 1, q * P:(q + 1) * P],
                                      lambda o: o[:, 0:(q + 1) * P].rearrange("p (k n) -> p k n", n=P))
                            if 1 <= h <= H and q % 2:
                                u, qq = (h - 1) % 2, 2 + q // 2
                                n = (qq + 1) * P
                                act.wait_ge(inv_s, b * H + h)
                                act.activation(sm[:, u, qq, 0:n], sm[:, u, qq, 0:n], ACT.Copy,
                                               scale=rs[:, u, qq:qq + 1]).then_inc(pa_s, 1)

            @block.vector
            def _(dve):
                dve.wait_ge(made, 2)
                N_CH = 2 * QT - 1 + 1 + 3 + H * 2
                with dve.Fori(0, B) as b:
                    ch = Chain(dve, ch_s, b * N_CH)
                    V.wait_turns(dve, b)
                    split_wait(dve, K["passed"])
                    src = lambda k: X[:, ds(b * QT + k, 1), :]
                    for k in range(QT):
                        ch.mark(dve.bn_stats(st[:, k, :], src(k)))
                    ch.wait()
                    split_wait(dve, K["passed"])
                    for k in range(QT):
                        ins = dve.bn_aggr(mv[:, k, :], st[:, k, :])
                        if k < QT - 1:
                            ch.mark(ins)
                    ins.then_inc(mv_s, 1)
                    dve.wait_ge(mv_s, b + 1)
                    dve.wait_ge(std_s, b + 1)
                    ln_apply(dve, ch, src, mv, std, rstd, xn, xn_s)
                    dve.wait_ge(pad_s, 16 * b + 16)
                    dve.tensor_scalar(padf[:], padi[:], 0.0, None, ALU.not_equal).then_inc(padf_s, 1)
                    dve.wait_ge(keep_s, b + 1)
                    ch.mark(dve.tensor_copy(keep[:], keepbank))
                    ch.wait()
                    ch.mark(dve.tensor_tensor(vis[:], causal[:], keep[:, None, :].broadcast_to([P, QT, S]), ALU.mult))
                    ch.wait()
                    ch.mark(dve.tensor_reduce(seen[:], vis[:], AX.X, ALU.max))
                    dve.tensor_scalar(bias[:], vis[:], BIG, -BIG, ALU.mult, ALU.add).then_inc(bias_s, 1)

                    def empty(job, dst, src=lambda o: o):
                        V.wait_full(dve, b, vat[job])
                        dve.tensor_copy(dst, src(V.bank(vat[job]))).then_inc(V.free, 1)

                    for k in range(QT):
                        for n in range(2):
                            empty(("v", k, n), v[:, k, n * 512:(n + 1) * 512])
                    empty(("xT",), xT[:, 1, :])
                    dve.wait_ge(bias_s, b + 1)

                    def largest(h, q):
                        n, at, u = (q + 1) * P, h * QT + q, h % 2
                        dve.wait_ge(s_full, b * H * QT + at + 1)
                        if h >= 2:
                            (A if q % 2 else V).wait_full(dve, b, (aat if q % 2 else vat)["turn", h - 2, q])
                        split_wait(dve, K["passed"])
                        dve.tensor_tensor_reduce(sm[:, u, q, 0:n], scores[at % 3][:, 0:n], bias[:, q, 0:n], 1.0, -3e38,
                                                 ALU.add, ALU.max, mx[:, u, q:q + 1]).then_inc(s_free, 1)
                        dve.wait_ge(s_free, b * H * QT + at + 1)
                        dve.tensor_scalar(nmx[:, u, q:q + 1], mx[:, u, q:q + 1], -SCALE, None, ALU.mult).then_inc(mx_s, 1)

                    def invert(h):
                        u = h % 2
                        dve.wait_ge(exp_s, b * H * QT + h * QT + QT)
                        ch.mark(dve.tensor_tensor(rs[:, u, :], su[:, u, :], seen[:], ALU.mult))
                        ch.wait()
                        ch.mark(dve.reciprocal(rs[:, u, :], rs[:, u, :]))
                        ch.wait()
                        dve.tensor_tensor(rs[:, u, :], rs[:, u, :], seen[:], ALU.mult).then_inc(inv_s, 1)
                        dve.wait_ge(inv_s, b * H + h + 1)

                    def scale(h, q):
                        n, u = (q + 1) * P, h % 2
                        dve.tensor_scalar(sm[:, u, q, 0:n], sm[:, u, q, 0:n], rs[:, u, q:q + 1], None, ALU.mult).then_inc(pn_s, 1)

                    for h in range(STEPS):
                        for q in range(QT):
                            if h < H:
                                largest(h, q)
                            if 2 <= h < H + 2 and q % 2 == 0:
                                if h >= 5:
                                    O.wait_full(dve, b, (h - 5) // 2)
                                empty(("turn", h - 2, q), pT[:, (h - 2) % 3, 0:q + 1, q * P:(q + 1) * P],
                                      lambda o: o[:, 0:(q + 1) * P].rearrange("p (k n) -> p k n", n=P))
                            if q == 0 and h >= 5 and h % 2:
                                O.wait_full(dve, b, (h - 5) // 2)
                                dve.tensor_copy(aT[:, (h - 5) // 2, :], O.bank(0)).then_inc(O.free, 1)
                            if 1 <= h <= H:
                                if q == 0:
                                    invert(h - 1)
                                if q < 2:
                                    scale(h - 1, q)
                    for q in range(QT):
                        V.wait_full(dve, b, vat["y", q])
                        x = X[:, ds(b * QT + q, 1), :]
                        dve.tensor_tensor(x, x, V.bank(vat["y", q])[:, None, 0:D], ALU.add).then_inc(V.free, 1)
                    assert ch.n == N_CH, ch.n


_OUTS = [((4, 512, 256), 'float32')]
_SWAPPED = ("L1_xattn_Wq", "L1_xattn_Wk", "L1_xattn_Wv", "L1_xattn_Wo", "L2_xattn_Wq", "L2_xattn_Wk",
            "L2_xattn_Wv", "L2_xattn_Wo", "L1_ffn_router_w", "L1_ffn_w1", "L1_ffn_w2", "L2_ffn_gate_w",
            "L2_ffn_fc1s", "L2_ffn_fc2s", "L3_ffn_router_w", "L3_ffn_expert_w1", "L3_ffn_expert_w2")
_COLUMNS = ("L0_xattn_b_kv", "L0_xattn_b_q", "L0_xattn_b1", "L0_ffn_cn_b1", "L0_ffn_cn_b2", "L0_ffn_gc_b1",
            "L1_xattn_bq", "L1_xattn_bk", "L1_ffn_b1", "L2_ffn_ln_w", "L2_ffn_ln_b", "L2_ffn_b1s", "L3_ffn_expert_b1")


def kernel(**inputs):
    import numpy as _np
    import concourse.bacc as _bacc
    from concourse import mybir as _mybir
    from concourse.bass_utils import run_bass_kernel_spmd as _run

    nc = _bacc.Bacc("TRN2", target_bir_lowering=False, num_devices=1)
    arrays, args = {}, {}
    for name in inputs:
        a = _np.asarray(inputs[name])
        if name in _SWAPPED:
            a = _np.swapaxes(a, -1, -2)
        a = _np.ascontiguousarray(a)
        laid = {name: a}
        if name in _COLUMNS:
            laid[name + "_cols"] = _np.ascontiguousarray(_np.swapaxes(a.reshape(*a.shape[:-1], -1, 128), -1, -2))
        for key, a in laid.items():
            arrays[f"in_{key}_dram"] = a
            args[key] = nc.dram_tensor(f"in_{key}_dram", a.shape, _mybir.dt.from_np(a.dtype), kind="ExternalInput").ap()
    outs = []
    for i, (shape, dtype) in enumerate(_OUTS):
        dt = _mybir.dt.from_np(_np.dtype(dtype))
        outs.append(nc.dram_tensor(f"out_{i}_dram", shape, dt, kind="ExternalOutput").ap())
    program(nc, args, outs[0], STAGES)
    r = _run(nc, [arrays], core_ids=[0])
    return r.results[0]["out_0_dram"]


STAGES = range(8)
```
